# Optimizing a Trainium2 kernel written in Bass

```python
import numpy as np
import jax
import jax.numpy as jnp

def _softmax(x, axis=-1):
    return jax.nn.softmax(x, axis=axis)

def _gelu(x):
    return jax.nn.gelu(x, approximate=True)

def _silu(x):
    return jax.nn.silu(x)

def _sigmoid(x):
    return jax.nn.sigmoid(x)

def _layernorm(x, axis=-1, eps=1e-05):
    m = jnp.mean(x, axis=axis, keepdims=True)
    v = jnp.var(x, axis=axis, keepdims=True)
    return (x - m) / jnp.sqrt(v + eps)

def _scatter_add(tgt, idx, src, axis=0):
    return tgt.at[idx].add(src)

def _segment_sum(src, seg, n):
    return jax.ops.segment_sum(src, seg, n)
kernel_name = 'mk_adaln_ffn_d4_seqx_r8_4b14ba'

def setup_inputs(seed: int=0):
    np.random.seed(seed)
    _w = jnp.asarray

    def _rec_inputs():
        import jax
        import jax.numpy as jnp
        _rk = jax.random.key(seed)
        x = -7.109e-05 + 0.9999 * jax.random.normal(jax.random.fold_in(_rk, 1), (64, 32, 512), jnp.float32)
        _lenS = 32 - jax.random.randint(jax.random.fold_in(_rk, 7), (64,), 0, max(1, 32 // 4) + 1, jnp.int32)
        _lenS2 = 32 - jax.random.randint(jax.random.fold_in(_rk, 8), (64,), 0, max(1, 32 // 4) + 1, jnp.int32)
        itok_B_0_15 = jax.random.randint(jax.random.fold_in(_rk, 11), (64,), 0, 16, jnp.int32)
        itok_B_6_15 = jax.random.randint(jax.random.fold_in(_rk, 12), (64,), 6, 16, jnp.int32)
        itok_Bx16_0_63 = jax.random.randint(jax.random.fold_in(_rk, 13), (64, 16), 0, 64, jnp.int32)
        itok_B_207_1644 = jax.random.randint(jax.random.fold_in(_rk, 14), (64,), 207, 1645, jnp.int32)
        return (x, itok_B_0_15, itok_B_6_15, itok_Bx16_0_63, itok_B_207_1644)
    x, itok_B_0_15, itok_B_6_15, itok_Bx16_0_63, itok_B_207_1644 = _rec_inputs()

    def _L0_cond_setup():
        import jax, jax.numpy as jnp
        import numpy as np
        B, C, T = (64, 32, 512)
        S, D = (16, 32)
        key = jax.random.key(seed)
        k1, k2, k3 = jax.random.split(key, 3)
        x = jax.random.normal(k1, (B, C, T), dtype=jnp.float32)
        condition = jax.random.randint(k2, (B,), 0, S, dtype=jnp.int64)
        bound = float(np.sqrt(6.0 / C))
        weights = jax.random.uniform(k3, (S, C, D), dtype=jnp.float32, minval=-bound, maxval=bound)
        return {'x': x, 'condition': condition, 'weights': weights}
    _L0_cond_all = _L0_cond_setup()
    _L0_cond_in = {k: v for k, v in _L0_cond_all.items() if k in ('weights',)}
    del _L0_cond_all

    def _L0_ffn_setup():
        import jax, jax.numpy as jnp
        import numpy as np
        ALPHA = 32
        R = 16
        SCALING = ALPHA / R
        key = jax.random.key(seed)
        k1, k2, k3, k4 = jax.random.split(key, 4)
        B_, S, D = (4, 256, 512)
        H, r, O = (8, R, 512)
        x = jax.random.normal(k1, (B_, S, D), dtype=jnp.float32)
        A = jax.random.normal(k2, (H, r, D), dtype=jnp.float32) * 0.02
        Bm = jax.random.normal(k3, (H, O, r), dtype=jnp.float32) * 0.02
        Wr = jax.random.normal(k4, (H, D), dtype=jnp.float32) * 0.02
        br = jnp.zeros((H,), dtype=jnp.float32)
        return {'x': x, 'A': A, 'B': Bm, 'Wr': Wr, 'br': br}
    _L0_ffn_all = _L0_ffn_setup()
    _L0_ffn_in = {k: v for k, v in _L0_ffn_all.items() if k in ('A', 'B', 'Wr', 'br')}
    del _L0_ffn_all

    def _L1_cond_setup():
        import jax, jax.numpy as jnp
        import numpy as np
        B, S, D_IN, D_OUT = (4, 256, 512, 512)
        RANK, MAX_LORAS = (16, 32)
        key = jax.random.key(seed)
        ks = jax.random.split(key, 6)
        x = jax.random.normal(ks[0], (B, S, D_IN), dtype=jnp.float32)
        adapter_ids = jax.random.randint(ks[1], (B,), 0, MAX_LORAS)
        base_weight = jax.random.normal(ks[2], (D_OUT, D_IN), dtype=jnp.float32) * D_IN ** (-0.5)
        base_bias = jax.random.normal(ks[3], (D_OUT,), dtype=jnp.float32) * 0.01
        lora_A_w = jax.random.normal(ks[4], (MAX_LORAS, RANK, D_IN), dtype=jnp.float32) * D_IN ** (-0.5)
        lora_B_w = jax.random.normal(ks[5], (MAX_LORAS, D_OUT, RANK), dtype=jnp.float32) * RANK ** (-0.5)
        return {'x': x, 'adapter_ids': adapter_ids, 'base_weight': base_weight, 'base_bias': base_bias, 'lora_A_w': lora_A_w, 'lora_B_w': lora_B_w}
    _L1_cond_all = _L1_cond_setup()
    _L1_cond_in = {k: v for k, v in _L1_cond_all.items() if k in ('base_weight', 'base_bias', 'lora_A_w', 'lora_B_w')}
    del _L1_cond_all

    def _L1_ffn_setup():
        import jax, jax.numpy as jnp
        import numpy as np
        B, L, H, Dh, M = (4, 256, 16, 32, 128)
        D = H * Dh
        key = jax.random.key(seed)
        kx, ku, kd, kp = jax.random.split(key, 4)
        x = jax.random.normal(kx, (B, L, D), dtype=jnp.float32)
        up = jax.random.normal(ku, (H, Dh, M), dtype=jnp.float32)
        down = jax.random.normal(kd, (H, M, Dh), dtype=jnp.float32)
        perm = jax.random.permutation(kp, D)
        return {'x': x, 'up': up, 'down': down, 'perm': perm}
    _L1_ffn_all = _L1_ffn_setup()
    _L1_ffn_in = {k: v for k, v in _L1_ffn_all.items() if k in ('up', 'down', 'perm')}
    del _L1_ffn_all

    def _L2_cond_setup():
        import jax, jax.numpy as jnp
        import numpy as np
        NUM_CONDITIONS = 16
        IN_CH = 32
        OUT_CH = 32
        B = 64
        T = 512
        key = jax.random.key(seed)
        k_x, k_w, k_c = jax.random.split(key, 3)
        x = jax.random.normal(k_x, (B, IN_CH, T), dtype=jnp.float32)
        bound = float(np.sqrt(6.0 / IN_CH))
        weights = jax.random.uniform(k_w, (NUM_CONDITIONS, IN_CH, OUT_CH), dtype=jnp.float32, minval=-bound, maxval=bound)
        condition = jax.random.randint(k_c, (B,), 0, NUM_CONDITIONS, dtype=jnp.int64)
        return {'x': x, 'weights': weights, 'condition': condition}
    _L2_cond_all = _L2_cond_setup()
    _L2_cond_in = {k: v for k, v in _L2_cond_all.items() if k in ('weights',)}
    del _L2_cond_all

    def _L2_ffn_setup():
        import jax, jax.numpy as jnp
        import numpy as np
        import math
        E, DK, R = (8, 32, 16)
        SCALING = 16.0 / 16.0
        key = jax.random.key(seed)
        ks = jax.random.split(key, 7)
        Bt, S, Din, Dout = (4, 256, 512, 512)
        x = jax.random.normal(ks[0], (Bt, S, Din), jnp.float32)
        W = jax.random.normal(ks[1], (Dout, Din), jnp.float32) * 0.02
        b = jnp.zeros((Dout,), jnp.float32)
        Wq = jax.random.normal(ks[2], (E * DK, Din), jnp.float32) * 0.02
        Wk = jax.random.normal(ks[3], (E * DK, Din), jnp.float32) * 0.02
        A = jax.random.normal(ks[4], (E, R, Din), jnp.float32) * 0.02
        Bm = jax.random.normal(ks[5], (E, Dout, R), jnp.float32) * 0.02
        return {'x': x, 'W': W, 'b': b, 'Wq': Wq, 'Wk': Wk, 'A': A, 'Bm': Bm}
    _L2_ffn_all = _L2_ffn_setup()
    _L2_ffn_in = {k: v for k, v in _L2_ffn_all.items() if k in ('W', 'b', 'Wq', 'Wk', 'A', 'Bm')}
    del _L2_ffn_all

    def _L3_cond_setup():
        import jax, jax.numpy as jnp
        import numpy as np
        B, S, HID = (4, 128, 512)
        D, HQ, HK = (128, 32, 8)
        PAGES, PSIZE, NPP = (64, 32, 16)
        THETA = 10000.0
        EPS = 1e-06
        SCALE = 1.0 / float(np.sqrt(D))

        def _rmsnorm(t, w):
            var = jnp.mean(t * t, axis=-1, keepdims=True)
            return t * jax.lax.rsqrt(var + EPS) * w

        def _rope(t, pos):
            inv_freq = 1.0 / THETA ** (jnp.arange(0, D, 2, dtype=jnp.float32) / D)
            freqs = pos[..., None].astype(jnp.float32) * inv_freq
            cos = jnp.cos(freqs)[:, :, None, :]
            sin = jnp.sin(freqs)[:, :, None, :]
            t1, t2 = (t[..., :D // 2], t[..., D // 2:])
            return jnp.concatenate([t1 * cos - t2 * sin, t2 * cos + t1 * sin], axis=-1)
        key = jax.random.key(seed)
        ks = jax.random.split(key, 10)
        x = jax.random.normal(ks[0], (B, S, HID), jnp.float32)
        Wq = jax.random.normal(ks[1], (HQ * D, HID), jnp.float32) * 0.02
        Wk = jax.random.normal(ks[2], (HK * D, HID), jnp.float32) * 0.02
        Wv = jax.random.normal(ks[3], (HK * D, HID), jnp.float32) * 0.02
        Wo = jax.random.normal(ks[4], (HID, HQ * D), jnp.float32) * 0.02
        q_norm_w = jax.random.uniform(ks[5], (D,), jnp.float32)
        k_norm_w = jax.random.uniform(ks[6], (D,), jnp.float32)
        k_cache = jax.random.normal(ks[7], (PAGES, PSIZE, HK, D), jnp.float32)
        v_cache = jax.random.normal(ks[8], (PAGES, PSIZE, HK, D), jnp.float32)
        block_table = jnp.arange(B * NPP, dtype=jnp.int32).reshape(B, NPP)
        cache_seqlens = jax.random.randint(ks[9], (B,), 0, 475).astype(jnp.int32)
        return dict(x=x, Wq=Wq, Wk=Wk, Wv=Wv, Wo=Wo, q_norm_w=q_norm_w, k_norm_w=k_norm_w, k_cache=k_cache, v_cache=v_cache, block_table=block_table, cache_seqlens=cache_seqlens)
    _L3_cond_all = _L3_cond_setup()
    _L3_cond_in = {k: v for k, v in _L3_cond_all.items() if k in ('Wq', 'Wk', 'Wv', 'Wo', 'q_norm_w', 'k_norm_w', 'k_cache', 'v_cache')}
    del _L3_cond_all

    def _L3_ffn_setup():
        import jax, jax.numpy as jnp
        import numpy as np
        B_, S, D_IN, D_OUT = (4, 256, 512, 512)
        N, RANK, ALPHA = (8, 16, 32)
        SCALE = ALPHA / RANK
        key = jax.random.key(seed)
        kx, ka, kb, kw, kbias = jax.random.split(key, 5)
        x = jax.random.normal(kx, (B_, S, D_IN), dtype=jnp.float32)
        lora_A = jax.random.normal(ka, (N, RANK, D_IN), dtype=jnp.float32) * (1.0 / np.sqrt(D_IN))
        lora_B = jax.random.normal(kb, (N, D_OUT, RANK), dtype=jnp.float32) * (1.0 / np.sqrt(RANK))
        W = jax.random.normal(kw, (D_OUT, D_IN), dtype=jnp.float32) * (1.0 / np.sqrt(D_IN))
        bias = jax.random.normal(kbias, (D_OUT,), dtype=jnp.float32) * 0.01
        lora_weights = jnp.full((N,), 1.0 / N, dtype=jnp.float32)
        return {'x': x, 'lora_A': lora_A, 'lora_B': lora_B, 'W': W, 'bias': bias, 'lora_weights': lora_weights}
    _L3_ffn_all = _L3_ffn_setup()
    _L3_ffn_in = {k: v for k, v in _L3_ffn_all.items() if k in ('lora_A', 'lora_B', 'W', 'bias', 'lora_weights')}
    del _L3_ffn_all
    return {'x': x, 'itok_B_0_15': itok_B_0_15, 'itok_B_6_15': itok_B_6_15, 'itok_Bx16_0_63': itok_Bx16_0_63, 'itok_B_207_1644': itok_B_207_1644, 'L0_cond_weights': _L0_cond_in['weights'], 'L0_ffn_A': _L0_ffn_in['A'], 'L0_ffn_B': _L0_ffn_in['B'], 'L0_ffn_Wr': _L0_ffn_in['Wr'], 'L0_ffn_br': _L0_ffn_in['br'], 'L1_cond_base_weight': _L1_cond_in['base_weight'], 'L1_cond_base_bias': _L1_cond_in['base_bias'], 'L1_cond_lora_A_w': _L1_cond_in['lora_A_w'], 'L1_cond_lora_B_w': _L1_cond_in['lora_B_w'], 'L1_ffn_up': _L1_ffn_in['up'], 'L1_ffn_down': _L1_ffn_in['down'], 'L1_ffn_perm': _L1_ffn_in['perm'], 'L2_cond_weights': _L2_cond_in['weights'], 'L2_ffn_W': _L2_ffn_in['W'], 'L2_ffn_b': _L2_ffn_in['b'], 'L2_ffn_Wq': _L2_ffn_in['Wq'], 'L2_ffn_Wk': _L2_ffn_in['Wk'], 'L2_ffn_A': _L2_ffn_in['A'], 'L2_ffn_Bm': _L2_ffn_in['Bm'], 'L3_cond_Wq': _L3_cond_in['Wq'], 'L3_cond_Wk': _L3_cond_in['Wk'], 'L3_cond_Wv': _L3_cond_in['Wv'], 'L3_cond_Wo': _L3_cond_in['Wo'], 'L3_cond_q_norm_w': _L3_cond_in['q_norm_w'], 'L3_cond_k_norm_w': _L3_cond_in['k_norm_w'], 'L3_cond_k_cache': _L3_cond_in['k_cache'], 'L3_cond_v_cache': _L3_cond_in['v_cache'], 'L3_ffn_lora_A': _L3_ffn_in['lora_A'], 'L3_ffn_lora_B': _L3_ffn_in['lora_B'], 'L3_ffn_W': _L3_ffn_in['W'], 'L3_ffn_bias': _L3_ffn_in['bias'], 'L3_ffn_lora_weights': _L3_ffn_in['lora_weights']}

def reference(x, itok_B_0_15, itok_B_6_15, itok_Bx16_0_63, itok_B_207_1644, L0_cond_weights, L0_ffn_A, L0_ffn_B, L0_ffn_Wr, L0_ffn_br, L1_cond_base_weight, L1_cond_base_bias, L1_cond_lora_A_w, L1_cond_lora_B_w, L1_ffn_up, L1_ffn_down, L1_ffn_perm, L2_cond_weights, L2_ffn_W, L2_ffn_b, L2_ffn_Wq, L2_ffn_Wk, L2_ffn_A, L2_ffn_Bm, L3_cond_Wq, L3_cond_Wk, L3_cond_Wv, L3_cond_Wo, L3_cond_q_norm_w, L3_cond_k_norm_w, L3_cond_k_cache, L3_cond_v_cache, L3_ffn_lora_A, L3_ffn_lora_B, L3_ffn_W, L3_ffn_bias, L3_ffn_lora_weights):
    import jax
    import jax.numpy as jnp

    def _L0_cond_ref(x, condition, weights):
        import jax, jax.numpy as jnp
        import numpy as np
        B, C, T = (64, 32, 512)
        S, D = (16, 32)
        W = weights[condition]
        return jnp.einsum('bct,bcd->bdt', x, W)

    def _L0_ffn_ref(x, A, B, Wr, br):
        import jax, jax.numpy as jnp
        import numpy as np
        ALPHA = 32
        R = 16
        SCALING = ALPHA / R
        H = A.shape[0]
        router_logits = jnp.einsum('bsd,hd->bsh', x, Wr) + br
        scores = H * jax.nn.softmax(router_logits, axis=-1)
        low = jnp.einsum('bsd,hrd->bshr', x, A)
        out = jnp.einsum('bshr,hor,bsh->bso', low, B, scores)
        return SCALING * out

    def _L1_cond_ref(x, adapter_ids, base_weight, base_bias, lora_A_w, lora_B_w):
        import jax, jax.numpy as jnp
        import numpy as np
        B, S, D_IN, D_OUT = (4, 256, 512, 512)
        RANK, MAX_LORAS = (16, 32)
        result = jnp.einsum('bsd,od->bso', x, base_weight) + base_bias
        A = lora_A_w[adapter_ids]
        Bw = lora_B_w[adapter_ids]
        h = jnp.einsum('bsd,brd->bsr', x, A)
        lora_out = jnp.einsum('bsr,bor->bso', h, Bw)
        result = result + lora_out
        return result.astype(x.dtype)

    def _L1_ffn_ref(x, up, down, perm):
        import jax, jax.numpy as jnp
        import numpy as np
        B, L, H, Dh, M = (4, 256, 16, 32, 128)
        D = H * Dh
        b, l, Dm = x.shape
        h, d = (up.shape[0], up.shape[1])
        unperm = jnp.argsort(perm)
        t = x.reshape(b * l, Dm)
        t = t[:, perm]
        t = t.reshape(b * l, h, d)
        t = jnp.einsum('bhd,hdm->bhm', t, up)
        t = jax.nn.gelu(t, approximate=False)
        t = jnp.einsum('bhm,hmd->bhd', t, down)
        t = t.reshape(b * l, h * d)
        t = t[:, unperm]
        out = t.reshape(b, l, Dm)
        return out

    def _L2_cond_ref(x, weights, condition):
        import jax, jax.numpy as jnp
        import numpy as np
        NUM_CONDITIONS = 16
        IN_CH = 32
        OUT_CH = 32
        B = 64
        T = 512
        W = weights[condition]
        return jnp.einsum('bct,bcd->bdt', x, W)

    def _L2_ffn_ref(x, W, b, Wq, Wk, A, Bm):
        import jax, jax.numpy as jnp
        import numpy as np
        import math
        E, DK, R = (8, 32, 16)
        SCALING = 16.0 / 16.0
        Bt, S, Din = x.shape
        result = jnp.einsum('bsi,oi->bso', x, W) + b
        q = jnp.einsum('bsi,ni->bsn', x, Wq).reshape(Bt, S, E, DK)
        k = jnp.einsum('bsi,ni->bsn', x, Wk).reshape(Bt, S, E, DK)
        scores = jnp.einsum('bsed,bsed->bse', q, k) / math.sqrt(DK)
        w = jax.nn.softmax(scores, axis=-1)
        h = jnp.einsum('bsi,eri->bser', x, A)
        combined = jnp.einsum('bse,bser,eor->bso', w, h, Bm) * SCALING
        return result + combined

    def _L3_cond_ref(x, Wq, Wk, Wv, Wo, q_norm_w, k_norm_w, k_cache, v_cache, block_table, cache_seqlens):
        import jax, jax.numpy as jnp
        import numpy as np
        B, S, HID = (4, 128, 512)
        D, HQ, HK = (128, 32, 8)
        PAGES, PSIZE, NPP = (64, 32, 16)
        THETA = 10000.0
        EPS = 1e-06
        SCALE = 1.0 / float(np.sqrt(D))

        def _rmsnorm(t, w):
            var = jnp.mean(t * t, axis=-1, keepdims=True)
            return t * jax.lax.rsqrt(var + EPS) * w

        def _rope(t, pos):
            inv_freq = 1.0 / THETA ** (jnp.arange(0, D, 2, dtype=jnp.float32) / D)
            freqs = pos[..., None].astype(jnp.float32) * inv_freq
            cos = jnp.cos(freqs)[:, :, None, :]
            sin = jnp.sin(freqs)[:, :, None, :]
            t1, t2 = (t[..., :D // 2], t[..., D // 2:])
            return jnp.concatenate([t1 * cos - t2 * sin, t2 * cos + t1 * sin], axis=-1)
        bsz, seqlen, _ = x.shape
        q = jnp.einsum('bsd,ed->bse', x, Wq).reshape(bsz, seqlen, HQ, D)
        k = jnp.einsum('bsd,ed->bse', x, Wk).reshape(bsz, seqlen, HK, D)
        v = jnp.einsum('bsd,ed->bse', x, Wv).reshape(bsz, seqlen, HK, D)
        q = _rmsnorm(q, q_norm_w)
        k = _rmsnorm(k, k_norm_w)
        pos = cache_seqlens[:, None] + jnp.arange(seqlen)[None, :]
        q = _rope(q, pos)
        k = _rope(k, pos)
        L = NPP * PSIZE
        kc = k_cache[block_table].reshape(bsz, L, HK, D)
        vc = v_cache[block_table].reshape(bsz, L, HK, D)
        k_all = jnp.concatenate([kc, k], axis=1)
        v_all = jnp.concatenate([vc, v], axis=1)
        valid_c = jnp.arange(L)[None, :] < cache_seqlens[:, None]
        valid = jnp.concatenate([valid_c, jnp.ones((bsz, seqlen), dtype=bool)], axis=1)
        rep = HQ // HK
        k_all = jnp.repeat(k_all, rep, axis=2)
        v_all = jnp.repeat(v_all, rep, axis=2)
        scores = jnp.einsum('bqhd,bkhd->bhqk', q, k_all) * SCALE
        scores = jnp.where(valid[:, None, None, :], scores, -1e+30)
        probs = jax.nn.softmax(scores, axis=-1)
        o = jnp.einsum('bhqk,bkhd->bqhd', probs, v_all)
        o = o.reshape(bsz, seqlen, HQ * D)
        return jnp.einsum('bse,de->bsd', o, Wo)

    def _L3_ffn_ref(x, lora_A, lora_B, W, bias, lora_weights):
        import jax, jax.numpy as jnp
        import numpy as np
        B_, S, D_IN, D_OUT = (4, 256, 512, 512)
        N, RANK, ALPHA = (8, 16, 32)
        SCALE = ALPHA / RANK
        h = jnp.einsum('bsd,nrd->nbsr', x, lora_A)
        coef = (SCALE * lora_weights)[:, None, None]
        lora_out = jnp.einsum('nbsr,nor->bso', h, lora_B * coef)
        base = jnp.einsum('bsd,od->bso', x, W) + bias
        return base + lora_out
    x = x + _L0_ffn_ref(_L0_cond_ref(x, itok_B_0_15, L0_cond_weights), L0_ffn_A, L0_ffn_B, L0_ffn_Wr, L0_ffn_br)
    x = x + _L1_ffn_ref(_L1_cond_ref(x, itok_B_6_15, L1_cond_base_weight, L1_cond_base_bias, L1_cond_lora_A_w, L1_cond_lora_B_w), L1_ffn_up, L1_ffn_down, L1_ffn_perm)
    x = x + _L2_ffn_ref(_L2_cond_ref(x, L2_cond_weights, itok_B_0_15), L2_ffn_W, L2_ffn_b, L2_ffn_Wq, L2_ffn_Wk, L2_ffn_A, L2_ffn_Bm)
    x = x + _L3_ffn_ref(_L3_cond_ref(x, L3_cond_Wq, L3_cond_Wk, L3_cond_Wv, L3_cond_Wo, L3_cond_q_norm_w, L3_cond_k_norm_w, L3_cond_k_cache, L3_cond_v_cache, itok_Bx16_0_63, itok_B_207_1644), L3_ffn_lora_A, L3_ffn_lora_B, L3_ffn_W, L3_ffn_bias, L3_ffn_lora_weights)
    return x

_drawn_inputs = setup_inputs


def setup_inputs(seed=0):
    import zlib

    import numpy as np

    out = dict(_drawn_inputs(seed))
    spreads = {'L0_ffn_br': (0.0, 0.1), 'L2_ffn_b': (0.0, 0.8), 'L3_ffn_lora_weights': (0.125, 0.6)}
    factors = {'L1_cond_base_bias': 7.458,
     'L3_cond_Wq': 8.0,
     'L3_cond_Wk': 8.0,
     'L3_cond_Wv': 2.803,
     'L3_cond_Wo': 2.765,
     'L3_cond_q_norm_w': 8.0,
     'L3_cond_k_norm_w': 8.0,
     'L3_cond_k_cache': 8.0,
     'L3_cond_v_cache': 8.0,
     'L3_ffn_lora_A': 4.28,
     'L3_ffn_lora_B': 4.847,
     'L3_ffn_W': 3.252,
     'L3_ffn_bias': 8.0}
    for name, (base, spread) in spreads.items():
        noise = np.random.default_rng([zlib.crc32(name.encode()), seed]).standard_normal(out[name].shape)
        drawn = base * np.exp(spread * noise) if base else spread * noise
        out[name] = jnp.asarray(drawn.astype(out[name].dtype))
    for name, factor in factors.items():
        out[name] = (out[name] * factor).astype(out[name].dtype)
    return out
```

```python
from contextlib import ExitStack

import numpy as np

import concourse.bass as bass
from concourse import mybir

F32 = mybir.dt.float32
F16 = mybir.dt.float16
I32 = mybir.dt.int32
ALU = mybir.AluOpType
ACT = mybir.ActivationFunctionType
AX = mybir.AxisListType
ds = bass.ds

NB, S, D = 64, 32, 512
P = 128
KC = D // P
NT = NB * S // P
BT = P // S
U = 4
NG = NT // U
GT = U * P
NC = 16
E, R = 8, 16
NA = 32
FH, FM = 16, 128
DK = 32
HQ, HK, HD = 32, 8, 128
PAGES, PS, NPP = 64, 32, 16
HP = HK // 2
QH = HQ // HP
CL = NPP * PS
CC = CL // P
WS = 64.0
PSC = 1024.0
EPS = 1e-6
BIG = 1e30
WQ_COLS, WKV_COLS, WO_COLS = KC * QH * HD, KC * 4 * HD, QH * D
W3_COLS = WQ_COLS + WKV_COLS + WO_COLS
CH = 1024
W_PIECES = HP * W3_COLS // CH
KV_PIECES = PAGES * PS * HP * 512 // (P * CH)
TWO_PI = 2.0 * np.pi
MAGIC = 1.5 * 2.0 ** 23


def cody_waite():
    c1 = np.float32(np.floor(TWO_PI * 2 ** 8) / 2 ** 8)
    c2 = np.float32(np.floor((TWO_PI - float(c1)) * 2 ** 20) / 2 ** 20)
    c3 = np.float32(TWO_PI - float(c1) - float(c2))
    return float(c1), float(c2), float(c3)


def build(nc, a, out, debug=None):
    with ExitStack() as top:
        banks = [top.enter_context(nc.psum_tensor(f"bank{i}", [P, 512], F32)) for i in range(8)]
        halves = [b[:, :].bitcast(F16) for b in banks]
        dram = {
            "kv": nc.dram_tensor("kv_split", [HP * PAGES * PS, 1024], F16, kind="Internal").ap(),
            "w3": nc.dram_tensor("w3_split", [W_PIECES, P, 2 * CH], F16, kind="Internal").ap(),
            "bt": nc.dram_tensor("lora_b_split", [NA * R, 2 * D], F16, kind="Internal").ap(),
            "x3": nc.dram_tensor("x3_rows", [NB * S, D], F32, kind="Internal").ap(),
        }

        def keep(name, shape, dt):
            return top.enter_context(nc.sbuf_tensor(name, shape, dt))

        res = {
            "ident": keep("ident", [P, P], F16),
            "identf": keep("identf", [P, P], F32),
            "cos": keep("cos", [P, NT, HD // 2], F32),
            "sin": keep("sin", [P, NT, HD // 2], F32),
            "len": keep("seqlen", [P, NB], F32),
            "kvidx": keep("kvidx", [P, HP, NB * CC], I32),
            "x3T": keep("x3T", [P, 2, KC, NB * S], F16),
        }
        early(nc, a, dram, res, banks, halves)
        if debug:
            debug(nc, res, dram)
            return
        late(nc, a, dram, res, banks, halves, out)


def mm3(pe, psum, left, right, first, last):
    pe.matmul(psum, left(0), right(0), start=first, stop=False, skip_group_check=True)
    pe.matmul(psum, left(0), right(1), start=False, stop=False, skip_group_check=True)
    return pe.matmul(psum, left(1), right(0), start=False, stop=last, skip_group_check=True)


def early(nc, a, dram, res, banks, halves):
    with ExitStack() as ctx:
        def sb(name, shape, dt):
            return ctx.enter_context(nc.sbuf_tensor(name, shape, dt))

        w = {
            "BD0": sb("BD0", [P, 2, NT, P], F16), "BD2": sb("BD2", [P, 2, NT, P], F16),
            "A0": sb("A0", [P, 2, KC, P + E], F16), "B0": sb("B0", [P, 2, D], F16),
            "ATA": sb("ATA", [P, 2, KC, NA * R], F16), "W1": sb("W1", [P, 2, KC, D], F16),
            "bias1": sb("bias1", [P, KC], F32), "OH": sb("OH", [P, KC, D], F16),
            "UP": sb("UP", [P, 2, FH, FM], F16), "DN": sb("DN", [P, 2, FH, P], F16),
            "QK2": sb("QK2", [P, 2, KC, 2 * E * DK], F16), "W2": sb("W2", [P, 2, KC, D], F16),
            "A2": sb("A2", [P, 2, KC, P], F16), "B2": sb("B2", [P, 2, D], F16),
            "b2": sb("b2", [P, D], F32), "br": sb("br", [P, E], F32),
            "idx1": sb("idx1", [U * R, NT], I32), "ids": sb("ids", [1, NB], I32),
            "hmask": sb("hmask", [U * R, P], F32),
        }
        early_weights(nc, a, dram, res, w, banks, halves)
        early_layers(nc, a, dram, res, w, banks, halves)


def early_weights(nc, a, dram, res, w, banks, halves):
    RAW = 2048
    plan = [("A0", "A0", KC * (P + E), WS), ("B0", "B0", D, WS), ("ATA", "ATA", KC * NA * R, WS),
            ("UP", "UP", FH * FM, 1.0), ("DN", "DN", FH * P, 1.0), ("QK2", "QK2", KC * 512, WS),
            ("W2", "W2", KC * D, WS), ("A2", "A2", KC * P, WS), ("B2", "B2", D, WS)]
    W1C = D + NA * R + 1
    with ExitStack() as ctx:
        def sb(name, shape, dt):
            return ctx.enter_context(nc.sbuf_tensor(name, shape, dt))

        def sem(name):
            return ctx.enter_context(nc.semaphore(name))

        raw = sb("raw", [P, 2, RAW], F32)
        iota = sb("iota", [P, D], F32)
        pmod = sb("pmod", [P, 2], F32)
        condi = sb("condi", [P, NT], I32)
        condf = sb("condf", [P, NT], F32)
        crow = sb("crow", [P, NT], I32)
        G = sb("G", [P, 2, NT, S], F32)
        permi = sb("permi", [P, KC], I32)
        permf = sb("permf", [P, KC], F32)
        W1R = sb("W1R", [P, KC, W1C], F32)
        W1H = sb("W1H", [P, 2, KC, 2 * D], F16)
        BT1 = sb("BT1", [P, KC, 2, D], F16)
        id1 = sb("id1", [U * R, NT], I32)
        id1f = sb("id1f", [U * R, NT], F32)
        pgi = sb("pgi", [P, NB * CC], I32)
        pgf = sb("pgf", [P, NB * CC], F32)
        pgh = sb("pgh", [P, HP, NB * CC], F32)
        leni = sb("leni", [P, NB], I32)
        posi = sb("posi", [P, NT], I32)
        posf = sb("posf", [P, NT], F32)
        posf2 = sb("posf2", [P, NT], F32)
        freq = sb("freq", [P, HD // 2], F32)
        halfpi = sb("halfpi", [P, 1], F32)
        ang, turns, rest, rest2 = (raw[:, i // 2, (i % 2) * 1024:(i % 2) * 1024 + 1024].rearrange(
            "p (t f) -> p t f", t=NT) for i in range(4))

        small_in = sem("small_in")
        raw_in = [sem(f"raw_in{i}") for i in range(2)]
        hi_done, lo_done = sem("hi_done"), sem("lo_done")
        ints, rows_ready, gath0, gath1 = sem("ints"), sem("rows_ready"), sem("gath0"), sem("gath1")
        zeroed, bd_hi, bd_lo = sem("zeroed"), sem("bd_hi"), sem("bd_lo")
        w1_hi, w1_lo, w1_t, w1_out = sem("w1_hi"), sem("w1_lo"), sem("w1_t"), sem("w1_out")
        bt_out, angle, trig = sem("bt_out"), sem("angle"), sem("trig")

        small = [(res["identf"], a["c_ident"]), (iota, a["c_iota"]), (pmod, a["c_pmod"]),
                 (condi, a["cond_rep"]), (permi, a["perm_cols"]), (id1, a["adapter_rep"]),
                 (pgi, a["page_rep"]), (leni, a["len_rep"]), (posi, a["pos_rep"]),
                 (freq, a["c_freq"]), (w["ids"], a["adapter_ids"]), (w["hmask"], a["c_hmask"]),
                 (w["b2"], a["b2_rep"]), (w["br"], a["br_rep"])]

        def flat(t):
            if len(t.shape) == 3:
                return t[:, :, :]
            return t[:, :, :, :].rearrange("p h a b -> p h (a b)")

        with nc.Block() as block:
            @block.sync
            def _(sp):
                for dst, src in small:
                    sp.dma_start(dst[...], src).then_inc(small_in, 16)
                for n, (src, _, cols, _) in enumerate(plan):
                    if n >= 2:
                        sp.wait_ge(lo_done, n - 1)
                    sp.dma_start(raw[:, n % 2, 0:cols], a[src]).then_inc(raw_in[n % 2], 16)
                for c in range(KC):
                    sp.wait_ge(w1_out, KC + c + 1)
                    sp.dma_start(dram["bt"][c * P:(c + 1) * P, :],
                                 BT1[:, c, :, :].rearrange("p h n -> p (h n)")).then_inc(bt_out, 16)
                sp.wait_ge(bt_out, 16 * KC)

            @block.gpsimd
            def _(pool):
                pool.memset(w["BD0"][:, :, :, :], 0.0).then_inc(zeroed, 1)
                pool.memset(w["BD2"][:, :, :, :], 0.0).then_inc(zeroed, 1)
                pool.wait_ge(rows_ready, 1)
                for t in range(NT):
                    for layer, src in enumerate(("cond0", "cond2")):
                        pool.indirect_dma_start(G[:, layer, t, :], None, a[src],
                                                bass.IndirectOffsetOnAxis(crow[:, t:t + 1], 0)).then_inc(gath0, 16)
                pool.wait_ge(small_in, 16 * len(small))
                for c in range(KC):
                    pool.indirect_dma_start(W1R[:, c, :], None, a["w1_rows"],
                                            bass.IndirectOffsetOnAxis(permi[:, c:c + 1], 0)).then_inc(gath1, 16)

            @block.scalar
            def _(act):
                act.wait_ge(small_in, 16 * len(small))
                act.activation(res["ident"][:, :], res["identf"][:, :], ACT.Copy).then_inc(trig, 1)
                for n, (_, dst, cols, scale) in enumerate(plan):
                    act.wait_ge(raw_in[n % 2], 16 * (n // 2 + 1))
                    act.activation(flat(w[dst])[:, 0, :], raw[:, n % 2, 0:cols], ACT.Copy,
                                   scale=scale).then_inc(hi_done, 1)
                act.wait_ge(gath0, 16 * 2 * NT)
                act.wait_ge(zeroed, 2)
                for layer, name in enumerate(("BD0", "BD2")):
                    for b in range(BT):
                        q = slice(S * b, S * b + S)
                        act.activation(w[name][q, 0, :, q], G[q, layer, :, :], ACT.Copy).then_inc(bd_hi, 1)
                act.wait_ge(gath1, 16 * KC)
                for c in range(KC):
                    act.activation(W1H[:, 0, c, :], W1R[:, c, 0:2 * D], ACT.Copy, scale=WS).then_inc(w1_hi, 1)
                act.activation(w["bias1"][:, :], W1R[:, :, 2 * D], ACT.Copy).then_inc(w1_hi, 1)
                for n in range(2 * KC):
                    act.wait_ge(w1_t, n + 1)
                    if n < KC:
                        act.activation(w["W1"][:, :, n, :].bitcast(F32), halves[n].rearrange(
                            "p (h c) -> p h c", h=2).bitcast(F32), ACT.Copy).then_inc(w1_out, 1)
                    else:
                        act.activation(BT1[:, n - KC, :, :].bitcast(F32), halves[n].rearrange(
                            "p (h c) -> p h c", h=2).bitcast(F32), ACT.Copy).then_inc(w1_out, 1)
                act.wait_ge(angle, 9)
                act.activation(res["sin"][:, :, :], rest[:, :, :], ACT.Sin).then_inc(trig, 1)
                act.activation(res["cos"][:, :, :], rest2[:, :, :], ACT.Sin, bias=halfpi[:, 0:1],
                               scale=-1.0).then_inc(trig, 1)

            @block.vector
            def _(dve):
                dve.wait_ge(small_in, 16 * len(small))
                dve.tensor_copy(condf[:, :], condi[:, :]).then_inc(ints, 1)
                dve.wait_ge(ints, 1)
                dve.tensor_scalar(crow[:, :], condf[:, :], float(S), pmod[:, 0:1], ALU.mult, ALU.add).then_inc(rows_ready, 1)
                dve.tensor_copy(permf[:, :], permi[:, :]).then_inc(ints, 1)
                dve.tensor_copy(id1f[:, :], id1[:, :]).then_inc(ints, 1)
                dve.tensor_copy(pgf[:, :], pgi[:, :]).then_inc(ints, 1)
                dve.tensor_copy(res["len"][:, :], leni[:, :]).then_inc(ints, 1)
                dve.tensor_copy(posf[:, :], posi[:, :]).then_inc(ints, 1)
                dve.wait_ge(ints, 6)
                dve.tensor_scalar(w["idx1"][:, :], id1f[:, :], float(R), pmod[0:U * R, 1:2], ALU.mult, ALU.add).then_inc(ints, 1)
                for hp in range(HP):
                    dve.tensor_scalar(pgh[:, hp, :], pgf[:, :], float(PS), float(hp * PAGES * PS), ALU.mult, ALU.add).then_inc(ints, 1)
                dve.wait_ge(ints, 7 + HP)
                dve.tensor_scalar(res["kvidx"][:, :, :], pgh[:, :, :], pmod[:, 0:1], None, ALU.add).then_inc(ints, 1)
                for c in range(KC):
                    dve.tensor_scalar(w["OH"][:, c, :], iota[:, :], permf[:, c:c + 1], None, ALU.is_equal).then_inc(ints, 1)
                for n, (_, dst, cols, scale) in enumerate(plan):
                    dve.wait_ge(hi_done, n + 1)
                    dve.scalar_tensor_tensor(flat(w[dst])[:, 1, :], raw[:, n % 2, 0:cols], scale,
                                             flat(w[dst])[:, 0, :], ALU.mult, ALU.subtract).then_inc(lo_done, 1)
                for layer, name in enumerate(("BD0", "BD2")):
                    for b in range(BT):
                        q = slice(S * b, S * b + S)
                        dve.wait_ge(bd_hi, layer * BT + b + 1)
                        dve.tensor_tensor(w[name][q, 1, :, q], G[q, layer, :, :], w[name][q, 0, :, q],
                                          ALU.subtract).then_inc(bd_lo, 1)
                for c in range(KC):
                    dve.wait_ge(w1_hi, c + 1)
                    dve.scalar_tensor_tensor(W1H[:, 1, c, :], W1R[:, c, 0:2 * D], WS, W1H[:, 0, c, :],
                                             ALU.mult, ALU.subtract).then_inc(w1_lo, 1)
                dve.wait_ge(lo_done, len(plan))
                c1, c2, c3 = cody_waite()
                n = [0]

                def step(ins):
                    n[0] += 1
                    ins.then_inc(angle, 1)
                    dve.wait_ge(angle, n[0])
                step(dve.memset(halfpi[:, :], float(np.pi / 2)))
                step(dve.tensor_scalar(posf2[:, :], posf[:, :], pmod[:, 0:1], None, ALU.add))
                step(dve.tensor_tensor(ang[:, :, :], posf2[:, :].unsqueeze(2).to_broadcast([P, NT, HD // 2]),
                                       freq[:, :].unsqueeze(1).to_broadcast([P, NT, HD // 2]), ALU.mult))
                step(dve.tensor_scalar(rest[:, :, :], ang[:, :, :], float(1.0 / TWO_PI), MAGIC, ALU.mult, ALU.add))
                step(dve.tensor_scalar(turns[:, :, :], rest[:, :, :], MAGIC, None, ALU.subtract))
                step(dve.scalar_tensor_tensor(rest[:, :, :], turns[:, :, :], -c1, ang[:, :, :], ALU.mult, ALU.add))
                step(dve.scalar_tensor_tensor(rest2[:, :, :], turns[:, :, :], -c2, rest[:, :, :], ALU.mult, ALU.add))
                step(dve.scalar_tensor_tensor(rest[:, :, :], turns[:, :, :], -c3, rest2[:, :, :], ALU.mult, ALU.add))
                step(dve.scalar_tensor_tensor(rest2[:, :, :], rest[:, :, :], -1.0, rest[:, :, :], ALU.mult, ALU.max))

            @block.tensor
            def _(pe):
                pe.wait_ge(trig, 1)
                pe.wait_ge(w1_lo, KC)
                for n in range(2 * KC):
                    for hl in range(2):
                        for c in range(KC):
                            last = pe.transpose(halves[n][:, (hl * KC + c) * P:(hl * KC + c + 1) * P],
                                                W1H[:, hl, c, n * P:(n + 1) * P], res["ident"][:, :])
                    last.then_inc(w1_t, 1)


def early_layers(nc, a, dram, res, w, banks, halves):
    WG, KG = W_PIECES // NG, KV_PIECES // NG
    QP = CH // 512
    MP = HP // QP
    with ExitStack() as ctx:
        def sb(name, shape, dt):
            return ctx.enter_context(nc.sbuf_tensor(name, shape, dt))

        def sem(name):
            return ctx.enter_context(nc.semaphore(name))

        X = sb("X", [P, U, D], F32)
        XH = sb("XH", [P, 2, U, D], F16)
        XT = sb("XT", [P, 2, KC, GT], F16)
        UT = sb("UT", [P, 2, KC, GT], F16)
        LL = sb("LL", [P, U, P + E], F32)
        LP = sb("LP", [P, U, P], F32)
        LH = sb("LH", [P, 2, U, P], F16)
        LT = sb("LT", [P, U, 2, P], F16)
        sm = sb("sm", [P, 3, U, E], F32)
        smr = sb("smr", [P, 3, U], F32)
        ALT = sb("ALT", [P, 2 * KC, U, U * R], F16)
        icol = sb("icol", [U * R, U], I32)
        HF = sb("HF", [U * R, GT], F32)
        HT = sb("HT", [U * R, 2, GT], F16)
        YF = sb("YF", [P, 2, GT], F32)
        YT = sb("YT", [P, 2, KC, GT], F16)
        ffn = sb("ffn", [P, 4 * GT], F32)
        GF = ffn[:, 0:2 * GT].rearrange("p (s n) -> p s n", s=2)
        GH = ffn[:, 2 * GT:4 * GT].bitcast(F16).rearrange("p (s h n) -> p s h n", s=2, h=2)
        BG = ffn[0:U * R, :].bitcast(F16).rearrange("p (u h n) -> p u h n", u=U, h=2)
        TT = UT
        QS, PR = (GF[:, i, :].rearrange("p (s n) -> p s n", s=2) for i in range(2))
        tick = sb("tick", [P, 4], F32)
        raw = sb("bg_raw", [P, 2, CH], F32)
        spl = sb("bg_split", [P, 2, CH], F16)

        names = ("x_in group_done xh_hi xh_lo ut_mm ut_hi ut_lo ll_mm ll_ev sm_step sm_exp lp lh_hi lh_lo lt_mm "
                 "lt_ev o_mm x_up xt_mm xt_act xt_dve alt_in ic_in bg_in h_mm hf ht_hi ht_lo y_mm yf yt_hi yt_lo "
                 "up_mm gelu gh_hi gh_lo dn_mm tt_hi tt_lo op_mm xb qk_mm qs pr sc hh_mm hh o2_mm x_out "
                 "bulk_hi bulk_lo bulk_in0 bulk_in1 hi_out lo_out il factor").split()
        s = {n: sem(n) for n in names}
        bulk_in = [s["bulk_in0"], s["bulk_in1"]]

        x_rows = a["x"].rearrange("(g u p) d -> g p u d", u=U, p=P)
        x3_rows = dram["x3"].rearrange("(g u p) d -> g p u d", u=U, p=P)
        bulk = a["bulk"]
        SM = 12

        with nc.Block() as block:
            def kv_rows(r, m, q, h):
                row = (m * QP + q) * (PAGES * PS)
                return dram["kv"][ds(r * P + row, P), h * 512:h * 512 + 512]

            def store_caches(sp, n, r, m):
                for h, (done, stored) in enumerate(((s["bulk_hi"], s["hi_out"]), (s["bulk_lo"], s["lo_out"]))):
                    sp.wait_ge(done, n + 1 + h)
                    for q in range(QP):
                        sp.dma_start(kv_rows(r, m, q, h), spl[:, h, q * 512:(q + 1) * 512]).then_inc(stored, 16)

            def load_piece(sp, n, slot, first):
                if not first:
                    sp.wait_ge(s["bulk_lo"], n)
                sp.dma_start(raw[:, slot, :], bulk[ds(n, 1), :, :].rearrange("o p c -> (o p) c")).then_inc(bulk_in[slot], 16)

            @block.sync
            def _(sp):
                sp.sem_inc(s["hi_out"], 16 * QP)
                sp.sem_inc(s["lo_out"], 16 * QP)
                load_piece(sp, 0, 0, True)
                load_piece(sp, 1, 1, True)
                with sp.Fori(0, NG) as g:
                    sp.wait_ge(s["group_done"], g + 1)
                    sp.dma_start(X[:, :, :], x_rows[ds(g, 1), :, :, :].rearrange("o p u d -> (o p) u d")).then_inc(s["x_in"], 16)
                    with sp.Fori(0, KG // 2) as k:
                        for m in range(MP):
                            n = g * (KG + WG) + k * 2 + m
                            store_caches(sp, n, g * (KG // 2) + k, m)
                            load_piece(sp, n + 2, m, False)
                    with sp.Fori(0, WG // 2) as k:
                        for m in range(2):
                            n = g * (KG + WG) + KG + k * 2 + m
                            sp.wait_ge(s["bulk_hi"], n + 1)
                            w_n = g * WG + k * 2 + m
                            sp.dma_start(dram["w3"][ds(w_n, 1), :, 0:CH].rearrange("o p c -> (o p) c"), spl[:, 0, :]).then_inc(s["hi_out"], 16 * QP)
                            sp.wait_ge(s["bulk_lo"], n + 2)
                            sp.dma_start(dram["w3"][ds(w_n, 1), :, CH:2 * CH].rearrange("o p c -> (o p) c"), spl[:, 1, :]).then_inc(s["lo_out"], 16 * QP)
                            load_piece(sp, n + 2, m, False)
                    sp.wait_ge(s["x_up"], g * 12 + 12)
                    sp.dma_start(x3_rows[ds(g, 1), :, :, :].rearrange("o p u d -> (o p) u d"), X[:, :, :]).then_inc(s["x_out"], 16)
                sp.wait_ge(s["x_out"], 16 * NG)
                sp.wait_ge(s["hi_out"], 16 * QP * (W_PIECES + KV_PIECES + 1))
                sp.wait_ge(s["lo_out"], 16 * QP * (W_PIECES + KV_PIECES + 1))
                for slot in range(2):
                    sp.wait_ge(bulk_in[slot], 16 * ((W_PIECES + KV_PIECES) // 2 + 1))

            @block.gpsimd
            def _(pool):
                pool.memset(tick[:, 1:2], 0.0).then_inc(s["bulk_lo"], 1)
                pool.memset(tick[:, 3:4], WS).then_inc(s["factor"], 1)
                pool.wait_ge(s["factor"], 1)
                with pool.Fori(0, NG) as g:
                    pool.wait_ge(s["group_done"], g + 1)
                    pool.tensor_copy(icol[:, :], w["idx1"][:, ds(g * U, U)]).then_inc(s["ic_in"], 1)
                    for b in range(U * BT):
                        v = pool.value_load(w["ids"][0:1, ds(g * (U * BT) + b, 1)], min_val=0, max_val=NA - 1)
                        pool.tensor_copy(ALT[:, :, b // BT, (b % BT) * R:(b % BT + 1) * R],
                                         w["ATA"][:, :, :, ds(v * R, R)].rearrange("p h k r -> p (h k) r")).then_inc(s["alt_in"], 1)
                    pool.wait_ge(s["ic_in"], g + 1)
                    pool.tensor_tensor(tick[0:U * R, 2:3], w["hmask"][:, 0:1], w["hmask"][:, 0:1], ALU.add).then_inc(s["il"], 1)
                    for u in range(U):
                        pool.indirect_dma_start(BG[:, u, :, :].rearrange("p h n -> p (h n)"), None, dram["bt"],
                                                bass.IndirectOffsetOnAxis(icol[:, u:u + 1], 0)).then_inc(s["bg_in"], 16)
                    for pieces, before, weights in ((KG, 0, False), (WG, KG, True)):
                        with pool.Fori(0, pieces // 2) as k:
                            for m in range(2):
                                n = g * (KG + WG) + (k * 2 + (before + m))
                                pool.wait_ge(bulk_in[m], (g * ((KG + WG) // 2) + (k + before // 2)) * 16 + 16)
                                pool.wait_ge(s["bulk_lo"], n + 1)
                                if weights:
                                    pool.tensor_tensor(raw[:, m, :], raw[:, m, :], tick[:, 3:4].to_broadcast([P, CH]), ALU.mult).then_inc(s["factor"], 1)
                                    pool.wait_ge(s["factor"], g * WG + (k * 2 + (m + 2)))
                                pool.wait_ge(s["hi_out"], n * 16 * QP + 16 * QP)
                                pool.tensor_tensor(spl[:, 0, :], raw[:, m, :], tick[:, 1:2].to_broadcast([P, CH]), ALU.add).then_inc(s["bulk_hi"], 1)
                                pool.wait_ge(s["bulk_hi"], n + 1)
                                pool.wait_ge(s["lo_out"], n * 16 * QP + 16 * QP)
                                pool.tensor_tensor(spl[:, 1, :], raw[:, m, :], spl[:, 0, :], ALU.subtract).then_inc(s["bulk_lo"], 1)

            @block.scalar
            def _(act):
                with act.Fori(0, NG) as g:
                    def split_x(k):
                        for u in range(U):
                            if k == 0 and u == 0:
                                act.wait_ge(s["x_in"], g * 16 + 16)
                            if k > 0:
                                act.wait_ge(s["x_up"], g * 12 + (k - 1) * U + u + 1)
                            act.activation(XH[:, 0, u, :], X[:, u, :], ACT.Copy).then_inc(s["xh_hi"], 1)

                    def mixed(k):
                        for u in range(U):
                            act.wait_ge(s["ut_mm"], g * 2 * U + k * U + u + 1)
                            act.activation(UT[:, 0, :, u * P:(u + 1) * P],
                                           banks[u][:, :].rearrange("p (c t) -> p c t", c=KC), ACT.Copy).then_inc(s["ut_hi"], 1)

                    def softmax_exp(k):
                        act.wait_ge(s["sm_step"], g * SM + k * (SM // 2) + 3)
                        act.activation(sm[:, 1, :, :], sm[:, 0, :, :], ACT.Exp).then_inc(s["sm_exp"], 1)

                    def low_rows(k):
                        act.wait_ge(s["lp"], g * 2 + k + 1)
                        act.activation(LH[:, 0, :, :], LP[:, :, :], ACT.Copy).then_inc(s["lh_hi"], 1)
                        act.wait_ge(s["lt_mm"], g * 2 + k + 1)
                        act.activation(LT[:, :, :, :].rearrange("p u h t -> p (u h t)").bitcast(F32),
                                       banks[(0, 1)[k]][:, :], ACT.Copy).then_inc(s["lt_ev"], 1)

                    act.wait_ge(s["group_done"], g + 1)
                    split_x(0)
                    mixed(0)
                    softmax_exp(0)
                    low_rows(0)
                    split_x(1)
                    for u in (0, 2):
                        act.wait_ge(s["xt_mm"], g * 2 * U + u + 1)
                        act.activation(XT[:, :, :, u * P:(u + 1) * P].rearrange("p h c t -> p (h c) t").bitcast(F32),
                                       halves[u].rearrange("p (n t) -> p n t", t=P).bitcast(F32), ACT.Copy).then_inc(s["xt_act"], 1)
                    act.wait_ge(s["hf"], g + 1)
                    act.activation(HT[:, 0, :], HF[:, :], ACT.Copy).then_inc(s["ht_hi"], 1)
                    for c in range(KC):
                        act.wait_ge(s["y_mm"], g * KC + c + 1)
                        if c >= 2:
                            act.wait_ge(s["yt_lo"], g * KC + c - 1)
                        act.activation(YF[:, c % 2, :], banks[c][:, :], ACT.Identity, bias=w["bias1"][:, c:c + 1],
                                       scale=1.0 / WS).then_inc(s["yf"], 1)
                        act.wait_ge(s["yf"], g * KC + c + 1)
                        act.activation(YT[:, 0, c, :], YF[:, c % 2, :], ACT.Copy).then_inc(s["yt_hi"], 1)
                    for k in range(FH):
                        act.wait_ge(s["up_mm"], g * FH + k + 1)
                        if k >= 2:
                            act.wait_ge(s["gh_lo"], g * FH + k - 1)
                        act.activation(GF[:, k % 2, :], banks[4 + k % 2][:, :], ACT.Gelu).then_inc(s["gelu"], 1)
                        if k % BT == 1 and k > BT:
                            q = k // BT - 1
                            act.wait_ge(s["dn_mm"], g * FH + q * BT + BT)
                            act.activation(TT[:, 0, q, :], banks[6 + q % 2][:, :], ACT.Copy).then_inc(s["tt_hi"], 1)
                    act.wait_ge(s["dn_mm"], g * FH + FH)
                    act.activation(TT[:, 0, KC - 1, :], banks[6 + (KC - 1) % 2][:, :], ACT.Copy).then_inc(s["tt_hi"], 1)
                    split_x(2)
                    mixed(1)
                    for u in range(U):
                        act.wait_ge(s["qk_mm"], g * U + u + 1)
                        if u >= 2:
                            act.wait_ge(s["pr"], g * U + u - 1)
                        act.activation(QS[:, u % 2, :], banks[u][:, 0:E * DK], ACT.Copy,
                                       scale=float(1.0 / (WS * WS * np.sqrt(DK)))).then_inc(s["qs"], 1)
                    softmax_exp(1)
                    low_rows(1)
                    split_x(3)
                    for u in (0, 2):
                        act.wait_ge(s["xt_mm"], g * 2 * U + U + u + 1)
                        act.activation(res["x3T"][:, :, :, ds(g * GT + u * P, P)].rearrange("p h c t -> p (h c) t"),
                                       halves[1 + u].rearrange("p (n t) -> p n t", t=P), ACT.Copy).then_inc(s["xt_act"], 1)

            @block.vector
            def _(dve):
                dve.memset(tick[:, 0:1], 0.0).then_inc(s["group_done"], 1)
                with dve.Fori(0, NG) as g:
                    def split_x(k):
                        for u in range(U):
                            dve.wait_ge(s["xh_hi"], g * 4 * U + k * U + u + 1)
                            dve.tensor_tensor(XH[:, 1, u, :], X[:, u, :], XH[:, 0, u, :], ALU.subtract).then_inc(s["xh_lo"], 1)

                    def mixed(k):
                        for u in range(U):
                            dve.wait_ge(s["ut_hi"], g * 2 * U + k * U + u + 1)
                            dve.tensor_tensor(UT[:, 1, :, u * P:(u + 1) * P],
                                              banks[u][:, :].rearrange("p (c t) -> p c t", c=KC),
                                              UT[:, 0, :, u * P:(u + 1) * P], ALU.subtract).then_inc(s["ut_lo"], 1)

                    def softmax(k, scale):
                        n = [0]

                        def step(ins):
                            n[0] += 1
                            ins.then_inc(s["sm_step"], 1)
                            dve.wait_ge(s["sm_step"], g * SM + k * (SM // 2) + n[0])
                        logits = LL[:, :, P:P + E]
                        step(dve.tensor_reduce(smr[:, 0, :], logits, AX.X, ALU.max))
                        step(dve.tensor_copy(tick[:, 0:1], smr[:, 0, 0:1]))
                        step(dve.tensor_tensor(sm[:, 0, :, :], logits, smr[:, 0, :].unsqueeze(2).to_broadcast([P, U, E]), ALU.subtract))
                        dve.wait_ge(s["sm_exp"], g * 2 + k + 1)
                        step(dve.tensor_reduce(smr[:, 1, :], sm[:, 1, :, :], AX.X, ALU.add))
                        step(dve.reciprocal(smr[:, 2, :], smr[:, 1, :]))
                        step(dve.scalar_tensor_tensor(sm[:, 2, :, :], sm[:, 1, :, :], scale,
                                                      smr[:, 2, :].unsqueeze(2).to_broadcast([P, U, E]), ALU.mult, ALU.mult))
                        assert n[0] == SM // 2
                        dve.tensor_tensor(LP[:, :, :].rearrange("p u (e r) -> p u e r", r=R),
                                          LL[:, :, 0:P].rearrange("p u (e r) -> p u e r", r=R),
                                          sm[:, 2, :, :].unsqueeze(3).to_broadcast([P, U, E, R]), ALU.mult).then_inc(s["lp"], 1)
                        dve.wait_ge(s["lh_hi"], g * 2 + k + 1)
                        dve.tensor_tensor(LH[:, 1, :, :], LP[:, :, :], LH[:, 0, :, :], ALU.subtract).then_inc(s["lh_lo"], 1)

                    dve.wait_ge(s["group_done"], g + 1)
                    split_x(0)
                    mixed(0)
                    for u in range(U):
                        dve.wait_ge(s["ll_mm"], g * U + u + 1)
                        dve.tensor_scalar(LL[:, u, :], banks[4 + u][:, 0:P + E], 1.0 / WS, None, ALU.mult).then_inc(s["ll_ev"], 1)
                    dve.wait_ge(s["ll_ev"], g * (U + 1) + U)
                    dve.tensor_tensor(LL[:, :, P:P + E], LL[:, :, P:P + E],
                                      w["br"][:, :].unsqueeze(1).to_broadcast([P, U, E]), ALU.add).then_inc(s["ll_ev"], 1)
                    dve.wait_ge(s["ll_ev"], g * (U + 1) + U + 1)
                    softmax(0, 2.0 * E)
                    for u in range(U):
                        dve.wait_ge(s["o_mm"], g * U + u + 1)
                        dve.scalar_tensor_tensor(X[:, u, :], banks[4 + u][:, :], 1.0 / WS, X[:, u, :], ALU.mult, ALU.add).then_inc(s["x_up"], 1)
                    split_x(1)
                    for u in (1, 3):
                        dve.wait_ge(s["xt_mm"], g * 2 * U + u + 1)
                        dve.tensor_copy(XT[:, :, :, u * P:(u + 1) * P].rearrange("p h c t -> p (h c) t").bitcast(F32),
                                        halves[u].rearrange("p (n t) -> p n t", t=P).bitcast(F32)).then_inc(s["xt_dve"], 1)
                    dve.wait_ge(s["h_mm"], g + 1)
                    dve.tensor_tensor(HF[:, :].rearrange("p (u t) -> p u t", t=P),
                                      banks[4][0:U * R, :].rearrange("p (u t) -> p u t", t=P),
                                      w["hmask"][:, :].unsqueeze(1).to_broadcast([U * R, U, P]), ALU.mult).then_inc(s["hf"], 1)
                    dve.wait_ge(s["ht_hi"], g + 1)
                    dve.tensor_tensor(HT[:, 1, :], HF[:, :], HT[:, 0, :], ALU.subtract).then_inc(s["ht_lo"], 1)
                    for c in range(KC):
                        dve.wait_ge(s["yt_hi"], g * KC + c + 1)
                        dve.tensor_tensor(YT[:, 1, c, :], YF[:, c % 2, :], YT[:, 0, c, :], ALU.subtract).then_inc(s["yt_lo"], 1)
                    for k in range(FH):
                        dve.wait_ge(s["gelu"], g * FH + k + 1)
                        if k >= 2:
                            dve.wait_ge(s["dn_mm"], g * FH + k - 1)
                        dve.tensor_copy(GH[:, k % 2, 0, :], GF[:, k % 2, :]).then_inc(s["gh_hi"], 1)
                        dve.wait_ge(s["gh_hi"], g * FH + k + 1)
                        dve.tensor_tensor(GH[:, k % 2, 1, :], GF[:, k % 2, :], GH[:, k % 2, 0, :], ALU.subtract).then_inc(s["gh_lo"], 1)
                        if k % BT == 2 and k > BT:
                            q = k // BT - 1
                            dve.wait_ge(s["tt_hi"], g * KC + q + 1)
                            dve.tensor_tensor(TT[:, 1, q, :], banks[6 + q % 2][:, :], TT[:, 0, q, :], ALU.subtract).then_inc(s["tt_lo"], 1)
                    dve.wait_ge(s["tt_hi"], g * KC + KC)
                    dve.tensor_tensor(TT[:, 1, KC - 1, :], banks[6 + (KC - 1) % 2][:, :], TT[:, 0, KC - 1, :], ALU.subtract).then_inc(s["tt_lo"], 1)
                    for u in range(U):
                        dve.wait_ge(s["op_mm"], g * U + u + 1)
                        dve.tensor_tensor(X[:, u, :], banks[u][:, :], X[:, u, :], ALU.add).then_inc(s["x_up"], 1)
                    split_x(2)
                    dve.wait_ge(s["xh_lo"], g * 4 * U + 3 * U)
                    dve.tensor_tensor(X[:, :, :], X[:, :, :], w["b2"][:, :].unsqueeze(1).to_broadcast([P, U, D]), ALU.add).then_inc(s["xb"], 1)
                    mixed(1)
                    for u in range(U):
                        dve.wait_ge(s["qs"], g * U + u + 1)
                        if u >= 2:
                            dve.wait_ge(s["sc"], g * U + u - 1)
                        dve.tensor_tensor(PR[:, u % 2, :], banks[u][:, E * DK:2 * E * DK], QS[:, u % 2, :], ALU.mult).then_inc(s["pr"], 1)
                        dve.wait_ge(s["pr"], g * U + u + 1)
                        dve.tensor_reduce(LL[:, u, P:P + E], PR[:, u % 2, :].rearrange("p (e k) -> p e k", k=DK), AX.X, ALU.add).then_inc(s["sc"], 1)
                    dve.wait_ge(s["hh_mm"], g + 1)
                    dve.tensor_scalar(LL[:, :, 0:P], banks[4][:, :].rearrange("p (u t) -> p u t", t=P), 1.0 / WS, None, ALU.mult).then_inc(s["hh"], 1)
                    dve.wait_ge(s["sc"], g * U + U)
                    dve.wait_ge(s["hh"], g + 1)
                    softmax(1, 1.0)
                    dve.wait_ge(s["xb"], g + 1)
                    for u in range(U):
                        dve.wait_ge(s["o2_mm"], g * U + u + 1)
                        dve.scalar_tensor_tensor(X[:, u, :], banks[(5, 6, 7, 0)[u]][:, :], 1.0 / WS, X[:, u, :], ALU.mult, ALU.add).then_inc(s["x_up"], 1)
                    split_x(3)
                    for u in (1, 3):
                        dve.wait_ge(s["xt_mm"], g * 2 * U + U + u + 1)
                        dve.tensor_copy(res["x3T"][:, :, :, ds(g * GT + u * P, P)].rearrange("p h c t -> p (h c) t"),
                                        halves[1 + u].rearrange("p (n t) -> p n t", t=P)).then_inc(s["xt_dve"], 1)
                    dve.wait_ge(s["xt_act"], g * 4 + 4)
                    dve.wait_ge(s["xt_dve"], g * 4 + 4)
                    dve.wait_ge(s["x_out"], g * 16 + 16)
                    dve.memset(tick[:, 0:1], 0.0).then_inc(s["group_done"], 1)

            @block.tensor
            def _(pe):
                with pe.Fori(0, NG) as g:
                    def mix(k, bd):
                        for u in range(U):
                            pe.wait_ge(s["xh_lo"], g * 4 * U + 2 * k * U + u + 1)
                            for c in range(KC):
                                last = mm3(pe, banks[u][:, c * P:(c + 1) * P],
                                           lambda h: XH[:, h, u, c * P:(c + 1) * P],
                                           lambda h: bd[:, h, ds(g * U + u, 1), :].rearrange("p o t -> p (o t)"), True, True)
                            last.then_inc(s["ut_mm"], 1)

                    def low_t(k):
                        pe.wait_ge(s["lh_lo"], g * 2 + k + 1)
                        for u in range(U):
                            for h in range(2):
                                last = pe.transpose(halves[k][:, (u * 2 + h) * P:(u * 2 + h + 1) * P], LH[:, h, u, :], res["ident"][:, :])
                        last.then_inc(s["lt_mm"], 1)

                    def turn_x(k, bank0):
                        for u in range(U):
                            pe.wait_ge(s["xh_lo"], g * 4 * U + (2 * k + 1) * U + u + 1)
                            for h in range(2):
                                for c in range(KC):
                                    last = pe.transpose(halves[bank0 + u][:, (h * KC + c) * P:(h * KC + c + 1) * P],
                                                        XH[:, h, u, c * P:(c + 1) * P], res["ident"][:, :])
                            last.then_inc(s["xt_mm"], 1)

                    def rows(bank, cols, src, u, wt, first=True, last=True):
                        for c in range(KC):
                            ins = mm3(pe, bank, lambda h: src[:, h, c, u * P:(u + 1) * P],
                                      lambda h: wt[:, h, c, 0:cols], first and c == 0, last and c == KC - 1)
                        return ins

                    pe.wait_ge(s["group_done"], g + 1)
                    mix(0, w["BD0"])
                    for u in range(U):
                        pe.wait_ge(s["ut_lo"], g * 2 * U + u + 1)
                        rows(banks[4 + u][:, 0:P + E], P + E, UT, u, w["A0"]).then_inc(s["ll_mm"], 1)
                    low_t(0)
                    pe.wait_ge(s["lt_ev"], g * 2 + 1)
                    for u in range(U):
                        mm3(pe, banks[4 + u][:, :], lambda h: LT[:, u, h, :], lambda h: w["B0"][:, h, :], True, True).then_inc(s["o_mm"], 1)
                    turn_x(0, 0)
                    pe.wait_ge(s["xt_act"], g * 4 + 2)
                    pe.wait_ge(s["xt_dve"], g * 4 + 2)
                    pe.wait_ge(s["alt_in"], g * (U * BT) + U * BT)
                    for u in range(U):
                        for c in range(KC):
                            last = mm3(pe, banks[4][0:U * R, u * P:(u + 1) * P], lambda h: ALT[:, h * KC + c, u, :],
                                       lambda h: XT[:, h, c, u * P:(u + 1) * P], c == 0, c == KC - 1)
                    last.then_inc(s["h_mm"], 1)
                    for o in range(KC):
                        for c in range(KC):
                            mm3(pe, banks[o][:, :], lambda h: w["W1"][:, h, c, o * P:(o + 1) * P],
                                lambda h: XT[:, h, c, :], c == 0, False)
                    pe.wait_ge(s["ht_lo"], g + 1)
                    pe.wait_ge(s["bg_in"], g * 16 * U + 16 * U)
                    for o in range(KC):
                        for u in range(U):
                            last = mm3(pe, banks[o][:, u * P:(u + 1) * P], lambda h: BG[:, u, h, o * P:(o + 1) * P],
                                       lambda h: HT[:, h, u * P:(u + 1) * P], False, True)
                        last.then_inc(s["y_mm"], 1)

                    def up(k):
                        if k % BT == 0:
                            pe.wait_ge(s["yt_lo"], g * KC + k // BT + 1)
                        if k >= 2:
                            pe.wait_ge(s["gelu"], g * FH + k - 1)
                        mm3(pe, banks[4 + k % 2][:, :], lambda h: w["UP"][:, h, k, :],
                            lambda h: YT[:, h, k // BT, :], True, True).then_inc(s["up_mm"], 1)

                    def down(k):
                        q = k // BT
                        pe.wait_ge(s["gh_lo"], g * FH + k + 1)
                        if k % BT == 0 and q >= 2:
                            pe.wait_ge(s["tt_lo"], g * KC + q - 1)
                        mm3(pe, banks[6 + q % 2][:, :], lambda h: w["DN"][:, h, k, :],
                            lambda h: GH[:, k % 2, h, :], k % BT == 0, k % BT == BT - 1).then_inc(s["dn_mm"], 1)

                    up(0)
                    for k in range(FH):
                        if k + 1 < FH:
                            up(k + 1)
                        down(k)
                    pe.wait_ge(s["tt_lo"], g * KC + KC)
                    for u in range(U):
                        for c in range(KC):
                            for h in range(2):
                                last = pe.matmul(banks[u][:, :], TT[:, h, c, u * P:(u + 1) * P], w["OH"][:, c, :],
                                                 start=c == 0 and h == 0, stop=c == KC - 1 and h == 1)
                        last.then_inc(s["op_mm"], 1)
                    mix(1, w["BD2"])
                    for u in range(U):
                        pe.wait_ge(s["ut_lo"], g * 2 * U + U + u + 1)
                        rows(banks[u][:, :], 2 * E * DK, UT, u, w["QK2"]).then_inc(s["qk_mm"], 1)
                    for u in range(U):
                        last = rows(banks[4][:, u * P:(u + 1) * P], P, UT, u, w["A2"])
                    last.then_inc(s["hh_mm"], 1)
                    for u in range(U):
                        if u == 3:
                            pe.wait_ge(s["pr"], g * U + 1)
                        rows(banks[(5, 6, 7, 0)[u]][:, :], D, UT, u, w["W2"], last=False)
                    pe.wait_ge(s["pr"], g * U + 2)
                    low_t(1)
                    pe.wait_ge(s["lt_ev"], g * 2 + 2)
                    for u in range(U):
                        mm3(pe, banks[(5, 6, 7, 0)[u]][:, :], lambda h: LT[:, u, h, :], lambda h: w["B2"][:, h, :],
                            False, True).then_inc(s["o2_mm"], 1)
                    turn_x(1, 1)


def late(nc, a, dram, res, banks, halves, out):
    with ExitStack() as ctx:
        Y = ctx.enter_context(nc.sbuf_tensor("Y", [P, NT, D], F32))
        attention(nc, a, dram, res, banks, halves, Y)
        last_ffn(nc, a, dram, res, banks, halves, Y, out)


def attention(nc, a, dram, res, banks, halves, Y):
    NR = HP * NT
    J = 2 * BT
    HR = HQ // HK
    WQ = HD * HR
    SC = 1.0 / float(np.sqrt(HD))
    BF16 = mybir.dt.bfloat16
    WQ_RANGE = range(WQ_COLS // CH)
    WKV_RANGE = range(WQ_COLS // CH, (WQ_COLS + WKV_COLS) // CH)
    WO_RANGE = range((WQ_COLS + WKV_COLS) // CH, W3_COLS // CH)
    with ExitStack() as ctx:
        def sb(name, shape, dt):
            return ctx.enter_context(nc.sbuf_tensor(name, shape, dt))

        W3 = sb("W3", [P, 2, W3_COLS], F16)
        wq = W3[:, :, 0:WQ_COLS].rearrange("p h (c n) -> p h c n", c=KC)
        wkv = W3[:, :, WQ_COLS:WQ_COLS + WKV_COLS].rearrange("p h (c n) -> p h c n", c=KC)
        wo = W3[:, :, WQ_COLS + WKV_COLS:].rearrange("p h (q n) -> p h q n", q=QH)
        KV = sb("KV", [P, BT, CC, 1024], F16)
        KT = sb("KT", [P, 2, 2, CL], F16)
        SS = sb("SS", [P, 2, CL + S], F32)
        PT = sb("PT", [P, 2, 2, CL + P], F16)
        MK = sb("MK", [P, BT, CL], BF16)
        iota = sb("iota2", [P, CL], F32)
        QT = sb("QT", [P, 2, J, P], F16)
        QTV = [QT[:, i, :, :].rearrange("p (b v) (h t) -> p v h b t", v=2, t=S) for i in range(2)]
        KN = sb("KN", [P, 2, 2, P], F16)
        TK = sb("TK", [P, 2 * HD], F32)
        TQ = sb("TQ", [P, 2, WQ], F32)
        T2 = sb("T2", [P, WQ], F32)
        VH = sb("VH", [P, 2, 2, 2 * HD], F16)
        VN = sb("VN", [S, BT, 2, 2 * HD], F16)
        SN = sb("SN", [P, J, S], F32)
        mnew = sb("mnew", [P, J], F32)
        OT = sb("OT", [P, 2, QH, P], F16)
        tab = sb("tab", [P, 4, HD], F32)
        nw = sb("nw", [P, 4, HD], F32)
        ssq = sb("ssq", [P, QH + 2], F32)
        var = sb("var", [P, QH + 2], F32)
        rstd = sb("rstd", [P, QH + 2], F32)
        power = sb("power", [P, 1], F32)
        junk = sb("junk", [P, HD], F32)
        ic = sb("ic", [P, BT, CC], I32)
        lcol = sb("lcol", [P, BT], F32)
        mark = sb("mark", [P, 1], F32)
        st = sb("st", [P, 2, 4], F32)

        names = ("const_in kt_mm kt_ev s_mm ttr sn_cp neg exp rec prob t_mm pt_hi pt_lo pv_mm o_hi o_lo "
                 "kv_mm q_mm wo_mm kn_mm qt_mm sn_mm sq vh_hi vh_lo rope t2_free turned var_ok pow_ok roped kn_hi "
                 "kn_lo qt_hi qt_lo sn_ev mnew_ok y_add kv_in0 kv_in1 kv_in2 kv_in3 vn_in0 vn_in1 vn_in2 vn_in3 "
                 "wkv_in wq_in wo_in ic_ok lc_ok mask_ok marked tab_ok nw_ok y_zero").split()
        s = {n: ctx.enter_context(nc.semaphore("a_" + n)) for n in names}
        kv_in = [s[f"kv_in{b}"] for b in range(BT)]
        vn_in = [s[f"vn_in{b}"] for b in range(BT)]
        KTB, PTB, PB = banks[2], banks[3], [banks[6], banks[7]]
        SB = [banks[0], banks[1]]
        OB = [banks[4], banks[5]]
        consts = [(iota, a["c_iota"]), (nw, a["norm_w"])]

        with nc.Block() as block:
            @block.sync
            def _(sp):
                def load_w(hp, pieces, name):
                    for i in pieces:
                        sp.dma_start(W3[:, :, i * CH:(i + 1) * CH],
                                     dram["w3"][ds(hp * (W3_COLS // CH) + i, 1), :, :].rearrange("o p (h c) -> (o p) h c", h=2)).then_inc(s[name], 16)

                def new_values(n, b, first):
                    if b == 0:
                        sp.wait_ge(s["vh_lo"], n + 1)
                    if not first:
                        sp.wait_ge(s["pv_mm"], n * J - J + 2 * b + 2)

                def copy_values(slot, b):
                    sp.dma_start(VN[:, b, :, :], VH[S * b:S * b + S, slot, :, :]).then_inc(vn_in[b], 16)

                for dst, src in consts:
                    sp.dma_start(dst[...], src).then_inc(s["const_in"], 16)
                load_w(0, WKV_RANGE, "wkv_in")
                load_w(0, WQ_RANGE, "wq_in")
                load_w(0, WO_RANGE, "wo_in")
                for b in range(BT):
                    new_values(0, b, True)
                    copy_values(0, b)
                new_values(1, 0, False)
                copy_values(1, 0)
                for b in range(1, BT):
                    new_values(1, b, False)
                    copy_values(1, b)

                def two(n):
                    for i in range(2):
                        for b in range(BT):
                            new_values(n + i, b, False)
                            copy_values(i, b)

                with sp.Fori(0, HP - 1) as hp:
                    with sp.Fori(1, NT // 2 - 1) as k:
                        two(hp * NT + 2 * k)
                    for b in range(BT):
                        new_values(hp * NT + (NT - 2), b, False)
                        copy_values(0, b)
                    sp.wait_ge(s["kv_mm"], hp * NT + NT)
                    load_w(hp + 1, WKV_RANGE, "wkv_in")
                    for b in range(BT):
                        if b == BT // 2:
                            sp.wait_ge(s["q_mm"], hp * (2 * NT) + 2 * NT)
                            load_w(hp + 1, WQ_RANGE, "wq_in")
                        new_values(hp * NT + (NT - 1), b, False)
                        copy_values(1, b)
                    for b in range(BT):
                        new_values(hp * NT + NT, b, False)
                        copy_values(0, b)
                    sp.wait_ge(s["wo_mm"], hp * NT + NT)
                    load_w(hp + 1, WO_RANGE, "wo_in")
                    for b in range(BT):
                        new_values(hp * NT + (NT + 1), b, False)
                        copy_values(1, b)
                with sp.Fori(1, NT // 2) as k:
                    two(2 * k + (HP - 1) * NT)
                for b in range(BT):
                    sp.wait_ge(vn_in[b], 16 * NR)

            @block.gpsimd
            def _(pool):
                def gather(n, b, first=False):
                    if not first:
                        pool.wait_ge(s["pv_mm"], n * J - J + 2 * b + 2)
                    pool.tensor_copy(ic[:, b, :], res["kvidx"][:, :, :].rearrange("p h i -> p (h i)")[:, ds(n * (BT * CC) + b * CC, CC)]).then_inc(s["ic_ok"], 1)
                    pool.wait_ge(s["ic_ok"], n * BT + b + 1)
                    pool.tensor_copy(lcol[:, b:b + 1], res["len"][:, ds(n % NT * BT + b, 1)]).then_inc(s["lc_ok"], 1)
                    for c in range(CC):
                        pool.indirect_dma_start(KV[:, b, c, :], None, dram["kv"],
                                                bass.IndirectOffsetOnAxis(ic[:, b, c:c + 1], 0)).then_inc(kv_in[b], 16)
                    pool.wait_ge(s["lc_ok"], n * BT + b + 1)
                    pool.tensor_tensor(mark[:, :], power[:, :], power[:, :], ALU.add).then_inc(s["marked"], 1)
                    pool.tensor_scalar(MK[:, b, :], iota[:, :], lcol[:, b:b + 1], -BIG, ALU.is_ge, ALU.mult).then_inc(s["mask_ok"], 1)

                def tables(n):
                    g = n % NT
                    for i, t in enumerate(("cos", "sin")):
                        for qk in range(2):
                            pool.tensor_tensor(tab[:, 2 * qk + i, :].rearrange("p (s f) -> p s f", s=2),
                                               res[t][:, ds(g, 1), :].to_broadcast([P, 2, HD // 2]),
                                               nw[:, 2 * qk + i, :].rearrange("p (s f) -> p s f", s=2), ALU.mult).then_inc(s["tab_ok"], 1)

                def rotate(n, i):
                    t = TK[:, :] if i == 0 else TQ[:, i - 1, :]
                    t2 = T2[:, 0:2 * HD] if i == 0 else T2[:, :]
                    h0, nh = (QH, 2) if i == 0 else (HR * (i - 1), HR)
                    pool.wait_ge(s["rope"], n * 3 + i + 1)
                    pool.wait_ge(s["sq"], n * (QH + 2) + (2, 2 + HR, 2 + 2 * HR)[i])
                    pool.tensor_tensor(t, t, t2, ALU.add).then_inc(s["turned"], 1)
                    pool.tensor_scalar(var[:, h0:h0 + nh], ssq[:, h0:h0 + nh], WS * WS / HD, EPS * WS * WS, ALU.mult, ALU.add).then_inc(s["var_ok"], 1)
                    pool.wait_ge(s["var_ok"], n * 3 + i + 1)
                    pool.tensor_tensor(rstd[:, h0:h0 + nh], var[:, h0:h0 + nh], power[:, :].to_broadcast([P, nh]), ALU.pow).then_inc(s["pow_ok"], 1)
                    pool.wait_ge(s["turned"], n * 3 + i + 1)
                    pool.wait_ge(s["pow_ok"], n * 3 + i + 1)
                    th = t.rearrange("p (h d) -> p h d", d=HD)
                    pool.tensor_tensor(th, th, rstd[:, h0:h0 + nh].unsqueeze(2).to_broadcast([P, nh, HD]), ALU.mult).then_inc(s["roped"], 1)

                pool.memset(power[:, :], -0.5).then_inc(s["marked"], 1)
                pool.wait_ge(s["const_in"], 16 * len(consts))
                for i in (1, 3):
                    pool.tensor_scalar(nw[:, i, 0:HD // 2], nw[:, i, 0:HD // 2], -1.0, None, ALU.mult).then_inc(s["nw_ok"], 1)
                pool.wait_ge(s["nw_ok"], 2)
                tables(0)
                pool.wait_ge(s["marked"], 1)
                gather(0, 0, True)
                gather(0, 1, True)
                for i in range(3):
                    rotate(0, i)
                tables(1)
                gather(0, 2, True)
                gather(0, 3, True)

                def body(n, ahead):
                    rotate(n + 1, 0)
                    gather(n + 1, 0)
                    rotate(n + 1, 1)
                    gather(n + 1, 1)
                    rotate(n + 1, 2)
                    if ahead:
                        tables(n + 2)
                    gather(n + 1, 2)
                    gather(n + 1, 3)
                with pool.Fori(0, NR - 2) as n:
                    body(n, True)
                body(NR - 2, False)

            def steps(eng, step, round_tail=None):
                for j in range(J):
                    step(0, j, True, False)
                with eng.Fori(1, NR - 1) as n:
                    for j in range(J):
                        step(n, j, False, False)
                for j in range(J):
                    step(NR - 1, j, False, True)

            @block.scalar
            def _(act):
                def kt_evac(m, j):
                    act.wait_ge(s["kt_mm"], m + 1)
                    if not (isinstance(m, int) and m < 2):
                        act.wait_ge(s["s_mm"], m - 1)
                    act.activation(KT[:, j % 2, :, :].rearrange("p h k -> p (h k)").bitcast(F32), KTB[:, :], ACT.Copy).then_inc(s["kt_ev"], 1)

                def exps(m, j):
                    act.wait_ge(s["neg"], m + 1)
                    act.activation(SS[:, j % 2, :], SS[:, j % 2, :], ACT.Exp, bias=st[:, j % 2, 1:2], scale=SC,
                                   accum_out=st[:, j % 2, 2:3]).then_inc(s["exp"], 1)

                def squares(n, i):
                    bank = (PB[0], PB[0], PB[1])[i]
                    h0, nh = (QH, 2) if i == 0 else (HR * (i - 1), HR)
                    act.wait_ge(s["kv_mm"] if i == 0 else s["q_mm"], n + 1 if i == 0 else n * 2 + i)
                    if not (isinstance(n, int) and n == 0):
                        act.wait_ge(s["var_ok"], n * 3 - 2 + i)
                    for h in range(nh):
                        done = n * (QH + 2) + (0, 2, 2 + HR)[i] + h
                        if not (isinstance(done, int) and done == 0):
                            act.wait_ge(s["sq"], done)
                        act.activation(junk[:, :], bank[:, h * HD:(h + 1) * HD], ACT.Square, scale=1.0 / WS,
                                       accum_out=ssq[:, h0 + h:h0 + h + 1]).then_inc(s["sq"], 1)

                def slot(n, j, nn):
                    if j == 0:
                        squares(nn, 0)
                        if not isinstance(nn, int):
                            for b in range(BT):
                                act.wait_ge(vn_in[b], nn * 16 - 16)
                        if isinstance(nn, int):
                            act.activation(VH[:, nn % 2, 0, :], PB[0][:, 2 * HD:], ACT.Copy, scale=1.0 / WS).then_inc(s["vh_hi"], 1)
                        else:
                            act.activation(VH[:, ds(nn % 2, 1), 0, :], PB[0][:, 2 * HD:].unsqueeze(1), ACT.Copy, scale=1.0 / WS).then_inc(s["vh_hi"], 1)
                    if j in (2, 3):
                        squares(nn, j - 1)
                    if j == 4:
                        act.wait_ge(s["kn_mm"], nn + 1)
                        act.activation(KN[:, 0, :, :], PB[0][:, 0:2 * HD].rearrange("p (h t) -> p h t", h=2), ACT.Copy).then_inc(s["kn_hi"], 1)
                    if j in (5, 6):
                        act.wait_ge(s["qt_mm"], nn * 2 + j - 4)
                        act.activation(QTV[0][:, j - 5], PB[6 - j][:, :].rearrange("p (h b t) -> p h b t", h=HR, t=S),
                                       ACT.Copy).then_inc(s["qt_hi"], 1)

                def pt_evac(m, j):
                    act.wait_ge(s["t_mm"], m + 1)
                    if not (isinstance(m, int) and m < 2):
                        act.wait_ge(s["pv_mm"], m - 1)
                    act.activation(PT[:, j % 2, 0, 0:CL], PTB[:, :], ACT.Copy).then_inc(s["pt_hi"], 1)
                    act.activation(PT[0:S, j % 2, 0, CL:CL + P], OB[j % 2][0:S, 0:P], ACT.Copy).then_inc(s["pt_hi"], 1)

                def o_evac(n, m, j, ready):
                    act.wait_ge(s["pv_mm"], m + 1)
                    if j == 0 and ready:
                        act.wait_ge(s["wo_mm"], n)
                    act.activation(OT[:, 0, HR * (j % 2):HR * (j % 2) + HR, S * (j // 2):S * (j // 2) + S],
                                   OB[j % 2][:, P:2 * P].rearrange("p (h t) -> p h t", h=HR), ACT.Copy, scale=1.0 / PSC).then_inc(s["o_hi"], 1)

                def step(n, j, first, last):
                    m = n * J + j
                    if not (last and j >= J - 2):
                        kt_evac(m + 2, j + 2)
                    if j == J - 1 and not last:
                        slot(n, j, n + 1)
                    if not (last and j == J - 1):
                        exps(m + 1, j + 1)
                    if j < J - 1 and not last:
                        slot(n, j, n + 1)
                    pt_evac(m, j)
                    if not (first and j == 0):
                        o_evac(n if j > 0 else n - 1, m - 1, (j - 1) % J, not first)

                for j in (0, 2, 3, 4, 5, 6):
                    slot(None, j, 0)
                kt_evac(0, 0)
                kt_evac(1, 1)
                exps(0, 0)
                steps(act, step)
                o_evac(NR - 1, NR * J - 1, J - 1, True)

            @block.vector
            def _(dve):
                def scores(m, j, first):
                    dve.wait_ge(s["mnew_ok"], first)
                    if j % 2 == 0:
                        dve.wait_ge(s["mask_ok"], first * BT + (j // 2 + 1 - BT))
                    if not (isinstance(m, int) and m < 2):
                        dve.wait_ge(s["t_mm"], m - 1)
                    dve.wait_ge(s["s_mm"], m + 1)
                    dve.tensor_copy(SS[:, j % 2, CL:CL + S], SN[:, j, :]).then_inc(s["sn_cp"], 1)
                    dve.tensor_tensor_reduce(SS[:, j % 2, 0:CL], SB[j % 2][:, :], MK[:, j // 2, :], 1.0, mnew[:, j:j + 1],
                                             ALU.add, ALU.max, st[:, j % 2, 0:1]).then_inc(s["ttr"], 1)
                    dve.wait_ge(s["ttr"], m + 1)
                    dve.tensor_scalar(st[:, j % 2, 1:2], st[:, j % 2, 0:1], -SC, None, ALU.mult).then_inc(s["neg"], 1)

                def norm(m, j):
                    dve.wait_ge(s["exp"], m + 1)
                    dve.reciprocal(st[:, j % 2, 3:4], st[:, j % 2, 2:3]).then_inc(s["rec"], 1)
                    dve.wait_ge(s["rec"], m + 1)
                    dve.tensor_scalar(SS[:, j % 2, :], SS[:, j % 2, :], st[:, j % 2, 3:4], PSC, ALU.mult, ALU.mult).then_inc(s["prob"], 1)

                def pt_evac(m, j):
                    dve.wait_ge(s["pt_hi"], m * 2 + 1)
                    dve.tensor_tensor(PT[:, j % 2, 1, 0:CL], PTB[:, :], PT[:, j % 2, 0, 0:CL], ALU.subtract).then_inc(s["pt_lo"], 1)
                    dve.wait_ge(s["pt_hi"], m * 2 + 2)
                    dve.tensor_tensor(PT[0:S, j % 2, 1, CL:CL + P], OB[j % 2][0:S, 0:P], PT[0:S, j % 2, 0, CL:CL + P], ALU.subtract).then_inc(s["pt_lo"], 1)

                def o_evac(m, j):
                    dve.wait_ge(s["o_hi"], m + 1)
                    o = [OT[:, h, HR * (j % 2):HR * (j % 2) + HR, S * (j // 2):S * (j // 2) + S] for h in range(2)]
                    dve.scalar_tensor_tensor(o[1], OB[j % 2][:, P:2 * P].rearrange("p (h t) -> p h t", h=HR), 1.0 / PSC, o[0],
                                             ALU.mult, ALU.subtract).then_inc(s["o_lo"], 1)

                def rope(nn, i):
                    bank = (PB[0], PB[0], PB[1])[i]
                    nh = 2 if i == 0 else HR
                    src = bank[:, 0:nh * HD].rearrange("p (h d) -> p h d", d=HD)
                    t1 = (TK[:, :] if i == 0 else TQ[:, i - 1, :]).rearrange("p (h d) -> p h d", d=HD)
                    t2 = T2[:, 0:nh * HD].rearrange("p (h d) -> p h d", d=HD)
                    ta = tab[:, 2 if i == 0 else 0, :]
                    tb = tab[:, 3 if i == 0 else 1, :]
                    H = HD // 2
                    first = isinstance(nn, int) and nn == 0
                    dve.wait_ge(s["sq"], nn * (QH + 2) + (2, 2 + HR, 2 + 2 * HR)[i])
                    dve.wait_ge(s["tab_ok"], nn * 4 + 4)
                    if not first:
                        dve.wait_ge(s["kn_mm"] if i == 0 else s["qt_mm"], nn if i == 0 else nn * 2 - 2 + i)
                    if not (first and i == 0):
                        dve.wait_ge(s["turned"], nn * 3 + i)
                    dve.tensor_tensor(t1, src, ta.unsqueeze(1).to_broadcast([P, nh, HD]), ALU.mult).then_inc(s["t2_free"], 1)
                    dve.tensor_tensor(t2[:, :, 0:H], src[:, :, H:], tb[:, 0:H].unsqueeze(1).to_broadcast([P, nh, H]), ALU.mult).then_inc(s["t2_free"], 1)
                    dve.tensor_tensor(t2[:, :, H:], src[:, :, 0:H], tb[:, H:].unsqueeze(1).to_broadcast([P, nh, H]), ALU.mult).then_inc(s["rope"], 1)

                def slot(n, j, nn):
                    if j == 0:
                        dve.wait_ge(s["vh_hi"], nn + 1)
                        if isinstance(nn, int):
                            dve.scalar_tensor_tensor(VH[:, nn % 2, 1, :], PB[0][:, 2 * HD:], 1.0 / WS, VH[:, nn % 2, 0, :],
                                                     ALU.mult, ALU.subtract).then_inc(s["vh_lo"], 1)
                        else:
                            dve.scalar_tensor_tensor(VH[:, ds(nn % 2, 1), 1, :], PB[0][:, 2 * HD:].unsqueeze(1), 1.0 / WS,
                                                     VH[:, ds(nn % 2, 1), 0, :], ALU.mult, ALU.subtract).then_inc(s["vh_lo"], 1)
                        rope(nn, 0)
                    if j in (2, 3):
                        rope(nn, j - 1)
                    if j == 4:
                        dve.wait_ge(s["kn_hi"], nn + 1)
                        dve.tensor_tensor(KN[:, 1, :, :], PB[0][:, 0:2 * HD].rearrange("p (h t) -> p h t", h=2), KN[:, 0, :, :],
                                          ALU.subtract).then_inc(s["kn_lo"], 1)
                    if j in (5, 6):
                        dve.wait_ge(s["qt_hi"], nn * 2 + j - 4)
                        dve.tensor_tensor(QTV[1][:, j - 5], PB[6 - j][:, :].rearrange("p (h b t) -> p h b t", h=HR, t=S), QTV[0][:, j - 5],
                                          ALU.subtract).then_inc(s["qt_lo"], 1)
                    if j == 7:
                        dve.wait_ge(s["sn_mm"], nn + 1)
                        if not (isinstance(nn, int) and nn == 0):
                            dve.wait_ge(s["sn_cp"], nn * J)
                        dve.tensor_copy(SN[:, :, :], PB[1][:, 0:J * S].rearrange("p (j t) -> p j t", j=J)).then_inc(s["sn_ev"], 1)
                        dve.wait_ge(s["sn_ev"], nn + 1)
                        dve.tensor_reduce(mnew[:, :], SN[:, :, :], AX.X, ALU.max).then_inc(s["mnew_ok"], 1)

                def y_add(n):
                    dve.wait_ge(s["wo_mm"], n + 1)
                    y = Y[:, ds(n % NT, 1), :].rearrange("p o d -> p (o d)")
                    dve.scalar_tensor_tensor(y, PB[1][:, :], 1.0 / WS, y, ALU.mult, ALU.add).then_inc(s["y_add"], 1)

                def step(n, j, first, last):
                    m = n * J + j
                    if j == J - 1 and not last:
                        slot(n, j, n + 1)
                    if not (last and j == J - 1):
                        scores(m + 1, (j + 1) % J, n + 1 if j < J - 1 else n + 2)
                    if j == 1 and not first:
                        y_add(n - 1)
                    if j < J - 1 and not last:
                        slot(n, j, n + 1)
                    if not (last and j == J - 1):
                        norm(m + 1, j + 1)
                    pt_evac(m, j)
                    if not (first and j == 0):
                        o_evac(m - 1, (j - 1) % J)

                dve.memset(Y[:, :, :], 0.0).then_inc(s["y_zero"], 1)
                dve.wait_ge(s["y_zero"], 1)
                for j in (0, 2, 3, 4, 5, 6, 7):
                    slot(None, j, 0)
                scores(0, 0, 1)
                norm(0, 0)
                steps(dve, step)
                o_evac(NR * J - 1, J - 1)
                y_add(NR - 1)

            @block.tensor
            def _(pe):
                def turn_keys(m, n, j):
                    b, v = j // 2, j % 2
                    if v == 0:
                        pe.wait_ge(kv_in[b], n * (16 * CC) + 16 * CC)
                    if not (isinstance(m, int) and m == 0):
                        pe.wait_ge(s["kt_ev"], m)
                    for h in range(2):
                        for c in range(CC):
                            k0 = h * 512 + v * 256
                            last = pe.transpose(halves[2][:, (h * CC + c) * P:(h * CC + c + 1) * P], KV[:, b, c, k0:k0 + HD], res["ident"][:, :])
                    last.then_inc(s["kt_mm"], 1)

                def score(m, n, j):
                    b, v = j // 2, j % 2
                    pe.wait_ge(s["kt_ev"], m + 1)
                    if v == 0 or j == 1:
                        pe.wait_ge(s["qt_lo"], n * 2 + 1 + v)
                    if not (isinstance(m, int) and m < 2):
                        pe.wait_ge(s["ttr"], m - 1)
                    mm3(pe, SB[j % 2][:, :], lambda h: QT[:, h, j, :],
                        lambda h: KT[:, j % 2, h, :], True, True).then_inc(s["s_mm"], 1)

                def turn_probs(m, j):
                    pe.wait_ge(s["prob"], m + 1)
                    if not (isinstance(m, int) and m == 0):
                        pe.wait_ge(s["pt_lo"], m * 2)
                    if not (isinstance(m, int) and m < 2):
                        pe.wait_ge(s["o_lo"], m - 1)
                    for c in range(CC):
                        pe.transpose(PTB[:, c * P:(c + 1) * P], SS[:, j % 2, c * P:(c + 1) * P], res["identf"][:, :])
                    pe.transpose(OB[j % 2][0:S, 0:P], SS[:, j % 2, CL:CL + S], res["identf"][:, :]).then_inc(s["t_mm"], 1)

                def weigh(m, n, j):
                    b, v = j // 2, j % 2
                    pe.wait_ge(s["pt_lo"], m * 2 + 2)
                    if v == 0:
                        pe.wait_ge(vn_in[b], n * 16 + 16)
                    o = OB[j % 2][:, P:2 * P]
                    for c in range(CC):
                        mm3(pe, o, lambda h: KV[:, b, c, h * 512 + v * 256 + HD:h * 512 + v * 256 + 2 * HD],
                            lambda h: PT[:, j % 2, h, c * P:(c + 1) * P], c == 0, False)
                    mm3(pe, o, lambda h: VN[:, b, h, v * HD:(v + 1) * HD],
                        lambda h: PT[0:S, j % 2, h, CL:CL + P], False, True).then_inc(s["pv_mm"], 1)

                def project(nn, bank, w, cols, g):
                    for c in range(KC):
                        last = mm3(pe, bank[:, 0:WQ], lambda h: res["x3T"][:, h, c, ds(g * P, P)],
                                   lambda h: w[:, h, c, cols:cols + WQ], c == 0, c == KC - 1)
                    return last

                def write_out(n):
                    pe.wait_ge(s["o_lo"], n * J + J)
                    pe.wait_ge(s["wo_in"], n // NT * (16 * len(WO_RANGE)) + 16 * len(WO_RANGE))
                    pe.wait_ge(s["sn_ev"], NR if isinstance(n, int) and n == NR - 1 else n + 2)
                    if isinstance(n, int) and n == NR - 1:
                        pe.wait_ge(s["y_add"], n)
                    for q in range(QH):
                        last = mm3(pe, PB[1][:, :], lambda h: OT[:, h, q, :], lambda h: wo[:, h, q, :], q == 0, q == QH - 1)
                    last.then_inc(s["wo_mm"], 1)

                def slot(n, j, nn):
                    first = isinstance(nn, int) and nn == 0
                    g = nn % NT
                    if j == 0:
                        pe.wait_ge(s["wkv_in"], nn // NT * (16 * len(WKV_RANGE)) + 16 * len(WKV_RANGE))
                        if not first:
                            pe.wait_ge(s["qt_lo"], nn * 2)
                        project(nn, PB[0], wkv, 0, g).then_inc(s["kv_mm"], 1)
                    if j == 2:
                        pe.wait_ge(s["wq_in"], nn // NT * (16 * len(WQ_RANGE)) + 16 * len(WQ_RANGE))
                        pe.wait_ge(s["rope"], nn * 3 + 1)
                        pe.wait_ge(s["vh_lo"], nn + 1)
                        project(nn, PB[0], wq, 0, g).then_inc(s["q_mm"], 1)
                    if j == 3:
                        if not first and not (isinstance(n, int) and n == 0):
                            pe.wait_ge(s["y_add"], n)
                        if isinstance(n, int) and n == 0:
                            pe.wait_ge(s["sn_ev"], 1)
                        project(nn, PB[1], wq, WQ, g).then_inc(s["q_mm"], 1)
                    if j == 4:
                        pe.wait_ge(s["roped"], nn * 3 + 1)
                        pe.wait_ge(s["rope"], nn * 3 + 2)
                        for h in range(2):
                            last = pe.transpose(PB[0][:, h * P:(h + 1) * P], TK[:, h * HD:(h + 1) * HD], res["identf"][:, :])
                        last.then_inc(s["kn_mm"], 1)
                    if j in (5, 6):
                        pe.wait_ge(s["roped"], nn * 3 + j - 3)
                        if j == 5:
                            pe.wait_ge(s["rope"], nn * 3 + 3)
                        else:
                            pe.wait_ge(s["kn_lo"], nn + 1)
                        for h in range(HR):
                            last = pe.transpose(PB[6 - j][:, h * P:(h + 1) * P], TQ[:, j - 5, h * HD:(h + 1) * HD], res["identf"][:, :])
                        last.then_inc(s["qt_mm"], 1)
                    if j == 7:
                        pe.wait_ge(s["qt_lo"], nn * 2 + 2)
                        for i in range(J):
                            b, v = i // 2, i % 2
                            last = mm3(pe, PB[1][:, i * S:(i + 1) * S], lambda h: QT[:, h, i, :],
                                       lambda h: KN[:, h, v, S * b:S * b + S], True, True)
                        last.then_inc(s["sn_mm"], 1)

                def step(n, j, first, last):
                    m = n * J + j
                    if j == J - 1 and not last:
                        slot(n, j, n + 1)
                    if not (last and j >= J - 2):
                        turn_keys(m + 2, n if j < J - 2 else n + 1, (j + 2) % J)
                    if not (last and j == J - 1):
                        score(m + 1, n if j < J - 1 else n + 1, (j + 1) % J)
                    if j == 1 and not first:
                        write_out(n - 1)
                    if j < J - 1 and not last:
                        slot(n, j, n + 1)
                    turn_probs(m, j)
                    if not (first and j == 0):
                        weigh(m - 1, n if j > 0 else n - 1, (j - 1) % J)

                for j in (0, 2, 3, 4, 5, 6, 7):
                    slot(None, j, 0)
                turn_keys(0, 0, 0)
                turn_keys(1, 0, 1)
                score(0, 0, 0)
                steps(pe, step)
                weigh(NR * J - 1, NR - 1, J - 1)
                write_out(NR - 1)


def last_ffn(nc, a, dram, res, banks, halves, Y, out):
    ER = E * R
    with ExitStack() as ctx:
        def sb(name, shape, dt):
            return ctx.enter_context(nc.sbuf_tensor(name, shape, dt))

        WT = sb("WT", [P, KC, D], F32)
        AB = sb("AB", [P, 2, D], F32)
        ABH = sb("ABH", [P, 2, 2, D], F16)
        lw = sb("lw", [P, 1], F32)
        lw2 = sb("lw2", [P, 1], F32)
        bias = sb("bias", [P, D], F32)
        MF = sb("MF", [P, KC, D], F32)
        MT = sb("MT", [P, 2, KC, D], F16)
        YH = sb("YH", [P, 2, 2, D], F16)
        YT = sb("YT3", [P, 2, 2, KC, P], F16)
        X3 = sb("X3", [P, 2, D], F32)
        XB = sb("XB", [P, 2, D], F32)
        RS = sb("RS", [P, 2, D], F32)

        names = ("f_in w2x b_ok ab_hi ab_lo m_mm mf mt_hi mt_lo y_hi y_lo yt_mm yt_ev o_mm xb res "
                 "x3_in0 x3_in1 out0 out1").split()
        s = {n: ctx.enter_context(nc.semaphore("f_" + n)) for n in names}
        x3_in, stored = [s["x3_in0"], s["x3_in1"]], [s["out0"], s["out1"]]
        ins = [(lw, a["lw_rep"]), (AB[:, 0, :], a["Af"]), (AB[:, 1, :], a["Bf"]),
               (WT[:, :, :].rearrange("p c n -> p (c n)"), a["Wf"]), (bias, a["bf_rep"])]

        with nc.Block() as block:
            def rows(t, n):
                return t[ds(n * P, P), :]

            @block.sync
            def _(sp):
                for dst, src in ins:
                    sp.dma_start(dst[...], src).then_inc(s["f_in"], 16)
                for i in range(2):
                    sp.dma_start(X3[:, i, :], rows(dram["x3"], i)).then_inc(x3_in[i], 16)

                def store(n, k, i, ahead):
                    sp.wait_ge(s["res"], n + 1)
                    sp.dma_start(rows(out, n), RS[:, i, :]).then_inc(stored[i], 16)
                    if ahead:
                        sp.wait_ge(s["xb"], n + 1)
                        sp.dma_start(X3[:, i, :], rows(dram["x3"], n + 2)).then_inc(x3_in[i], 16)
                with sp.Fori(0, NT // 2 - 1) as k:
                    for i in range(2):
                        store(k * 2 + i, k, i, True)
                for i in range(2):
                    store(NT - 2 + i, NT // 2 - 1, i, False)
                for i in range(2):
                    sp.wait_ge(stored[i], 16 * (NT // 2))

            @block.gpsimd
            def _(pool):
                def tile(n, k, i, first):
                    pool.wait_ge(x3_in[i], k * 16 + 16)
                    if not first:
                        pool.wait_ge(s["res"], n - 1)
                    pool.tensor_tensor(XB[:, i, :], X3[:, i, :], bias[:, :], ALU.add).then_inc(s["xb"], 1)
                pool.wait_ge(s["f_in"], 16 * len(ins))
                for i in range(2):
                    tile(i, 0, i, True)
                with pool.Fori(1, NT // 2) as k:
                    for i in range(2):
                        tile(k * 2 + i, k, i, False)

            @block.scalar
            def _(act):
                act.wait_ge(s["f_in"], 16 * len(ins))
                act.activation(ABH[:, 0, 0, :], AB[:, 0, :], ACT.Copy).then_inc(s["ab_hi"], 1)
                act.wait_ge(s["b_ok"], 1)
                act.activation(ABH[:, 1, 0, :], AB[:, 1, :], ACT.Copy).then_inc(s["ab_hi"], 1)
                for c in range(KC):
                    act.wait_ge(s["mf"], c + 1)
                    act.activation(MT[:, 0, c, :], MF[:, c, :], ACT.Copy).then_inc(s["mt_hi"], 1)

                def tile(n, i, first):
                    if not first:
                        act.wait_ge(s["yt_mm"], n - 1)
                    act.activation(YH[:, i, 0, :], Y[:, ds(n, 1), :].rearrange("p o d -> p (o d)"), ACT.Copy).then_inc(s["y_hi"], 1)
                    act.wait_ge(s["yt_mm"], n + 1)
                    if not first:
                        act.wait_ge(s["o_mm"], n - 1)
                    act.activation(YT[:, i, :, :, :].rearrange("p h c t -> p (h c t)").bitcast(F32),
                                   banks[i][:, :], ACT.Copy).then_inc(s["yt_ev"], 1)
                for i in range(2):
                    tile(i, i, True)
                with act.Fori(1, NT // 2) as k:
                    for i in range(2):
                        tile(k * 2 + i, i, False)

            @block.vector
            def _(dve):
                dve.wait_ge(s["f_in"], 16 * len(ins))
                dve.tensor_scalar(lw2[:, :], lw[:, :], 2.0, None, ALU.mult).then_inc(s["w2x"], 1)
                dve.wait_ge(s["w2x"], 1)
                dve.tensor_scalar(AB[:, 1, :], AB[:, 1, :], lw2[:, 0:1], None, ALU.mult).then_inc(s["b_ok"], 1)
                for i in range(2):
                    dve.wait_ge(s["ab_hi"], i + 1)
                    dve.wait_ge(s["b_ok"], 1)
                    dve.tensor_tensor(ABH[:, i, 1, :], AB[:, i, :], ABH[:, i, 0, :], ALU.subtract).then_inc(s["ab_lo"], 1)
                for c in range(KC):
                    dve.wait_ge(s["m_mm"], c + 1)
                    dve.tensor_tensor(MF[:, c, :], banks[4 + c][:, :], WT[:, c, :], ALU.add).then_inc(s["mf"], 1)
                for c in range(KC):
                    dve.wait_ge(s["mt_hi"], c + 1)
                    dve.tensor_tensor(MT[:, 1, c, :], MF[:, c, :], MT[:, 0, c, :], ALU.subtract).then_inc(s["mt_lo"], 1)

                def y_lo(n, i):
                    dve.wait_ge(s["y_hi"], n + 1)
                    dve.tensor_tensor(YH[:, i, 1, :], Y[:, ds(n, 1), :].rearrange("p o d -> p (o d)"), YH[:, i, 0, :],
                                      ALU.subtract).then_inc(s["y_lo"], 1)

                def result(n, k, i, first):
                    dve.wait_ge(s["o_mm"], n + 1)
                    dve.wait_ge(s["xb"], n + 1)
                    if not first:
                        dve.wait_ge(stored[i], k * 16)
                    dve.tensor_tensor(RS[:, i, :], banks[2 + i][:, :], XB[:, i, :], ALU.add).then_inc(s["res"], 1)
                y_lo(0, 0)
                y_lo(1, 1)
                result(0, 0, 0, True)
                y_lo(2, 0)
                result(1, 0, 1, True)
                with dve.Fori(1, NT // 2 - 1) as k:
                    for i in range(2):
                        y_lo(k * 2 + i + 1, 1 - i)
                        result(k * 2 + i, k, i, False)
                y_lo(NT - 1, 1)
                for i in range(2):
                    result(NT - 2 + i, NT // 2 - 1, i, False)

            @block.tensor
            def _(pe):
                pe.wait_ge(s["ab_lo"], 2)
                for c in range(KC):
                    mm3(pe, banks[4 + c][:, :], lambda h: ABH[:, 0, h, c * P:(c + 1) * P], lambda h: ABH[:, 1, h, :],
                        True, True).then_inc(s["m_mm"], 1)

                def turn(n, i, first):
                    pe.wait_ge(s["y_lo"], n + 1)
                    if not first:
                        pe.wait_ge(s["yt_ev"], n - 1)
                    for h in range(2):
                        for c in range(KC):
                            last = pe.transpose(halves[i][:, (h * KC + c) * P:(h * KC + c + 1) * P],
                                                YH[:, i, h, c * P:(c + 1) * P], res["ident"][:, :])
                    last.then_inc(s["yt_mm"], 1)

                def product(n, i, first):
                    pe.wait_ge(s["yt_ev"], n + 1)
                    if not first:
                        pe.wait_ge(s["res"], n - 1)
                    for c in range(KC):
                        last = mm3(pe, banks[2 + i][:, :], lambda h: YT[:, i, h, c, :], lambda h: MT[:, h, c, :],
                                   c == 0, c == KC - 1)
                    last.then_inc(s["o_mm"], 1)
                turn(0, 0, True)
                pe.wait_ge(s["mt_lo"], KC)
                turn(1, 1, True)
                product(0, 0, True)
                turn(2, 0, False)
                product(1, 1, True)
                with pe.Fori(1, NT // 2 - 1) as k:
                    for i in range(2):
                        turn(k * 2 + i + 1, 1 - i, False)
                        product(k * 2 + i, i, False)
                turn(NT - 1, 1, False)
                for i in range(2):
                    product(NT - 2 + i, i, False)


def layout(v):
    f = np.float32
    p = np.arange(P)

    def chunks_t(m):
        return np.ascontiguousarray(m.T.reshape(KC, P, -1).transpose(1, 0, 2)).reshape(P, -1)

    A = {n: np.asarray(x) for n, x in v.items()}
    o = {}
    o["x"] = A["x"].reshape(NB * S, D)
    o["c_ident"] = np.eye(P, dtype=f)
    o["c_iota"] = np.broadcast_to(np.arange(D, dtype=f), (P, D)).copy()
    o["c_pmod"] = np.stack([p % S, p % R], 1).astype(f)
    freq = np.power(np.float32(10000.0), np.arange(0, HD, 2, dtype=f) / f(HD))
    o["c_freq"] = np.broadcast_to((f(1.0) / freq).astype(f), (P, HD // 2)).copy()
    o["c_hmask"] = ((np.arange(U * R) // R)[:, None] == (p // S)[None, :]).astype(f) / f(WS)
    seq = BT * np.arange(NT)[None, :] + (p // S)[:, None]
    o["cond_rep"] = A["itok_B_0_15"][seq]
    o["adapter_rep"] = A["itok_B_6_15"][BT * np.arange(NT)[None, :] + (np.arange(U * R) // R)[:, None]]
    o["adapter_ids"] = A["itok_B_6_15"].reshape(1, NB)
    o["perm_cols"] = np.ascontiguousarray(A["L1_ffn_perm"].reshape(KC, P).T)
    bt = A["itok_Bx16_0_63"]
    o["page_rep"] = np.ascontiguousarray(bt.reshape(NB, CC, NPP // CC)[:, :, p // PS].transpose(2, 0, 1)).reshape(P, NB * CC)
    o["len_rep"] = np.broadcast_to(A["itok_B_207_1644"], (P, NB)).copy()
    o["pos_rep"] = A["itok_B_207_1644"][seq]
    o["cond0"] = A["L0_cond_weights"].reshape(NC * S, S)
    o["cond2"] = A["L2_cond_weights"].reshape(NC * S, S)
    o["A0"] = chunks_t(np.concatenate([A["L0_ffn_A"].reshape(E * R, D), A["L0_ffn_Wr"]], 0))
    o["B0"] = np.ascontiguousarray(A["L0_ffn_B"].transpose(0, 2, 1)).reshape(E * R, D)
    o["br_rep"] = np.broadcast_to(A["L0_ffn_br"], (P, E)).copy()
    o["ATA"] = chunks_t(A["L1_cond_lora_A_w"].reshape(NA * R, D))
    o["w1_rows"] = np.concatenate([A["L1_cond_base_weight"],
                                   A["L1_cond_lora_B_w"].transpose(1, 0, 2).reshape(D, NA * R),
                                   A["L1_cond_base_bias"].reshape(D, 1)], 1)
    up = np.zeros((P, FH, FM), f)
    dn = np.zeros((P, FH, P), f)
    for h in range(FH):
        q = slice(32 * (h % BT), 32 * (h % BT) + 32)
        up[q, h, :] = A["L1_ffn_up"][h]
        dn[:, h, q] = A["L1_ffn_down"][h]
    o["UP"], o["DN"] = up.reshape(P, -1), dn.reshape(P, -1)
    o["QK2"] = chunks_t(np.concatenate([A["L2_ffn_Wq"], A["L2_ffn_Wk"]], 0))
    o["W2"] = chunks_t(A["L2_ffn_W"])
    o["A2"] = chunks_t(A["L2_ffn_A"].reshape(E * R, D))
    o["B2"] = np.ascontiguousarray(A["L2_ffn_Bm"].transpose(0, 2, 1)).reshape(E * R, D)
    o["b2_rep"] = np.broadcast_to(A["L2_ffn_b"], (P, D)).copy()
    o["Af"] = A["L3_ffn_lora_A"].reshape(E * R, D)
    o["Bf"] = np.ascontiguousarray(A["L3_ffn_lora_B"].transpose(0, 2, 1)).reshape(E * R, D)
    o["Wf"] = chunks_t(A["L3_ffn_W"])
    o["lw_rep"] = np.repeat(A["L3_ffn_lora_weights"], R).reshape(P, 1)
    o["bf_rep"] = np.broadcast_to(A["L3_ffn_bias"], (P, D)).copy()
    w3 = []
    for hp in range(HP):
        q = A["L3_cond_Wq"][hp * QH * HD:(hp + 1) * QH * HD]
        kv = np.concatenate([A[n][hp * 2 * HD:(hp + 1) * 2 * HD] for n in ("L3_cond_Wk", "L3_cond_Wv")], 0)
        wo = A["L3_cond_Wo"][:, hp * QH * HD:(hp + 1) * QH * HD].reshape(D, QH, HD).transpose(2, 1, 0).reshape(HD, QH * D)
        w3.append(np.concatenate([chunks_t(q), chunks_t(kv), wo], 1))
    kv = np.stack([A["L3_cond_k_cache"], A["L3_cond_v_cache"]], 3)
    kv = kv.reshape(NT, P, HP * 512 // CH, CH).transpose(0, 2, 1, 3).reshape(KV_PIECES, P, CH)
    w3 = np.stack(w3).reshape(HP, P, W3_COLS // CH, CH).transpose(0, 2, 1, 3).reshape(W_PIECES, P, CH)
    wq, wk = A["L3_cond_q_norm_w"], A["L3_cond_k_norm_w"]
    h = HD // 2
    o["norm_w"] = np.broadcast_to(np.stack([wq, np.concatenate([wq[h:], wq[:h]]), wk, np.concatenate([wk[h:], wk[:h]])]), (P, 4, HD)).copy()
    wg, kg = W_PIECES // NG, KV_PIECES // NG
    parts = [x for g in range(NG) for x in (kv[g * kg:(g + 1) * kg], w3[g * wg:(g + 1) * wg])]
    o["bulk"] = np.concatenate(parts + [np.zeros((2, P, CH), f)])
    return {n: np.ascontiguousarray(x) for n, x in o.items()}


def kernel(**inputs):
    import concourse.bacc as bacc
    from concourse.bass_utils import run_bass_kernel_spmd

    nc = bacc.Bacc("TRN2", target_bir_lowering=False, num_devices=1)
    arrays = layout(inputs)
    a = {n: nc.dram_tensor(f"in_{n}", x.shape, mybir.dt.from_np(x.dtype), kind="ExternalInput").ap() for n, x in arrays.items()}
    out = nc.dram_tensor("out", [NB * S, D], F32, kind="ExternalOutput").ap()
    build(nc, a, out)
    r = run_bass_kernel_spmd(nc, [{f"in_{n}": x for n, x in arrays.items()}], core_ids=[0])
    return r.results[0]["out"].reshape(NB, S, D)
```

```python
from contextlib import ExitStack

import numpy as np

import concourse.bass as bass
from concourse import mybir

F32 = mybir.dt.float32
F16 = mybir.dt.float16
I32 = mybir.dt.int32
ALU = mybir.AluOpType
ACT = mybir.ActivationFunctionType
AX = mybir.AxisListType
ds = bass.ds

NB, S, D = 64, 32, 512
P = 128
KC = D // P
NT = NB * S // P
BT = P // S
U = 4
NG = NT // U
GT = U * P
NC = 16
E, R = 8, 16
NA = 32
FH, FM = 16, 128
DK = 32
HQ, HK, HD = 32, 8, 128
PAGES, PS, NPP = 64, 32, 16
HP = HK // 2
QH = HQ // HP
CL = NPP * PS
CC = CL // P
WS = 64.0
PSC = 1024.0
EPS = 1e-6
BIG = 1e30
WQ_COLS, WKV_COLS, WO_COLS = KC * QH * HD, KC * 4 * HD, QH * D
W3_COLS = WQ_COLS + WKV_COLS + WO_COLS
CH = 1024
W_PIECES = HP * W3_COLS // CH
KV_PIECES = PAGES * PS * HP * 512 // (P * CH)
TWO_PI = 2.0 * np.pi
MAGIC = 1.5 * 2.0 ** 23


def cody_waite():
    c1 = np.float32(np.floor(TWO_PI * 2 ** 8) / 2 ** 8)
    c2 = np.float32(np.floor((TWO_PI - float(c1)) * 2 ** 20) / 2 ** 20)
    c3 = np.float32(TWO_PI - float(c1) - float(c2))
    return float(c1), float(c2), float(c3)


def build(nc, a, out, debug=None):
    with ExitStack() as top:
        banks = [top.enter_context(nc.psum_tensor(f"bank{i}", [P, 512], F32)) for i in range(8)]
        halves = [b[:, :].bitcast(F16) for b in banks]
        dram = {
            "kv": nc.dram_tensor("kv_split", [HP * PAGES * PS, 1024], F16, kind="Internal").ap(),
            "w3": nc.dram_tensor("w3_split", [W_PIECES, P, 2 * CH], F16, kind="Internal").ap(),
            "bt": nc.dram_tensor("lora_b_split", [NA * R, 2 * D], F16, kind="Internal").ap(),
            "x3": nc.dram_tensor("x3_rows", [NB * S, D], F32, kind="Internal").ap(),
        }

        def keep(name, shape, dt):
            return top.enter_context(nc.sbuf_tensor(name, shape, dt))

        res = {
            "ident": keep("ident", [P, P], F16),
            "identf": keep("identf", [P, P], F32),
            "cos": keep("cos", [P, NT, HD // 2], F32),
            "sin": keep("sin", [P, NT, HD // 2], F32),
            "len": keep("seqlen", [P, NB], F32),
            "kvidx": keep("kvidx", [P, HP, NB * CC], I32),
            "x3T": keep("x3T", [P, 2, KC, NB * S], F16),
        }
        early(nc, a, dram, res, banks, halves)
        if debug:
            debug(nc, res, dram)
            return
        late(nc, a, dram, res, banks, halves, out)


def mm3(pe, psum, left, right, first, last):
    pe.matmul(psum, left(0), right(0), start=first, stop=False, skip_group_check=True)
    pe.matmul(psum, left(0), right(1), start=False, stop=False, skip_group_check=True)
    return pe.matmul(psum, left(1), right(0), start=False, stop=last, skip_group_check=True)


def early(nc, a, dram, res, banks, halves):
    with ExitStack() as ctx:
        def sb(name, shape, dt):
            return ctx.enter_context(nc.sbuf_tensor(name, shape, dt))

        w = {
            "BD0": sb("BD0", [P, 2, NT, P], F16), "BD2": sb("BD2", [P, 2, NT, P], F16),
            "A0": sb("A0", [P, 2, KC, P + E], F16), "B0": sb("B0", [P, 2, D], F16),
            "ATA": sb("ATA", [P, 2, KC, NA * R], F16), "W1": sb("W1", [P, 2, KC, D], F16),
            "bias1": sb("bias1", [P, KC], F32), "OH": sb("OH", [P, KC, D], F16),
            "UP": sb("UP", [P, 2, FH, FM], F16), "DN": sb("DN", [P, 2, FH, P], F16),
            "QK2": sb("QK2", [P, 2, KC, 2 * E * DK], F16), "W2": sb("W2", [P, 2, KC, D], F16),
            "A2": sb("A2", [P, 2, KC, P], F16), "B2": sb("B2", [P, 2, D], F16),
            "b2": sb("b2", [P, D], F32), "br": sb("br", [P, E], F32),
            "idx1": sb("idx1", [U * R, NT], I32), "ids": sb("ids", [1, NB], I32),
            "hmask": sb("hmask", [U * R, P], F32),
        }
        early_weights(nc, a, dram, res, w, banks, halves)
        early_layers(nc, a, dram, res, w, banks, halves)


def early_weights(nc, a, dram, res, w, banks, halves):
    RAW = 2048
    plan = [("A0", "A0", KC * (P + E), WS), ("B0", "B0", D, WS), ("ATA", "ATA", KC * NA * R, WS),
            ("UP", "UP", FH * FM, 1.0), ("DN", "DN", FH * P, 1.0), ("QK2", "QK2", KC * 512, WS),
            ("W2", "W2", KC * D, WS), ("A2", "A2", KC * P, WS), ("B2", "B2", D, WS)]
    W1C = D + NA * R + 1
    with ExitStack() as ctx:
        def sb(name, shape, dt):
            return ctx.enter_context(nc.sbuf_tensor(name, shape, dt))

        def sem(name):
            return ctx.enter_context(nc.semaphore(name))

        raw = sb("raw", [P, 2, RAW], F32)
        iota = sb("iota", [P, D], F32)
        pmod = sb("pmod", [P, 2], F32)
        condi = sb("condi", [P, NT], I32)
        condf = sb("condf", [P, NT], F32)
        crow = sb("crow", [P, NT], I32)
        G = sb("G", [P, 2, NT, S], F32)
        permi = sb("permi", [P, KC], I32)
        permf = sb("permf", [P, KC], F32)
        W1R = sb("W1R", [P, KC, W1C], F32)
        W1H = sb("W1H", [P, 2, KC, 2 * D], F16)
        BT1 = sb("BT1", [P, KC, 2, D], F16)
        id1 = sb("id1", [U * R, NT], I32)
        id1f = sb("id1f", [U * R, NT], F32)
        pgi = sb("pgi", [P, NB * CC], I32)
        pgf = sb("pgf", [P, NB * CC], F32)
        pgh = sb("pgh", [P, HP, NB * CC], F32)
        leni = sb("leni", [P, NB], I32)
        posi = sb("posi", [P, NT], I32)
        posf = sb("posf", [P, NT], F32)
        posf2 = sb("posf2", [P, NT], F32)
        freq = sb("freq", [P, HD // 2], F32)
        halfpi = sb("halfpi", [P, 1], F32)
        ang, turns, rest, rest2 = (raw[:, i // 2, (i % 2) * 1024:(i % 2) * 1024 + 1024].rearrange(
            "p (t f) -> p t f", t=NT) for i in range(4))

        small_in = sem("small_in")
        raw_in = [sem(f"raw_in{i}") for i in range(2)]
        hi_done, lo_done = sem("hi_done"), sem("lo_done")
        ints, rows_ready, gath0, gath1 = sem("ints"), sem("rows_ready"), sem("gath0"), sem("gath1")
        zeroed, bd_hi, bd_lo = sem("zeroed"), sem("bd_hi"), sem("bd_lo")
        w1_hi, w1_lo, w1_t, w1_out = sem("w1_hi"), sem("w1_lo"), sem("w1_t"), sem("w1_out")
        bt_out, angle, trig = sem("bt_out"), sem("angle"), sem("trig")

        small = [(res["identf"], a["c_ident"]), (iota, a["c_iota"]), (pmod, a["c_pmod"]),
                 (condi, a["cond_rep"]), (permi, a["perm_cols"]), (id1, a["adapter_rep"]),
                 (pgi, a["page_rep"]), (leni, a["len_rep"]), (posi, a["pos_rep"]),
                 (freq, a["c_freq"]), (w["ids"], a["adapter_ids"]), (w["hmask"], a["c_hmask"]),
                 (w["b2"], a["b2_rep"]), (w["br"], a["br_rep"])]

        def flat(t):
            if len(t.shape) == 3:
                return t[:, :, :]
            return t[:, :, :, :].rearrange("p h a b -> p h (a b)")

        with nc.Block() as block:
            @block.sync
            def _(sp):
                for dst, src in small:
                    sp.dma_start(dst[...], src).then_inc(small_in, 16)
                for n, (src, _, cols, _) in enumerate(plan):
                    if n >= 2:
                        sp.wait_ge(lo_done, n - 1)
                    sp.dma_start(raw[:, n % 2, 0:cols], a[src]).then_inc(raw_in[n % 2], 16)
                for c in range(KC):
                    sp.wait_ge(w1_out, KC + c + 1)
                    sp.dma_start(dram["bt"][c * P:(c + 1) * P, :],
                                 BT1[:, c, :, :].rearrange("p h n -> p (h n)")).then_inc(bt_out, 16)
                sp.wait_ge(bt_out, 16 * KC)

            @block.gpsimd
            def _(pool):
                pool.memset(w["BD0"][:, :, :, :], 0.0).then_inc(zeroed, 1)
                pool.memset(w["BD2"][:, :, :, :], 0.0).then_inc(zeroed, 1)
                pool.wait_ge(rows_ready, 1)
                for t in range(NT):
                    for layer, src in enumerate(("cond0", "cond2")):
                        pool.indirect_dma_start(G[:, layer, t, :], None, a[src],
                                                bass.IndirectOffsetOnAxis(crow[:, t:t + 1], 0)).then_inc(gath0, 16)
                pool.wait_ge(small_in, 16 * len(small))
                for c in range(KC):
                    pool.indirect_dma_start(W1R[:, c, :], None, a["w1_rows"],
                                            bass.IndirectOffsetOnAxis(permi[:, c:c + 1], 0)).then_inc(gath1, 16)

            @block.scalar
            def _(act):
                act.wait_ge(small_in, 16 * len(small))
                act.activation(res["ident"][:, :], res["identf"][:, :], ACT.Copy).then_inc(trig, 1)
                for n, (_, dst, cols, scale) in enumerate(plan):
                    act.wait_ge(raw_in[n % 2], 16 * (n // 2 + 1))
                    act.activation(flat(w[dst])[:, 0, :], raw[:, n % 2, 0:cols], ACT.Copy,
                                   scale=scale).then_inc(hi_done, 1)
                act.wait_ge(gath0, 16 * 2 * NT)
                act.wait_ge(zeroed, 2)
                for layer, name in enumerate(("BD0", "BD2")):
                    for b in range(BT):
                        q = slice(S * b, S * b + S)
                        act.activation(w[name][q, 0, :, q], G[q, layer, :, :], ACT.Copy).then_inc(bd_hi, 1)
                act.wait_ge(gath1, 16 * KC)
                for c in range(KC):
                    act.activation(W1H[:, 0, c, :], W1R[:, c, 0:2 * D], ACT.Copy, scale=WS).then_inc(w1_hi, 1)
                act.activation(w["bias1"][:, :], W1R[:, :, 2 * D], ACT.Copy).then_inc(w1_hi, 1)
                for n in range(2 * KC):
                    act.wait_ge(w1_t, n + 1)
                    if n < KC:
                        act.activation(w["W1"][:, :, n, :].bitcast(F32), halves[n].rearrange(
                            "p (h c) -> p h c", h=2).bitcast(F32), ACT.Copy).then_inc(w1_out, 1)
                    else:
                        act.activation(BT1[:, n - KC, :, :].bitcast(F32), halves[n].rearrange(
                            "p (h c) -> p h c", h=2).bitcast(F32), ACT.Copy).then_inc(w1_out, 1)
                act.wait_ge(angle, 9)
                act.activation(res["sin"][:, :, :], rest[:, :, :], ACT.Sin).then_inc(trig, 1)
                act.activation(res["cos"][:, :, :], rest2[:, :, :], ACT.Sin, bias=halfpi[:, 0:1],
                               scale=-1.0).then_inc(trig, 1)

            @block.vector
            def _(dve):
                dve.wait_ge(small_in, 16 * len(small))
                dve.tensor_copy(condf[:, :], condi[:, :]).then_inc(ints, 1)
                dve.wait_ge(ints, 1)
                dve.tensor_scalar(crow[:, :], condf[:, :], float(S), pmod[:, 0:1], ALU.mult, ALU.add).then_inc(rows_ready, 1)
                dve.tensor_copy(permf[:, :], permi[:, :]).then_inc(ints, 1)
                dve.tensor_copy(id1f[:, :], id1[:, :]).then_inc(ints, 1)
                dve.tensor_copy(pgf[:, :], pgi[:, :]).then_inc(ints, 1)
                dve.tensor_copy(res["len"][:, :], leni[:, :]).then_inc(ints, 1)
                dve.tensor_copy(posf[:, :], posi[:, :]).then_inc(ints, 1)
                dve.wait_ge(ints, 6)
                dve.tensor_scalar(w["idx1"][:, :], id1f[:, :], float(R), pmod[0:U * R, 1:2], ALU.mult, ALU.add).then_inc(ints, 1)
                for hp in range(HP):
                    dve.tensor_scalar(pgh[:, hp, :], pgf[:, :], float(PS), float(hp * PAGES * PS), ALU.mult, ALU.add).then_inc(ints, 1)
                dve.wait_ge(ints, 7 + HP)
                dve.tensor_scalar(res["kvidx"][:, :, :], pgh[:, :, :], pmod[:, 0:1], None, ALU.add).then_inc(ints, 1)
                for c in range(KC):
                    dve.tensor_scalar(w["OH"][:, c, :], iota[:, :], permf[:, c:c + 1], None, ALU.is_equal).then_inc(ints, 1)
                for n, (_, dst, cols, scale) in enumerate(plan):
                    dve.wait_ge(hi_done, n + 1)
                    dve.scalar_tensor_tensor(flat(w[dst])[:, 1, :], raw[:, n % 2, 0:cols], scale,
                                             flat(w[dst])[:, 0, :], ALU.mult, ALU.subtract).then_inc(lo_done, 1)
                for layer, name in enumerate(("BD0", "BD2")):
                    for b in range(BT):
                        q = slice(S * b, S * b + S)
                        dve.wait_ge(bd_hi, layer * BT + b + 1)
                        dve.tensor_tensor(w[name][q, 1, :, q], G[q, layer, :, :], w[name][q, 0, :, q],
                                          ALU.subtract).then_inc(bd_lo, 1)
                for c in range(KC):
                    dve.wait_ge(w1_hi, c + 1)
                    dve.scalar_tensor_tensor(W1H[:, 1, c, :], W1R[:, c, 0:2 * D], WS, W1H[:, 0, c, :],
                                             ALU.mult, ALU.subtract).then_inc(w1_lo, 1)
                dve.wait_ge(lo_done, len(plan))
                c1, c2, c3 = cody_waite()
                n = [0]

                def step(ins):
                    n[0] += 1
                    ins.then_inc(angle, 1)
                    dve.wait_ge(angle, n[0])
                step(dve.memset(halfpi[:, :], float(np.pi / 2)))
                step(dve.tensor_scalar(posf2[:, :], posf[:, :], pmod[:, 0:1], None, ALU.add))
                step(dve.tensor_tensor(ang[:, :, :], posf2[:, :].unsqueeze(2).to_broadcast([P, NT, HD // 2]),
                                       freq[:, :].unsqueeze(1).to_broadcast([P, NT, HD // 2]), ALU.mult))
                step(dve.tensor_scalar(rest[:, :, :], ang[:, :, :], float(1.0 / TWO_PI), MAGIC, ALU.mult, ALU.add))
                step(dve.tensor_scalar(turns[:, :, :], rest[:, :, :], MAGIC, None, ALU.subtract))
                step(dve.scalar_tensor_tensor(rest[:, :, :], turns[:, :, :], -c1, ang[:, :, :], ALU.mult, ALU.add))
                step(dve.scalar_tensor_tensor(rest2[:, :, :], turns[:, :, :], -c2, rest[:, :, :], ALU.mult, ALU.add))
                step(dve.scalar_tensor_tensor(rest[:, :, :], turns[:, :, :], -c3, rest2[:, :, :], ALU.mult, ALU.add))
                step(dve.scalar_tensor_tensor(rest2[:, :, :], rest[:, :, :], -1.0, rest[:, :, :], ALU.mult, ALU.max))

            @block.tensor
            def _(pe):
                pe.wait_ge(trig, 1)
                pe.wait_ge(w1_lo, KC)
                for n in range(2 * KC):
                    for hl in range(2):
                        for c in range(KC):
                            last = pe.transpose(halves[n][:, (hl * KC + c) * P:(hl * KC + c + 1) * P],
                                                W1H[:, hl, c, n * P:(n + 1) * P], res["ident"][:, :])
                    last.then_inc(w1_t, 1)


def early_layers(nc, a, dram, res, w, banks, halves):
    WG, KG = W_PIECES // NG, KV_PIECES // NG
    QP = CH // 512
    MP = HP // QP
    with ExitStack() as ctx:
        def sb(name, shape, dt):
            return ctx.enter_context(nc.sbuf_tensor(name, shape, dt))

        def sem(name):
            return ctx.enter_context(nc.semaphore(name))

        X = sb("X", [P, U, D], F32)
        XH = sb("XH", [P, 2, U, D], F16)
        XT = sb("XT", [P, 2, KC, GT], F16)
        UT = sb("UT", [P, 2, KC, GT], F16)
        LL = sb("LL", [P, U, P + E], F32)
        LP = sb("LP", [P, U, P], F32)
        LH = sb("LH", [P, 2, U, P], F16)
        LT = sb("LT", [P, U, 2, P], F16)
        sm = sb("sm", [P, 3, U, E], F32)
        smr = sb("smr", [P, 3, U], F32)
        ALT = sb("ALT", [P, 2 * KC, U, U * R], F16)
        icol = sb("icol", [U * R, U], I32)
        HF = sb("HF", [U * R, GT], F32)
        HT = sb("HT", [U * R, 2, GT], F16)
        YF = sb("YF", [P, 2, GT], F32)
        YT = sb("YT", [P, 2, KC, GT], F16)
        ffn = sb("ffn", [P, 4 * GT], F32)
        GF = ffn[:, 0:2 * GT].rearrange("p (s n) -> p s n", s=2)
        GH = ffn[:, 2 * GT:4 * GT].bitcast(F16).rearrange("p (s h n) -> p s h n", s=2, h=2)
        BG = ffn[0:U * R, :].bitcast(F16).rearrange("p (u h n) -> p u h n", u=U, h=2)
        TT = UT
        QS, PR = (GF[:, i, :].rearrange("p (s n) -> p s n", s=2) for i in range(2))
        tick = sb("tick", [P, 4], F32)
        raw = sb("bg_raw", [P, 2, CH], F32)
        spl = sb("bg_split", [P, 2, CH], F16)

        names = ("x_in group_done xh_hi xh_lo ut_mm ut_hi ut_lo ll_mm ll_ev sm_step sm_exp lp lh_hi lh_lo lt_mm "
                 "lt_ev o_mm x_up xt_mm xt_act xt_dve alt_in ic_in bg_in h_mm hf ht_hi ht_lo y_mm yf yt_hi yt_lo "
                 "up_mm gelu gh_hi gh_lo dn_mm tt_hi tt_lo op_mm xb qk_mm qs pr sc hh_mm hh o2_mm x_out "
                 "bulk_hi bulk_lo bulk_in0 bulk_in1 hi_out lo_out il factor").split()
        s = {n: sem(n) for n in names}
        bulk_in = [s["bulk_in0"], s["bulk_in1"]]

        x_rows = a["x"].rearrange("(g u p) d -> g p u d", u=U, p=P)
        x3_rows = dram["x3"].rearrange("(g u p) d -> g p u d", u=U, p=P)
        bulk = a["bulk"]
        SM = 12

        with nc.Block() as block:
            def kv_rows(r, m, q, h):
                row = (m * QP + q) * (PAGES * PS)
                return dram["kv"][ds(r * P + row, P), h * 512:h * 512 + 512]

            def store_caches(sp, n, r, m):
                for h, (done, stored) in enumerate(((s["bulk_hi"], s["hi_out"]), (s["bulk_lo"], s["lo_out"]))):
                    sp.wait_ge(done, n + 1 + h)
                    for q in range(QP):
                        sp.dma_start(kv_rows(r, m, q, h), spl[:, h, q * 512:(q + 1) * 512]).then_inc(stored, 16)

            def load_piece(sp, n, slot, first):
                if not first:
                    sp.wait_ge(s["bulk_lo"], n)
                sp.dma_start(raw[:, slot, :], bulk[ds(n, 1), :, :].rearrange("o p c -> (o p) c")).then_inc(bulk_in[slot], 16)

            @block.sync
            def _(sp):
                sp.sem_inc(s["hi_out"], 16 * QP)
                sp.sem_inc(s["lo_out"], 16 * QP)
                load_piece(sp, 0, 0, True)
                load_piece(sp, 1, 1, True)
                with sp.Fori(0, NG) as g:
                    sp.wait_ge(s["group_done"], g + 1)
                    sp.dma_start(X[:, :, :], x_rows[ds(g, 1), :, :, :].rearrange("o p u d -> (o p) u d")).then_inc(s["x_in"], 16)
                    with sp.Fori(0, KG // 2) as k:
                        for m in range(MP):
                            n = g * (KG + WG) + k * 2 + m
                            store_caches(sp, n, g * (KG // 2) + k, m)
                            load_piece(sp, n + 2, m, False)
                    with sp.Fori(0, WG // 2) as k:
                        for m in range(2):
                            n = g * (KG + WG) + KG + k * 2 + m
                            sp.wait_ge(s["bulk_hi"], n + 1)
                            w_n = g * WG + k * 2 + m
                            sp.dma_start(dram["w3"][ds(w_n, 1), :, 0:CH].rearrange("o p c -> (o p) c"), spl[:, 0, :]).then_inc(s["hi_out"], 16 * QP)
                            sp.wait_ge(s["bulk_lo"], n + 2)
                            sp.dma_start(dram["w3"][ds(w_n, 1), :, CH:2 * CH].rearrange("o p c -> (o p) c"), spl[:, 1, :]).then_inc(s["lo_out"], 16 * QP)
                            load_piece(sp, n + 2, m, False)
                    sp.wait_ge(s["x_up"], g * 12 + 12)
                    sp.dma_start(x3_rows[ds(g, 1), :, :, :].rearrange("o p u d -> (o p) u d"), X[:, :, :]).then_inc(s["x_out"], 16)
                sp.wait_ge(s["x_out"], 16 * NG)
                sp.wait_ge(s["hi_out"], 16 * QP * (W_PIECES + KV_PIECES + 1))
                sp.wait_ge(s["lo_out"], 16 * QP * (W_PIECES + KV_PIECES + 1))
                for slot in range(2):
                    sp.wait_ge(bulk_in[slot], 16 * ((W_PIECES + KV_PIECES) // 2 + 1))

            @block.gpsimd
            def _(pool):
                pool.memset(tick[:, 1:2], 0.0).then_inc(s["bulk_lo"], 1)
                pool.memset(tick[:, 3:4], WS).then_inc(s["factor"], 1)
                pool.wait_ge(s["factor"], 1)
                with pool.Fori(0, NG) as g:
                    pool.wait_ge(s["group_done"], g + 1)
                    pool.tensor_copy(icol[:, :], w["idx1"][:, ds(g * U, U)]).then_inc(s["ic_in"], 1)
                    for b in range(U * BT):
                        v = pool.value_load(w["ids"][0:1, ds(g * (U * BT) + b, 1)], min_val=0, max_val=NA - 1)
                        pool.tensor_copy(ALT[:, :, b // BT, (b % BT) * R:(b % BT + 1) * R],
                                         w["ATA"][:, :, :, ds(v * R, R)].rearrange("p h k r -> p (h k) r")).then_inc(s["alt_in"], 1)
                    pool.wait_ge(s["ic_in"], g + 1)
                    pool.tensor_tensor(tick[0:U * R, 2:3], w["hmask"][:, 0:1], w["hmask"][:, 0:1], ALU.add).then_inc(s["il"], 1)
                    for u in range(U):
                        pool.indirect_dma_start(BG[:, u, :, :].rearrange("p h n -> p (h n)"), None, dram["bt"],
                                                bass.IndirectOffsetOnAxis(icol[:, u:u + 1], 0)).then_inc(s["bg_in"], 16)
                    for pieces, before, weights in ((KG, 0, False), (WG, KG, True)):
                        with pool.Fori(0, pieces // 2) as k:
                            for m in range(2):
                                n = g * (KG + WG) + (k * 2 + (before + m))
                                pool.wait_ge(bulk_in[m], (g * ((KG + WG) // 2) + (k + before // 2)) * 16 + 16)
                                pool.wait_ge(s["bulk_lo"], n + 1)
                                if weights:
                                    pool.tensor_tensor(raw[:, m, :], raw[:, m, :], tick[:, 3:4].to_broadcast([P, CH]), ALU.mult).then_inc(s["factor"], 1)
                                    pool.wait_ge(s["factor"], g * WG + (k * 2 + (m + 2)))
                                pool.wait_ge(s["hi_out"], n * 16 * QP + 16 * QP)
                                pool.tensor_tensor(spl[:, 0, :], raw[:, m, :], tick[:, 1:2].to_broadcast([P, CH]), ALU.add).then_inc(s["bulk_hi"], 1)
                                pool.wait_ge(s["bulk_hi"], n + 1)
                                pool.wait_ge(s["lo_out"], n * 16 * QP + 16 * QP)
                                pool.tensor_tensor(spl[:, 1, :], raw[:, m, :], spl[:, 0, :], ALU.subtract).then_inc(s["bulk_lo"], 1)

            @block.scalar
            def _(act):
                with act.Fori(0, NG) as g:
                    def split_x(k):
                        for u in range(U):
                            if k == 0 and u == 0:
                                act.wait_ge(s["x_in"], g * 16 + 16)
                            if k > 0:
                                act.wait_ge(s["x_up"], g * 12 + (k - 1) * U + u + 1)
                            act.activation(XH[:, 0, u, :], X[:, u, :], ACT.Copy).then_inc(s["xh_hi"], 1)

                    def mixed(k):
                        for u in range(U):
                            act.wait_ge(s["ut_mm"], g * 2 * U + k * U + u + 1)
                            act.activation(UT[:, 0, :, u * P:(u + 1) * P],
                                           banks[u][:, :].rearrange("p (c t) -> p c t", c=KC), ACT.Copy).then_inc(s["ut_hi"], 1)

                    def softmax_exp(k):
                        act.wait_ge(s["sm_step"], g * SM + k * (SM // 2) + 3)
                        act.activation(sm[:, 1, :, :], sm[:, 0, :, :], ACT.Exp).then_inc(s["sm_exp"], 1)

                    def low_rows(k):
                        act.wait_ge(s["lp"], g * 2 + k + 1)
                        act.activation(LH[:, 0, :, :], LP[:, :, :], ACT.Copy).then_inc(s["lh_hi"], 1)
                        act.wait_ge(s["lt_mm"], g * 2 + k + 1)
                        act.activation(LT[:, :, :, :].rearrange("p u h t -> p (u h t)").bitcast(F32),
                                       banks[(0, 1)[k]][:, :], ACT.Copy).then_inc(s["lt_ev"], 1)

                    act.wait_ge(s["group_done"], g + 1)
                    split_x(0)
                    mixed(0)
                    softmax_exp(0)
                    low_rows(0)
                    split_x(1)
                    for u in (0, 2):
                        act.wait_ge(s["xt_mm"], g * 2 * U + u + 1)
                        act.activation(XT[:, :, :, u * P:(u + 1) * P].rearrange("p h c t -> p (h c) t").bitcast(F32),
                                       halves[u].rearrange("p (n t) -> p n t", t=P).bitcast(F32), ACT.Copy).then_inc(s["xt_act"], 1)
                    act.wait_ge(s["hf"], g + 1)
                    act.activation(HT[:, 0, :], HF[:, :], ACT.Copy).then_inc(s["ht_hi"], 1)
                    for c in range(KC):
                        act.wait_ge(s["y_mm"], g * KC + c + 1)
                        if c >= 2:
                            act.wait_ge(s["yt_lo"], g * KC + c - 1)
                        act.activation(YF[:, c % 2, :], banks[c][:, :], ACT.Identity, bias=w["bias1"][:, c:c + 1],
                                       scale=1.0 / WS).then_inc(s["yf"], 1)
                        act.wait_ge(s["yf"], g * KC + c + 1)
                        act.activation(YT[:, 0, c, :], YF[:, c % 2, :], ACT.Copy).then_inc(s["yt_hi"], 1)
                    for k in range(FH):
                        act.wait_ge(s["up_mm"], g * FH + k + 1)
                        if k >= 2:
                            act.wait_ge(s["gh_lo"], g * FH + k - 1)
                        act.activation(GF[:, k % 2, :], banks[4 + k % 2][:, :], ACT.Gelu).then_inc(s["gelu"], 1)
                        if k % BT == 1 and k > BT:
                            q = k // BT - 1
                            act.wait_ge(s["dn_mm"], g * FH + q * BT + BT)
                            act.activation(TT[:, 0, q, :], banks[6 + q % 2][:, :], ACT.Copy).then_inc(s["tt_hi"], 1)
                    act.wait_ge(s["dn_mm"], g * FH + FH)
                    act.activation(TT[:, 0, KC - 1, :], banks[6 + (KC - 1) % 2][:, :], ACT.Copy).then_inc(s["tt_hi"], 1)
                    split_x(2)
                    mixed(1)
                    for u in range(U):
                        act.wait_ge(s["qk_mm"], g * U + u + 1)
                        if u >= 2:
                            act.wait_ge(s["pr"], g * U + u - 1)
                        act.activation(QS[:, u % 2, :], banks[u][:, 0:E * DK], ACT.Copy,
                                       scale=float(1.0 / (WS * WS * np.sqrt(DK)))).then_inc(s["qs"], 1)
                    softmax_exp(1)
                    low_rows(1)
                    split_x(3)
                    for u in (0, 2):
                        act.wait_ge(s["xt_mm"], g * 2 * U + U + u + 1)
                        act.activation(res["x3T"][:, :, :, ds(g * GT + u * P, P)].rearrange("p h c t -> p (h c) t"),
                                       halves[1 + u].rearrange("p (n t) -> p n t", t=P), ACT.Copy).then_inc(s["xt_act"], 1)

            @block.vector
            def _(dve):
                dve.memset(tick[:, 0:1], 0.0).then_inc(s["group_done"], 1)
                with dve.Fori(0, NG) as g:
                    def split_x(k):
                        for u in range(U):
                            dve.wait_ge(s["xh_hi"], g * 4 * U + k * U + u + 1)
                            dve.tensor_tensor(XH[:, 1, u, :], X[:, u, :], XH[:, 0, u, :], ALU.subtract).then_inc(s["xh_lo"], 1)

                    def mixed(k):
                        for u in range(U):
                            dve.wait_ge(s["ut_hi"], g * 2 * U + k * U + u + 1)
                            dve.tensor_tensor(UT[:, 1, :, u * P:(u + 1) * P],
                                              banks[u][:, :].rearrange("p (c t) -> p c t", c=KC),
                                              UT[:, 0, :, u * P:(u + 1) * P], ALU.subtract).then_inc(s["ut_lo"], 1)

                    def softmax(k, scale):
                        n = [0]

                        def step(ins):
                            n[0] += 1
                            ins.then_inc(s["sm_step"], 1)
                            dve.wait_ge(s["sm_step"], g * SM + k * (SM // 2) + n[0])
                        logits = LL[:, :, P:P + E]
                        step(dve.tensor_reduce(smr[:, 0, :], logits, AX.X, ALU.max))
                        step(dve.tensor_copy(tick[:, 0:1], smr[:, 0, 0:1]))
                        step(dve.tensor_tensor(sm[:, 0, :, :], logits, smr[:, 0, :].unsqueeze(2).to_broadcast([P, U, E]), ALU.subtract))
                        dve.wait_ge(s["sm_exp"], g * 2 + k + 1)
                        step(dve.tensor_reduce(smr[:, 1, :], sm[:, 1, :, :], AX.X, ALU.add))
                        step(dve.reciprocal(smr[:, 2, :], smr[:, 1, :]))
                        step(dve.scalar_tensor_tensor(sm[:, 2, :, :], sm[:, 1, :, :], scale,
                                                      smr[:, 2, :].unsqueeze(2).to_broadcast([P, U, E]), ALU.mult, ALU.mult))
                        assert n[0] == SM // 2
                        dve.tensor_tensor(LP[:, :, :].rearrange("p u (e r) -> p u e r", r=R),
                                          LL[:, :, 0:P].rearrange("p u (e r) -> p u e r", r=R),
                                          sm[:, 2, :, :].unsqueeze(3).to_broadcast([P, U, E, R]), ALU.mult).then_inc(s["lp"], 1)
                        dve.wait_ge(s["lh_hi"], g * 2 + k + 1)
                        dve.tensor_tensor(LH[:, 1, :, :], LP[:, :, :], LH[:, 0, :, :], ALU.subtract).then_inc(s["lh_lo"], 1)

                    dve.wait_ge(s["group_done"], g + 1)
                    split_x(0)
                    mixed(0)
                    for u in range(U):
                        dve.wait_ge(s["ll_mm"], g * U + u + 1)
                        dve.tensor_scalar(LL[:, u, :], banks[4 + u][:, 0:P + E], 1.0 / WS, None, ALU.mult).then_inc(s["ll_ev"], 1)
                    dve.wait_ge(s["ll_ev"], g * (U + 1) + U)
                    dve.tensor_tensor(LL[:, :, P:P + E], LL[:, :, P:P + E],
                                      w["br"][:, :].unsqueeze(1).to_broadcast([P, U, E]), ALU.add).then_inc(s["ll_ev"], 1)
                    dve.wait_ge(s["ll_ev"], g * (U + 1) + U + 1)
                    softmax(0, 2.0 * E)
                    for u in range(U):
                        dve.wait_ge(s["o_mm"], g * U + u + 1)
                        dve.scalar_tensor_tensor(X[:, u, :], banks[4 + u][:, :], 1.0 / WS, X[:, u, :], ALU.mult, ALU.add).then_inc(s["x_up"], 1)
                    split_x(1)
                    for u in (1, 3):
                        dve.wait_ge(s["xt_mm"], g * 2 * U + u + 1)
                        dve.tensor_copy(XT[:, :, :, u * P:(u + 1) * P].rearrange("p h c t -> p (h c) t").bitcast(F32),
                                        halves[u].rearrange("p (n t) -> p n t", t=P).bitcast(F32)).then_inc(s["xt_dve"], 1)
                    dve.wait_ge(s["h_mm"], g + 1)
                    dve.tensor_tensor(HF[:, :].rearrange("p (u t) -> p u t", t=P),
                                      banks[4][0:U * R, :].rearrange("p (u t) -> p u t", t=P),
                                      w["hmask"][:, :].unsqueeze(1).to_broadcast([U * R, U, P]), ALU.mult).then_inc(s["hf"], 1)
                    dve.wait_ge(s["ht_hi"], g + 1)
                    dve.tensor_tensor(HT[:, 1, :], HF[:, :], HT[:, 0, :], ALU.subtract).then_inc(s["ht_lo"], 1)
                    for c in range(KC):
                        dve.wait_ge(s["yt_hi"], g * KC + c + 1)
                        dve.tensor_tensor(YT[:, 1, c, :], YF[:, c % 2, :], YT[:, 0, c, :], ALU.subtract).then_inc(s["yt_lo"], 1)
                    for k in range(FH):
                        dve.wait_ge(s["gelu"], g * FH + k + 1)
                        if k >= 2:
                            dve.wait_ge(s["dn_mm"], g * FH + k - 1)
                        dve.tensor_copy(GH[:, k % 2, 0, :], GF[:, k % 2, :]).then_inc(s["gh_hi"], 1)
                        dve.wait_ge(s["gh_hi"], g * FH + k + 1)
                        dve.tensor_tensor(GH[:, k % 2, 1, :], GF[:, k % 2, :], GH[:, k % 2, 0, :], ALU.subtract).then_inc(s["gh_lo"], 1)
                        if k % BT == 2 and k > BT:
                            q = k // BT - 1
                            dve.wait_ge(s["tt_hi"], g * KC + q + 1)
                            dve.tensor_tensor(TT[:, 1, q, :], banks[6 + q % 2][:, :], TT[:, 0, q, :], ALU.subtract).then_inc(s["tt_lo"], 1)
                    dve.wait_ge(s["tt_hi"], g * KC + KC)
                    dve.tensor_tensor(TT[:, 1, KC - 1, :], banks[6 + (KC - 1) % 2][:, :], TT[:, 0, KC - 1, :], ALU.subtract).then_inc(s["tt_lo"], 1)
                    for u in range(U):
                        dve.wait_ge(s["op_mm"], g * U + u + 1)
                        dve.tensor_tensor(X[:, u, :], banks[u][:, :], X[:, u, :], ALU.add).then_inc(s["x_up"], 1)
                    split_x(2)
                    dve.wait_ge(s["xh_lo"], g * 4 * U + 3 * U)
                    dve.tensor_tensor(X[:, :, :], X[:, :, :], w["b2"][:, :].unsqueeze(1).to_broadcast([P, U, D]), ALU.add).then_inc(s["xb"], 1)
                    mixed(1)
                    for u in range(U):
                        dve.wait_ge(s["qs"], g * U + u + 1)
                        if u >= 2:
                            dve.wait_ge(s["sc"], g * U + u - 1)
                        dve.tensor_tensor(PR[:, u % 2, :], banks[u][:, E * DK:2 * E * DK], QS[:, u % 2, :], ALU.mult).then_inc(s["pr"], 1)
                        dve.wait_ge(s["pr"], g * U + u + 1)
                        dve.tensor_reduce(LL[:, u, P:P + E], PR[:, u % 2, :].rearrange("p (e k) -> p e k", k=DK), AX.X, ALU.add).then_inc(s["sc"], 1)
                    dve.wait_ge(s["hh_mm"], g + 1)
                    dve.tensor_scalar(LL[:, :, 0:P], banks[4][:, :].rearrange("p (u t) -> p u t", t=P), 1.0 / WS, None, ALU.mult).then_inc(s["hh"], 1)
                    dve.wait_ge(s["sc"], g * U + U)
                    dve.wait_ge(s["hh"], g + 1)
                    softmax(1, 1.0)
                    dve.wait_ge(s["xb"], g + 1)
                    for u in range(U):
                        dve.wait_ge(s["o2_mm"], g * U + u + 1)
                        dve.scalar_tensor_tensor(X[:, u, :], banks[(5, 6, 7, 0)[u]][:, :], 1.0 / WS, X[:, u, :], ALU.mult, ALU.add).then_inc(s["x_up"], 1)
                    split_x(3)
                    for u in (1, 3):
                        dve.wait_ge(s["xt_mm"], g * 2 * U + U + u + 1)
                        dve.tensor_copy(res["x3T"][:, :, :, ds(g * GT + u * P, P)].rearrange("p h c t -> p (h c) t"),
                                        halves[1 + u].rearrange("p (n t) -> p n t", t=P)).then_inc(s["xt_dve"], 1)
                    dve.wait_ge(s["xt_act"], g * 4 + 4)
                    dve.wait_ge(s["xt_dve"], g * 4 + 4)
                    dve.wait_ge(s["x_out"], g * 16 + 16)
                    dve.memset(tick[:, 0:1], 0.0).then_inc(s["group_done"], 1)

            @block.tensor
            def _(pe):
                with pe.Fori(0, NG) as g:
                    def mix(k, bd):
                        for u in range(U):
                            pe.wait_ge(s["xh_lo"], g * 4 * U + 2 * k * U + u + 1)
                            for c in range(KC):
                                last = mm3(pe, banks[u][:, c * P:(c + 1) * P],
                                           lambda h: XH[:, h, u, c * P:(c + 1) * P],
                                           lambda h: bd[:, h, ds(g * U + u, 1), :].rearrange("p o t -> p (o t)"), True, True)
                            last.then_inc(s["ut_mm"], 1)

                    def low_t(k):
                        pe.wait_ge(s["lh_lo"], g * 2 + k + 1)
                        for u in range(U):
                            for h in range(2):
                                last = pe.transpose(halves[k][:, (u * 2 + h) * P:(u * 2 + h + 1) * P], LH[:, h, u, :], res["ident"][:, :])
                        last.then_inc(s["lt_mm"], 1)

                    def turn_x(k, bank0):
                        for u in range(U):
                            pe.wait_ge(s["xh_lo"], g * 4 * U + (2 * k + 1) * U + u + 1)
                            for h in range(2):
                                for c in range(KC):
                                    last = pe.transpose(halves[bank0 + u][:, (h * KC + c) * P:(h * KC + c + 1) * P],
                                                        XH[:, h, u, c * P:(c + 1) * P], res["ident"][:, :])
                            last.then_inc(s["xt_mm"], 1)

                    def rows(bank, cols, src, u, wt, first=True, last=True):
                        for c in range(KC):
                            ins = mm3(pe, bank, lambda h: src[:, h, c, u * P:(u + 1) * P],
                                      lambda h: wt[:, h, c, 0:cols], first and c == 0, last and c == KC - 1)
                        return ins

                    pe.wait_ge(s["group_done"], g + 1)
                    mix(0, w["BD0"])
                    for u in range(U):
                        pe.wait_ge(s["ut_lo"], g * 2 * U + u + 1)
                        rows(banks[4 + u][:, 0:P + E], P + E, UT, u, w["A0"]).then_inc(s["ll_mm"], 1)
                    low_t(0)
                    pe.wait_ge(s["lt_ev"], g * 2 + 1)
                    for u in range(U):
                        mm3(pe, banks[4 + u][:, :], lambda h: LT[:, u, h, :], lambda h: w["B0"][:, h, :], True, True).then_inc(s["o_mm"], 1)
                    turn_x(0, 0)
                    pe.wait_ge(s["xt_act"], g * 4 + 2)
                    pe.wait_ge(s["xt_dve"], g * 4 + 2)
                    pe.wait_ge(s["alt_in"], g * (U * BT) + U * BT)
                    for u in range(U):
                        for c in range(KC):
                            last = mm3(pe, banks[4][0:U * R, u * P:(u + 1) * P], lambda h: ALT[:, h * KC + c, u, :],
                                       lambda h: XT[:, h, c, u * P:(u + 1) * P], c == 0, c == KC - 1)
                    last.then_inc(s["h_mm"], 1)
                    for o in range(KC):
                        for c in range(KC):
                            mm3(pe, banks[o][:, :], lambda h: w["W1"][:, h, c, o * P:(o + 1) * P],
                                lambda h: XT[:, h, c, :], c == 0, False)
                    pe.wait_ge(s["ht_lo"], g + 1)
                    pe.wait_ge(s["bg_in"], g * 16 * U + 16 * U)
                    for o in range(KC):
                        for u in range(U):
                            last = mm3(pe, banks[o][:, u * P:(u + 1) * P], lambda h: BG[:, u, h, o * P:(o + 1) * P],
                                       lambda h: HT[:, h, u * P:(u + 1) * P], False, True)
                        last.then_inc(s["y_mm"], 1)

                    def up(k):
                        if k % BT == 0:
                            pe.wait_ge(s["yt_lo"], g * KC + k // BT + 1)
                        if k >= 2:
                            pe.wait_ge(s["gelu"], g * FH + k - 1)
                        mm3(pe, banks[4 + k % 2][:, :], lambda h: w["UP"][:, h, k, :],
                            lambda h: YT[:, h, k // BT, :], True, True).then_inc(s["up_mm"], 1)

                    def down(k):
                        q = k // BT
                        pe.wait_ge(s["gh_lo"], g * FH + k + 1)
                        if k % BT == 0 and q >= 2:
                            pe.wait_ge(s["tt_lo"], g * KC + q - 1)
                        mm3(pe, banks[6 + q % 2][:, :], lambda h: w["DN"][:, h, k, :],
                            lambda h: GH[:, k % 2, h, :], k % BT == 0, k % BT == BT - 1).then_inc(s["dn_mm"], 1)

                    up(0)
                    for k in range(FH):
                        if k + 1 < FH:
                            up(k + 1)
                        down(k)
                    pe.wait_ge(s["tt_lo"], g * KC + KC)
                    for u in range(U):
                        for c in range(KC):
                            for h in range(2):
                                last = pe.matmul(banks[u][:, :], TT[:, h, c, u * P:(u + 1) * P], w["OH"][:, c, :],
                                                 start=c == 0 and h == 0, stop=c == KC - 1 and h == 1)
                        last.then_inc(s["op_mm"], 1)
                    mix(1, w["BD2"])
                    for u in range(U):
                        pe.wait_ge(s["ut_lo"], g * 2 * U + U + u + 1)
                        rows(banks[u][:, :], 2 * E * DK, UT, u, w["QK2"]).then_inc(s["qk_mm"], 1)
                    for u in range(U):
                        last = rows(banks[4][:, u * P:(u + 1) * P], P, UT, u, w["A2"])
                    last.then_inc(s["hh_mm"], 1)
                    for u in range(U):
                        if u == 3:
                            pe.wait_ge(s["pr"], g * U + 1)
                        rows(banks[(5, 6, 7, 0)[u]][:, :], D, UT, u, w["W2"], last=False)
                    pe.wait_ge(s["pr"], g * U + 2)
                    low_t(1)
                    pe.wait_ge(s["lt_ev"], g * 2 + 2)
                    for u in range(U):
                        mm3(pe, banks[(5, 6, 7, 0)[u]][:, :], lambda h: LT[:, u, h, :], lambda h: w["B2"][:, h, :],
                            False, True).then_inc(s["o2_mm"], 1)
                    turn_x(1, 1)


def late(nc, a, dram, res, banks, halves, out):
    with ExitStack() as ctx:
        Y = ctx.enter_context(nc.sbuf_tensor("Y", [P, NT, D], F32))
        attention(nc, a, dram, res, banks, halves, Y)
        last_ffn(nc, a, dram, res, banks, halves, Y, out)


def attention(nc, a, dram, res, banks, halves, Y):
    NR = HP * NT
    J = 2 * BT
    HR = HQ // HK
    WQ = HD * HR
    SC = 1.0 / float(np.sqrt(HD))
    BF16 = mybir.dt.bfloat16
    WQ_RANGE = range(WQ_COLS // CH)
    WKV_RANGE = range(WQ_COLS // CH, (WQ_COLS + WKV_COLS) // CH)
    WO_RANGE = range((WQ_COLS + WKV_COLS) // CH, W3_COLS // CH)
    with ExitStack() as ctx:
        def sb(name, shape, dt):
            return ctx.enter_context(nc.sbuf_tensor(name, shape, dt))

        W3 = sb("W3", [P, 2, W3_COLS], F16)
        wq = W3[:, :, 0:WQ_COLS].rearrange("p h (c n) -> p h c n", c=KC)
        wkv = W3[:, :, WQ_COLS:WQ_COLS + WKV_COLS].rearrange("p h (c n) -> p h c n", c=KC)
        wo = W3[:, :, WQ_COLS + WKV_COLS:].rearrange("p h (q n) -> p h q n", q=QH)
        KV = sb("KV", [P, BT, CC, 1024], F16)
        KT = sb("KT", [P, 2, 2, CL], F16)
        SS = sb("SS", [P, 2, CL + S], F32)
        PH = sb("PH", [P, 2, 2, CL + S], F16)
        PT = sb("PT", [P, 2, 2, CL + P], F16)
        MK = sb("MK", [P, BT, CL], BF16)
        iota = sb("iota2", [P, CL], F16)
        mark = sb("mark", [P, 1], F32)
        QT = sb("QT", [P, 2, J, P], F16)
        QTV = [QT[:, i, :, :].rearrange("p (b v) (h t) -> p v h b t", v=2, t=S) for i in range(2)]
        KN = sb("KN", [P, 2, 2, P], F16)
        TK = sb("TK", [P, 2 * HD], F32)
        TQ = sb("TQ", [P, 2, WQ], F32)
        T2 = sb("T2", [P, 2, WQ], F32)
        VH = sb("VH", [P, 2, 2, 2 * HD], F16)
        VN = sb("VN", [S, BT, 2, 2 * HD], F16)
        SN = sb("SN", [P, J, S], F32)
        mnew = sb("mnew", [P, J], F32)
        OT = sb("OT", [P, 2, 2, QH, P], F16)
        tab = sb("tab", [P, 4, HD], F32)
        nw = sb("nw", [P, 4, HD], F32)
        ssq = sb("ssq", [P, QH + 2], F32)
        var = sb("var", [P, QH + 2], F32)
        rstd = sb("rstd", [P, QH + 2], F32)
        power = sb("power", [P, 1], F32)
        junk = sb("junk", [P, HD], F32)
        ic = sb("ic", [P, BT, CC], I32)
        lcol = sb("lcol", [P, BT], F32)
        st = sb("st", [P, 2, 5], F32)

        names = ("const_in kt_mm kt_ev s_mm ttr sn_cp neg exp sum rec ph_hi prob t_mm pt_ev pv_mm o_hi o_lo "
                 "kv_mm q_mm wo_mm kn_mm qt_mm sn_mm sq vh_hi vh_lo rope t2_free turned var_ok pow_ok roped kn_hi "
                 "kn_lo qt_hi qt_lo sn_ev mnew_ok y_add kv_in0 kv_in1 kv_in2 kv_in3 vn_in0 vn_in1 vn_in2 vn_in3 "
                 "wkv_in wq_in wo_in ic_ok lc_ok mask_ok marked tab_ok nw_ok").split()
        s = {n: ctx.enter_context(nc.semaphore("a_" + n)) for n in names}
        kv_in = [s[f"kv_in{b}"] for b in range(BT)]
        vn_in = [s[f"vn_in{b}"] for b in range(BT)]
        KTB, PTB, PB = banks[2], banks[3], [banks[6], banks[7]]
        SB = [banks[0], banks[1]]
        OB = [banks[4], banks[5]]
        consts = [(iota, a["c_iota16"]), (nw, a["norm_w"])]

        with nc.Block() as block:
            @block.sync
            def _(sp):
                def load_w(hp, pieces, name):
                    for i in pieces:
                        sp.dma_start(W3[:, :, i * CH:(i + 1) * CH],
                                     dram["w3"][ds(hp * (W3_COLS // CH) + i, 1), :, :].rearrange("o p (h c) -> (o p) h c", h=2)).then_inc(s[name], 16)

                def new_values(n, b, first):
                    if b == 0:
                        sp.wait_ge(s["vh_lo"], n + 1)
                    if not first:
                        sp.wait_ge(s["pv_mm"], n * J - J + 2 * b + 2)

                def copy_values(slot, b):
                    sp.dma_start(VN[:, b, :, :], VH[S * b:S * b + S, slot, :, :]).then_inc(vn_in[b], 16)

                for dst, src in consts:
                    sp.dma_start(dst[...], src).then_inc(s["const_in"], 16)
                load_w(0, WKV_RANGE, "wkv_in")
                load_w(0, WQ_RANGE, "wq_in")
                load_w(0, WO_RANGE, "wo_in")
                for b in range(BT):
                    new_values(0, b, True)
                    copy_values(0, b)
                new_values(1, 0, False)
                copy_values(1, 0)
                for b in range(1, BT):
                    new_values(1, b, False)
                    copy_values(1, b)

                def two(n):
                    for i in range(2):
                        for b in range(BT):
                            new_values(n + i, b, False)
                            copy_values(i, b)

                with sp.Fori(0, HP - 1) as hp:
                    with sp.Fori(1, NT // 2 - 1) as k:
                        two(hp * NT + 2 * k)
                    for b in range(BT):
                        new_values(hp * NT + (NT - 2), b, False)
                        copy_values(0, b)
                    sp.wait_ge(s["kv_mm"], hp * NT + NT)
                    load_w(hp + 1, WKV_RANGE, "wkv_in")
                    for b in range(BT):
                        if b == 1:
                            sp.wait_ge(s["q_mm"], hp * (2 * NT) + 2 * NT)
                            load_w(hp + 1, WQ_RANGE, "wq_in")
                        new_values(hp * NT + (NT - 1), b, False)
                        copy_values(1, b)
                    for b in range(BT):
                        new_values(hp * NT + NT, b, False)
                        copy_values(0, b)
                    sp.wait_ge(s["wo_mm"], hp * NT + NT)
                    load_w(hp + 1, WO_RANGE, "wo_in")
                    for b in range(BT):
                        new_values(hp * NT + (NT + 1), b, False)
                        copy_values(1, b)
                with sp.Fori(1, NT // 2) as k:
                    two(2 * k + (HP - 1) * NT)
                for b in range(BT):
                    sp.wait_ge(vn_in[b], 16 * NR)

            @block.gpsimd
            def _(pool):
                def indices(n):
                    for b in range(BT):
                        if not (isinstance(n, int) and n == 0):
                            pool.wait_ge(kv_in[b], n * (16 * CC))
                    pool.tensor_copy(ic[:, :, :].rearrange("p b c -> p (b c)"),
                                     res["kvidx"][:, :, :].rearrange("p h i -> p (h i)")[:, ds(n * (BT * CC), BT * CC)]).then_inc(s["ic_ok"], 1)

                def gather(n, b, first=False):
                    if not first:
                        pool.wait_ge(s["pv_mm"], n * J - J + 2 * b + 2)
                    pool.wait_ge(s["ic_ok"], n + 1)
                    pool.wait_ge(s["marked"], n * BT + b + 1)
                    pool.tensor_tensor(mark[:, :], power[:, :], power[:, :], ALU.add).then_inc(s["marked"], 1)
                    for c in range(CC):
                        pool.indirect_dma_start(KV[:, b, c, :], None, dram["kv"],
                                                bass.IndirectOffsetOnAxis(ic[:, b, c:c + 1], 0)).then_inc(kv_in[b], 16)

                def tables(n):
                    g = n % NT
                    for i, t in enumerate(("cos", "sin")):
                        for qk in range(2):
                            pool.tensor_tensor(tab[:, 2 * qk + i, :].rearrange("p (s f) -> p s f", s=2),
                                               res[t][:, ds(g, 1), :].to_broadcast([P, 2, HD // 2]),
                                               nw[:, 2 * qk + i, :].rearrange("p (s f) -> p s f", s=2), ALU.mult).then_inc(s["tab_ok"], 1)

                def rotate(n, i):
                    t = TK[:, :] if i == 0 else TQ[:, i - 1, :]
                    t2 = T2[:, i % 2, 0:2 * HD] if i == 0 else T2[:, i % 2, :]
                    h0, nh = (QH, 2) if i == 0 else (HR * (i - 1), HR)
                    pool.wait_ge(s["rope"], n * 3 + i + 1)
                    pool.wait_ge(s["sq"], n * (QH + 2) + (2, 2 + HR, 2 + 2 * HR)[i])
                    pool.tensor_tensor(t, t, t2, ALU.add).then_inc(s["turned"], 1)
                    pool.tensor_scalar(var[:, h0:h0 + nh], ssq[:, h0:h0 + nh], WS * WS / HD, EPS * WS * WS, ALU.mult, ALU.add).then_inc(s["var_ok"], 1)
                    pool.wait_ge(s["var_ok"], n * 3 + i + 1)
                    pool.tensor_tensor(rstd[:, h0:h0 + nh], var[:, h0:h0 + nh], power[:, :].to_broadcast([P, nh]), ALU.pow).then_inc(s["pow_ok"], 1)
                    pool.wait_ge(s["turned"], n * 3 + i + 1)
                    pool.wait_ge(s["pow_ok"], n * 3 + i + 1)
                    th = t.rearrange("p (h d) -> p h d", d=HD)
                    pool.tensor_tensor(th, th, rstd[:, h0:h0 + nh].unsqueeze(2).to_broadcast([P, nh, HD]), ALU.mult).then_inc(s["roped"], 1)

                pool.memset(power[:, :], -0.5).then_inc(s["marked"], 1)
                pool.wait_ge(s["const_in"], 16 * len(consts))
                for i in (1, 3):
                    pool.tensor_scalar(nw[:, i, 0:HD // 2], nw[:, i, 0:HD // 2], -1.0, None, ALU.mult).then_inc(s["nw_ok"], 1)
                pool.wait_ge(s["nw_ok"], 2)
                tables(0)
                pool.wait_ge(s["marked"], 1)
                indices(0)
                gather(0, 0, True)
                gather(0, 1, True)
                for i in range(3):
                    rotate(0, i)
                tables(1)
                gather(0, 2, True)
                gather(0, 3, True)

                def body(n, first, ahead):
                    if not first:
                        gather(n, 3)
                    rotate(n + 1, 0)
                    indices(n + 1)
                    gather(n + 1, 0)
                    rotate(n + 1, 1)
                    rotate(n + 1, 2)
                    if ahead:
                        tables(n + 2)
                    gather(n + 1, 1)
                    gather(n + 1, 2)
                body(0, True, True)
                with pool.Fori(1, NR - 2) as n:
                    body(n, False, True)
                body(NR - 2, False, False)
                gather(NR - 1, 3)

            WO_HEADS = {4: (0, 1), 5: (2,), 6: (3, 4), 7: (5, 6, 7)}
            assert sum(len(q) for q in WO_HEADS.values()) == QH

            def outputs(n, h, j):
                slot = ds(n % 2, 1)
                return OT[:, slot, h, HR * (j % 2):HR * (j % 2) + HR, S * (j // 2):S * (j // 2) + S].rearrange("p o h t -> p (o h) t")

            def steps(eng, step):
                for j in range(J):
                    step(0, j, True, False)
                with eng.Fori(1, NR - 1) as n:
                    for j in range(J):
                        step(n, j, False, False)
                for j in range(J):
                    step(NR - 1, j, False, True)

            @block.scalar
            def _(act):
                def kt_evac(m, j):
                    act.wait_ge(s["kt_mm"], m + 1)
                    if not (isinstance(m, int) and m < 2):
                        act.wait_ge(s["s_mm"], m - 1)
                    act.activation(KT[:, j % 2, :, :].rearrange("p h k -> p (h k)").bitcast(F32), KTB[:, :], ACT.Copy).then_inc(s["kt_ev"], 1)

                def exps(m, j):
                    act.wait_ge(s["neg"], m + 1)
                    act.activation(SS[:, j % 2, :], SS[:, j % 2, :], ACT.Exp, bias=st[:, j % 2, 1:2], scale=SC,
                                   accum_out=st[:, j % 2, 2:3]).then_inc(s["exp"], 1)

                def squares(n, i):
                    bank = PB[i % 2]
                    h0, nh = (QH, 2) if i == 0 else (HR * (i - 1), HR)
                    act.wait_ge(s["kv_mm"] if i == 0 else s["q_mm"], n + 1 if i == 0 else n * 2 + i)
                    if not (isinstance(n, int) and n == 0):
                        act.wait_ge(s["var_ok"], n * 3 - 2 + i)
                    for h in range(nh):
                        done = n * (QH + 2) + (0, 2, 2 + HR)[i] + h
                        if not (isinstance(done, int) and done == 0):
                            act.wait_ge(s["sq"], done)
                        act.activation(junk[:, :], bank[:, h * HD:(h + 1) * HD], ACT.Square, scale=1.0 / WS,
                                       accum_out=ssq[:, h0 + h:h0 + h + 1]).then_inc(s["sq"], 1)

                def slot(n, j, nn):
                    if j == 0:
                        squares(nn, 0)
                        if not isinstance(nn, int):
                            for b in range(BT):
                                act.wait_ge(vn_in[b], nn * 16 - 16)
                        if isinstance(nn, int):
                            act.activation(VH[:, nn % 2, 0, :], PB[0][:, 2 * HD:], ACT.Copy, scale=1.0 / WS).then_inc(s["vh_hi"], 1)
                        else:
                            act.activation(VH[:, ds(nn % 2, 1), 0, :], PB[0][:, 2 * HD:].unsqueeze(1), ACT.Copy, scale=1.0 / WS).then_inc(s["vh_hi"], 1)
                    if j in (1, 2):
                        squares(nn, j)
                    if j == 3:
                        act.wait_ge(s["kn_mm"], nn + 1)
                        act.activation(KN[:, 0, :, :], PB[1][:, 0:2 * HD].rearrange("p (h t) -> p h t", h=2), ACT.Copy).then_inc(s["kn_hi"], 1)
                    if j in (4, 5):
                        act.wait_ge(s["qt_mm"], nn * 2 + j - 3)
                        act.activation(QTV[0][:, j - 4], PB[0][:, :].rearrange("p (h b t) -> p h b t", h=HR, t=S),
                                       ACT.Copy).then_inc(s["qt_hi"], 1)

                def prob_hi(m, j):
                    act.wait_ge(s["rec"], m + 1)
                    if not (isinstance(m, int) and m < 2):
                        act.wait_ge(s["t_mm"], m - 1)
                    act.activation(PH[:, j % 2, 0, :], SS[:, j % 2, :], ACT.Copy, scale=st[:, j % 2, 4:5]).then_inc(s["ph_hi"], 1)

                def pt_evac(m, j):
                    act.wait_ge(s["t_mm"], m + 1)
                    if not (isinstance(m, int) and m < 2):
                        act.wait_ge(s["pv_mm"], m - 1)
                    act.activation(PT[:, j % 2, :, 0:CL].bitcast(F32), PTB[:, :].rearrange("p (h k) -> p h k", h=2), ACT.Copy).then_inc(s["pt_ev"], 1)
                    act.activation(PT[0:S, j % 2, :, CL:CL + P].bitcast(F32), OB[j % 2][0:S, 0:P].rearrange("p (h k) -> p h k", h=2),
                                   ACT.Copy).then_inc(s["pt_ev"], 1)

                def o_evac(n, m, j):
                    act.wait_ge(s["pv_mm"], m + 1)
                    if j == 0 and not (isinstance(n, int) and n < 2):
                        act.wait_ge(s["y_add"], n)
                    act.activation(outputs(n, 0, j), OB[j % 2][:, P:2 * P].rearrange("p (h t) -> p h t", h=HR), ACT.Copy,
                                   scale=1.0 / PSC).then_inc(s["o_hi"], 1)

                def step(n, j, first, last):
                    m = n * J + j
                    if not (last and j == J - 1):
                        exps(m + 1, j + 1)
                    if j in (1, 2, 3) and not last:
                        slot(n, j - 1, n + 1)
                    if not (first and j == 0):
                        o_evac(n if j > 0 else n - 1, m - 1, (j - 1) % J)
                    if not (last and j == J - 1):
                        prob_hi(m + 1, j + 1)
                    pt_evac(m, j)
                    if not (last and j >= J - 3):
                        kt_evac(m + 3, j + 3)
                    if j in (3, 4, 5) and not last:
                        slot(n, j, n + 1)

                for j in range(7):
                    slot(None, j, 0)
                for m in range(3):
                    kt_evac(m, m)
                exps(0, 0)
                prob_hi(0, 0)
                steps(act, step)
                o_evac(NR - 1, NR * J - 1, J - 1)

            @block.vector
            def _(dve):
                def scores(m, j, first):
                    dve.wait_ge(s["mnew_ok"], first)
                    if j % 2 == 0:
                        dve.wait_ge(s["mask_ok"], first * BT + (j // 2 + 1 - BT))
                    if not (isinstance(m, int) and m < 2):
                        dve.wait_ge(s["prob"], m - 1)
                    dve.wait_ge(s["s_mm"], m + 1)
                    dve.tensor_copy(SS[:, j % 2, CL:CL + S], SN[:, j, :]).then_inc(s["sn_cp"], 1)
                    dve.tensor_tensor_reduce(SS[:, j % 2, 0:CL], SB[j % 2][:, :], MK[:, j // 2, :], 1.0, mnew[:, j:j + 1],
                                             ALU.add, ALU.max, st[:, j % 2, 0:1]).then_inc(s["ttr"], 1)
                    dve.wait_ge(s["ttr"], m + 1)
                    dve.tensor_scalar(st[:, j % 2, 1:2], st[:, j % 2, 0:1], -SC, None, ALU.mult).then_inc(s["neg"], 1)

                def sums(m, j):
                    dve.wait_ge(s["exp"], m + 1)
                    dve.tensor_scalar(st[:, j % 2, 3:4], st[:, j % 2, 2:3], 1.0 / PSC, None, ALU.mult).then_inc(s["sum"], 1)
                    dve.wait_ge(s["sum"], m + 1)
                    dve.reciprocal(st[:, j % 2, 4:5], st[:, j % 2, 3:4]).then_inc(s["rec"], 1)

                def prob_lo(m, j):
                    dve.wait_ge(s["ph_hi"], m + 1)
                    dve.scalar_tensor_tensor(PH[:, j % 2, 1, :], SS[:, j % 2, :], st[:, j % 2, 4:5], PH[:, j % 2, 0, :],
                                             ALU.mult, ALU.subtract).then_inc(s["prob"], 1)

                def o_evac(n, m, j):
                    dve.wait_ge(s["o_hi"], m + 1)
                    dve.scalar_tensor_tensor(outputs(n, 1, j), OB[j % 2][:, P:2 * P].rearrange("p (h t) -> p h t", h=HR), 1.0 / PSC,
                                             outputs(n, 0, j), ALU.mult, ALU.subtract).then_inc(s["o_lo"], 1)

                def rope(nn, i):
                    bank = PB[i % 2]
                    nh = 2 if i == 0 else HR
                    src = bank[:, 0:nh * HD].rearrange("p (h d) -> p h d", d=HD)
                    t1 = (TK[:, :] if i == 0 else TQ[:, i - 1, :]).rearrange("p (h d) -> p h d", d=HD)
                    t2 = T2[:, i % 2, 0:nh * HD].rearrange("p (h d) -> p h d", d=HD)
                    ta = tab[:, 2 if i == 0 else 0, :]
                    tb = tab[:, 3 if i == 0 else 1, :]
                    H = HD // 2
                    first = isinstance(nn, int) and nn == 0
                    dve.wait_ge(s["sq"], nn * (QH + 2) + (2, 2 + HR, 2 + 2 * HR)[i])
                    dve.wait_ge(s["tab_ok"], nn * 4 + 4)
                    if not first:
                        dve.wait_ge(s["kn_mm"] if i == 0 else s["qt_mm"], nn if i == 0 else nn * 2 - 2 + i)
                    if i == 2 or not first:
                        dve.wait_ge(s["turned"], nn * 3 + (0, -1, 1)[i])
                    dve.tensor_tensor(t1, src, ta.unsqueeze(1).to_broadcast([P, nh, HD]), ALU.mult).then_inc(s["t2_free"], 1)
                    dve.tensor_tensor(t2[:, :, 0:H], src[:, :, H:], tb[:, 0:H].unsqueeze(1).to_broadcast([P, nh, H]), ALU.mult).then_inc(s["t2_free"], 1)
                    dve.tensor_tensor(t2[:, :, H:], src[:, :, 0:H], tb[:, H:].unsqueeze(1).to_broadcast([P, nh, H]), ALU.mult).then_inc(s["rope"], 1)

                def slot(n, j, nn):
                    if j == 0:
                        dve.wait_ge(s["vh_hi"], nn + 1)
                        if isinstance(nn, int):
                            dve.scalar_tensor_tensor(VH[:, nn % 2, 1, :], PB[0][:, 2 * HD:], 1.0 / WS, VH[:, nn % 2, 0, :],
                                                     ALU.mult, ALU.subtract).then_inc(s["vh_lo"], 1)
                        else:
                            dve.scalar_tensor_tensor(VH[:, ds(nn % 2, 1), 1, :], PB[0][:, 2 * HD:].unsqueeze(1), 1.0 / WS,
                                                     VH[:, ds(nn % 2, 1), 0, :], ALU.mult, ALU.subtract).then_inc(s["vh_lo"], 1)
                        rope(nn, 0)
                    if j in (1, 2):
                        rope(nn, j)
                    if j == 3:
                        dve.wait_ge(s["kn_hi"], nn + 1)
                        dve.tensor_tensor(KN[:, 1, :, :], PB[1][:, 0:2 * HD].rearrange("p (h t) -> p h t", h=2), KN[:, 0, :, :],
                                          ALU.subtract).then_inc(s["kn_lo"], 1)
                    if j in (4, 5):
                        dve.wait_ge(s["qt_hi"], nn * 2 + j - 3)
                        dve.tensor_tensor(QTV[1][:, j - 4], PB[0][:, :].rearrange("p (h b t) -> p h b t", h=HR, t=S), QTV[0][:, j - 4],
                                          ALU.subtract).then_inc(s["qt_lo"], 1)
                    if j == 6:
                        dve.wait_ge(s["sn_mm"], nn + 1)
                        if not (isinstance(nn, int) and nn == 0):
                            dve.wait_ge(s["sn_cp"], nn * J)
                        dve.tensor_copy(SN[:, :, :], PB[0][:, 0:J * S].rearrange("p (j t) -> p j t", j=J)).then_inc(s["sn_ev"], 1)
                        dve.wait_ge(s["sn_ev"], nn + 1)
                        dve.tensor_reduce(mnew[:, :], SN[:, :, :], AX.X, ALU.max).then_inc(s["mnew_ok"], 1)

                def y_add(n):
                    dve.wait_ge(s["wo_mm"], n + 1)
                    y = Y[:, ds(n % NT, 1), :].rearrange("p o d -> p (o d)")
                    dve.scalar_tensor_tensor(y, PB[1][:, :], 1.0 / WS, y, ALU.mult, ALU.add).then_inc(s["y_add"], 1)

                def step(n, j, first, last):
                    m = n * J + j
                    if not (last and j == J - 1):
                        sums(m + 1, j + 1)
                    if j == 6 and not last:
                        slot(n, j, n + 1)
                    if not (last and j >= J - 2):
                        scores(m + 2, (j + 2) % J, n + 1 if j < J - 2 else n + 2)
                    if not (first and j == 0):
                        o_evac(n if j > 0 else n - 1, m - 1, (j - 1) % J)
                    if not (last and j == J - 1):
                        prob_lo(m + 1, j + 1)
                    if not last:
                        if j == 0:
                            dve.wait_ge(s["mask_ok"], n * BT + BT)
                            lengths(n + 1)
                        for b in {0: (0,), 1: (1,), 7: (2, 3)}.get(j, ()):
                            mask(n + 1, b)
                    if j in (1, 2, 3) and not last:
                        slot(n, j - 1, n + 1)
                    if j in (3, 4, 5) and not last:
                        slot(n, j, n + 1)
                    if j == 7 and not first:
                        y_add(n - 1)

                def lengths(n):
                    dve.tensor_copy(lcol[:, :], res["len"][:, ds(n % NT * BT, BT)]).then_inc(s["lc_ok"], 1)

                def mask(n, b):
                    dve.wait_ge(s["lc_ok"], n + 1)
                    dve.tensor_scalar(MK[:, b, :], iota[:, :], lcol[:, b:b + 1], -BIG, ALU.is_ge, ALU.mult).then_inc(s["mask_ok"], 1)

                dve.wait_ge(s["const_in"], 16 * len(consts))
                lengths(0)
                for b in range(BT):
                    mask(0, b)
                dve.memset(Y[:, :, :], 0.0).then_inc(s["y_add"], 1)
                dve.wait_ge(s["y_add"], 1)
                for j in range(7):
                    slot(None, j, 0)
                for m in range(2):
                    scores(m, m, 1)
                sums(0, 0)
                prob_lo(0, 0)
                steps(dve, step)
                o_evac(NR - 1, NR * J - 1, J - 1)
                y_add(NR - 1)

            @block.tensor
            def _(pe):
                def turn_keys(m, n, j):
                    b, v = j // 2, j % 2
                    if v == 0:
                        pe.wait_ge(kv_in[b], n * (16 * CC) + 16 * CC)
                    if not (isinstance(m, int) and m == 0):
                        pe.wait_ge(s["kt_ev"], m)
                    for h in range(2):
                        for c in range(CC):
                            k0 = h * 512 + v * 256
                            last = pe.transpose(halves[2][:, (h * CC + c) * P:(h * CC + c + 1) * P], KV[:, b, c, k0:k0 + HD], res["ident"][:, :])
                    last.then_inc(s["kt_mm"], 1)

                def score(m, n, j):
                    b, v = j // 2, j % 2
                    pe.wait_ge(s["kt_ev"], m + 1)
                    if v == 0 or j == 1:
                        pe.wait_ge(s["qt_lo"], n * 2 + 1 + v)
                    if not (isinstance(m, int) and m < 2):
                        pe.wait_ge(s["ttr"], m - 1)
                    mm3(pe, SB[j % 2][:, :], lambda h: QT[:, h, j, :],
                        lambda h: KT[:, j % 2, h, :], True, True).then_inc(s["s_mm"], 1)

                def turn_probs(m, j):
                    pe.wait_ge(s["prob"], m + 1)
                    if not (isinstance(m, int) and m == 0):
                        pe.wait_ge(s["pt_ev"], m * 2)
                    if not (isinstance(m, int) and m < 2):
                        pe.wait_ge(s["o_lo"], m - 1)
                    for h in range(2):
                        for c in range(CC):
                            pe.transpose(halves[3][:, (h * CC + c) * P:(h * CC + c + 1) * P], PH[:, j % 2, h, c * P:(c + 1) * P], res["ident"][:, :])
                        last = pe.transpose(halves[4 + j % 2][0:S, h * P:(h + 1) * P], PH[:, j % 2, h, CL:CL + S], res["ident"][:, :])
                    last.then_inc(s["t_mm"], 1)

                def weigh(m, n, j):
                    b, v = j // 2, j % 2
                    pe.wait_ge(s["pt_ev"], m * 2 + 2)
                    if v == 0:
                        pe.wait_ge(vn_in[b], n * 16 + 16)
                    o = OB[j % 2][:, P:2 * P]
                    for c in range(CC):
                        mm3(pe, o, lambda h: KV[:, b, c, h * 512 + v * 256 + HD:h * 512 + v * 256 + 2 * HD],
                            lambda h: PT[:, j % 2, h, c * P:(c + 1) * P], c == 0, False)
                    mm3(pe, o, lambda h: VN[:, b, h, v * HD:(v + 1) * HD],
                        lambda h: PT[0:S, j % 2, h, CL:CL + P], False, True).then_inc(s["pv_mm"], 1)

                def project(nn, bank, w, cols, g):
                    for c in range(KC):
                        last = mm3(pe, bank[:, 0:WQ], lambda h: res["x3T"][:, h, c, ds(g * P, P)],
                                   lambda h: w[:, h, c, cols:cols + WQ], c == 0, c == KC - 1)
                    return last

                def write_out(n, heads):
                    if heads[0] == 0:
                        pe.wait_ge(s["o_lo"], n * J + J)
                        pe.wait_ge(s["wo_in"], n // NT * (16 * len(WO_RANGE)) + 16 * len(WO_RANGE))
                        pe.wait_ge(s["kn_lo"], NR if isinstance(n, int) and n >= NR - 2 else n + 3)
                        pe.wait_ge(s["y_add"], n + 1)
                    for q in heads:
                        last = mm3(pe, PB[1][:, :], lambda h: OT[:, ds(n % 2, 1), h, q, :].rearrange("p o t -> p (o t)"),
                                   lambda h: wo[:, h, q, :], q == 0, q == QH - 1)
                    if heads[-1] == QH - 1:
                        last.then_inc(s["wo_mm"], 1)

                def slot(n, j, nn):
                    first = isinstance(nn, int) and nn == 0
                    g = nn % NT
                    if j == 0:
                        pe.wait_ge(s["wkv_in"], nn // NT * (16 * len(WKV_RANGE)) + 16 * len(WKV_RANGE))
                        if not first:
                            pe.wait_ge(s["sn_ev"], nn)
                        project(nn, PB[0], wkv, 0, g).then_inc(s["kv_mm"], 1)
                    if j == 1:
                        pe.wait_ge(s["wq_in"], nn // NT * (16 * len(WQ_RANGE)) + 16 * len(WQ_RANGE))
                        if not first:
                            pe.wait_ge(s["kn_lo"], nn)
                            if not isinstance(nn, int):
                                pe.wait_ge(s["y_add"], nn - 1)
                        project(nn, PB[1], wq, 0, g).then_inc(s["q_mm"], 1)
                    if j == 2:
                        pe.wait_ge(s["rope"], nn * 3 + 1)
                        pe.wait_ge(s["vh_lo"], nn + 1)
                        project(nn, PB[0], wq, WQ, g).then_inc(s["q_mm"], 1)
                    if j == 3:
                        pe.wait_ge(s["roped"], nn * 3 + 1)
                        pe.wait_ge(s["rope"], nn * 3 + 2)
                        for h in range(2):
                            last = pe.transpose(PB[1][:, h * P:(h + 1) * P], TK[:, h * HD:(h + 1) * HD], res["identf"][:, :])
                        last.then_inc(s["kn_mm"], 1)
                    if j in (4, 5):
                        pe.wait_ge(s["roped"], nn * 3 + j - 2)
                        if j == 4:
                            pe.wait_ge(s["rope"], nn * 3 + 3)
                        else:
                            pe.wait_ge(s["qt_lo"], nn * 2 + 1)
                        for h in range(HR):
                            last = pe.transpose(PB[0][:, h * P:(h + 1) * P], TQ[:, j - 4, h * HD:(h + 1) * HD], res["identf"][:, :])
                        last.then_inc(s["qt_mm"], 1)
                    if j == 6:
                        pe.wait_ge(s["qt_lo"], nn * 2 + 2)
                        for i in range(J):
                            b, v = i // 2, i % 2
                            last = mm3(pe, PB[0][:, i * S:(i + 1) * S], lambda h: QT[:, h, i, :],
                                       lambda h: KN[:, h, v, S * b:S * b + S], True, True)
                        last.then_inc(s["sn_mm"], 1)

                def step(n, j, first, last):
                    m = n * J + j
                    if not (first and j == 0):
                        weigh(m - 1, n if j > 0 else n - 1, (j - 1) % J)
                    if j == 6 and not first:
                        write_out(n - 1, WO_HEADS[j])
                    if j == 6 and not last:
                        slot(n, j, n + 1)
                    if not (last and j >= J - 2):
                        score(m + 2, n if j < J - 2 else n + 1, (j + 2) % J)
                    turn_probs(m, j)
                    if not (last and j >= J - 3):
                        turn_keys(m + 3, n if j < J - 3 else n + 1, (j + 3) % J)
                    if j in (4, 5, 7) and not first:
                        write_out(n - 1, WO_HEADS[j])
                    if j < 6 and not last:
                        slot(n, j, n + 1)

                for j in range(7):
                    slot(None, j, 0)
                for m in range(2):
                    turn_keys(m, 0, m)
                for m in range(2):
                    score(m, 0, m)
                turn_keys(2, 0, 2)
                steps(pe, step)
                weigh(NR * J - 1, NR - 1, J - 1)
                write_out(NR - 1, range(QH))


def last_ffn(nc, a, dram, res, banks, halves, Y, out):
    ER = E * R
    with ExitStack() as ctx:
        def sb(name, shape, dt):
            return ctx.enter_context(nc.sbuf_tensor(name, shape, dt))

        WT = sb("WT", [P, KC, D], F32)
        AB = sb("AB", [P, 2, D], F32)
        ABH = sb("ABH", [P, 2, 2, D], F16)
        lw = sb("lw", [P, 1], F32)
        lw2 = sb("lw2", [P, 1], F32)
        bias = sb("bias", [P, D], F32)
        MF = sb("MF", [P, KC, D], F32)
        MT = sb("MT", [P, 2, KC, D], F16)
        YH = sb("YH", [P, 2, 2, D], F16)
        YT = sb("YT3", [P, 2, 2, KC, P], F16)
        X3 = sb("X3", [P, 2, D], F32)
        XB = sb("XB", [P, 2, D], F32)
        RS = sb("RS", [P, 2, D], F32)

        names = ("f_in w2x b_ok ab_hi ab_lo m_mm mf mt_hi mt_lo y_hi y_lo yt_mm yt_ev o_mm xb res "
                 "x3_in0 x3_in1 out0 out1").split()
        s = {n: ctx.enter_context(nc.semaphore("f_" + n)) for n in names}
        x3_in, stored = [s["x3_in0"], s["x3_in1"]], [s["out0"], s["out1"]]
        ins = [(lw, a["lw_rep"]), (AB[:, 0, :], a["Af"]), (AB[:, 1, :], a["Bf"]),
               (WT[:, :, :].rearrange("p c n -> p (c n)"), a["Wf"]), (bias, a["bf_rep"])]

        with nc.Block() as block:
            def rows(t, n):
                return t[ds(n * P, P), :]

            @block.sync
            def _(sp):
                for dst, src in ins:
                    sp.dma_start(dst[...], src).then_inc(s["f_in"], 16)
                for i in range(2):
                    sp.dma_start(X3[:, i, :], rows(dram["x3"], i)).then_inc(x3_in[i], 16)

                def store(n, k, i, ahead):
                    sp.wait_ge(s["res"], n + 1)
                    sp.dma_start(rows(out, n), RS[:, i, :]).then_inc(stored[i], 16)
                    if ahead:
                        sp.wait_ge(s["xb"], n + 1)
                        sp.dma_start(X3[:, i, :], rows(dram["x3"], n + 2)).then_inc(x3_in[i], 16)
                with sp.Fori(0, NT // 2 - 1) as k:
                    for i in range(2):
                        store(k * 2 + i, k, i, True)
                for i in range(2):
                    store(NT - 2 + i, NT // 2 - 1, i, False)
                for i in range(2):
                    sp.wait_ge(stored[i], 16 * (NT // 2))

            @block.gpsimd
            def _(pool):
                def tile(n, k, i, first):
                    pool.wait_ge(x3_in[i], k * 16 + 16)
                    if not first:
                        pool.wait_ge(s["res"], n - 1)
                    pool.tensor_tensor(XB[:, i, :], X3[:, i, :], bias[:, :], ALU.add).then_inc(s["xb"], 1)
                pool.wait_ge(s["f_in"], 16 * len(ins))
                for i in range(2):
                    tile(i, 0, i, True)
                with pool.Fori(1, NT // 2) as k:
                    for i in range(2):
                        tile(k * 2 + i, k, i, False)

            @block.scalar
            def _(act):
                act.wait_ge(s["f_in"], 16 * len(ins))
                act.activation(ABH[:, 0, 0, :], AB[:, 0, :], ACT.Copy).then_inc(s["ab_hi"], 1)
                act.wait_ge(s["b_ok"], 1)
                act.activation(ABH[:, 1, 0, :], AB[:, 1, :], ACT.Copy).then_inc(s["ab_hi"], 1)
                for c in range(KC):
                    act.wait_ge(s["mf"], c + 1)
                    act.activation(MT[:, 0, c, :], MF[:, c, :], ACT.Copy).then_inc(s["mt_hi"], 1)

                def tile(n, i, first):
                    if not first:
                        act.wait_ge(s["yt_mm"], n - 1)
                    act.activation(YH[:, i, 0, :], Y[:, ds(n, 1), :].rearrange("p o d -> p (o d)"), ACT.Copy).then_inc(s["y_hi"], 1)
                    act.wait_ge(s["yt_mm"], n + 1)
                    if not first:
                        act.wait_ge(s["o_mm"], n - 1)
                    act.activation(YT[:, i, :, :, :].rearrange("p h c t -> p (h c t)").bitcast(F32),
                                   banks[i][:, :], ACT.Copy).then_inc(s["yt_ev"], 1)
                for i in range(2):
                    tile(i, i, True)
                with act.Fori(1, NT // 2) as k:
                    for i in range(2):
                        tile(k * 2 + i, i, False)

            @block.vector
            def _(dve):
                dve.wait_ge(s["f_in"], 16 * len(ins))
                dve.tensor_scalar(lw2[:, :], lw[:, :], 2.0, None, ALU.mult).then_inc(s["w2x"], 1)
                dve.wait_ge(s["w2x"], 1)
                dve.tensor_scalar(AB[:, 1, :], AB[:, 1, :], lw2[:, 0:1], None, ALU.mult).then_inc(s["b_ok"], 1)
                for i in range(2):
                    dve.wait_ge(s["ab_hi"], i + 1)
                    dve.wait_ge(s["b_ok"], 1)
                    dve.tensor_tensor(ABH[:, i, 1, :], AB[:, i, :], ABH[:, i, 0, :], ALU.subtract).then_inc(s["ab_lo"], 1)
                for c in range(KC):
                    dve.wait_ge(s["m_mm"], c + 1)
                    dve.tensor_tensor(MF[:, c, :], banks[4 + c][:, :], WT[:, c, :], ALU.add).then_inc(s["mf"], 1)
                for c in range(KC):
                    dve.wait_ge(s["mt_hi"], c + 1)
                    dve.tensor_tensor(MT[:, 1, c, :], MF[:, c, :], MT[:, 0, c, :], ALU.subtract).then_inc(s["mt_lo"], 1)

                def y_lo(n, i):
                    dve.wait_ge(s["y_hi"], n + 1)
                    dve.tensor_tensor(YH[:, i, 1, :], Y[:, ds(n, 1), :].rearrange("p o d -> p (o d)"), YH[:, i, 0, :],
                                      ALU.subtract).then_inc(s["y_lo"], 1)

                def result(n, k, i, first):
                    dve.wait_ge(s["o_mm"], n + 1)
                    dve.wait_ge(s["xb"], n + 1)
                    if not first:
                        dve.wait_ge(stored[i], k * 16)
                    dve.tensor_tensor(RS[:, i, :], banks[2 + i][:, :], XB[:, i, :], ALU.add).then_inc(s["res"], 1)
                y_lo(0, 0)
                y_lo(1, 1)
                result(0, 0, 0, True)
                y_lo(2, 0)
                result(1, 0, 1, True)
                with dve.Fori(1, NT // 2 - 1) as k:
                    for i in range(2):
                        y_lo(k * 2 + i + 1, 1 - i)
                        result(k * 2 + i, k, i, False)
                y_lo(NT - 1, 1)
                for i in range(2):
                    result(NT - 2 + i, NT // 2 - 1, i, False)

            @block.tensor
            def _(pe):
                pe.wait_ge(s["ab_lo"], 2)
                for c in range(KC):
                    mm3(pe, banks[4 + c][:, :], lambda h: ABH[:, 0, h, c * P:(c + 1) * P], lambda h: ABH[:, 1, h, :],
                        True, True).then_inc(s["m_mm"], 1)

                def turn(n, i, first):
                    pe.wait_ge(s["y_lo"], n + 1)
                    if not first:
                        pe.wait_ge(s["yt_ev"], n - 1)
                    for h in range(2):
                        for c in range(KC):
                            last = pe.transpose(halves[i][:, (h * KC + c) * P:(h * KC + c + 1) * P],
                                                YH[:, i, h, c * P:(c + 1) * P], res["ident"][:, :])
                    last.then_inc(s["yt_mm"], 1)

                def product(n, i, first):
                    pe.wait_ge(s["yt_ev"], n + 1)
                    if not first:
                        pe.wait_ge(s["res"], n - 1)
                    for c in range(KC):
                        last = mm3(pe, banks[2 + i][:, :], lambda h: YT[:, i, h, c, :], lambda h: MT[:, h, c, :],
                                   c == 0, c == KC - 1)
                    last.then_inc(s["o_mm"], 1)
                turn(0, 0, True)
                pe.wait_ge(s["mt_lo"], KC)
                turn(1, 1, True)
                product(0, 0, True)
                turn(2, 0, False)
                product(1, 1, True)
                with pe.Fori(1, NT // 2 - 1) as k:
                    for i in range(2):
                        turn(k * 2 + i + 1, 1 - i, False)
                        product(k * 2 + i, i, False)
                turn(NT - 1, 1, False)
                for i in range(2):
                    product(NT - 2 + i, i, False)


def layout(v):
    f = np.float32
    p = np.arange(P)

    def chunks_t(m):
        return np.ascontiguousarray(m.T.reshape(KC, P, -1).transpose(1, 0, 2)).reshape(P, -1)

    A = {n: np.asarray(x) for n, x in v.items()}
    o = {}
    o["x"] = A["x"].reshape(NB * S, D)
    o["c_ident"] = np.eye(P, dtype=f)
    o["c_iota"] = np.broadcast_to(np.arange(D, dtype=f), (P, D)).copy()
    o["c_iota16"] = np.broadcast_to(np.arange(CL, dtype=np.float16), (P, CL)).copy()
    o["c_pmod"] = np.stack([p % S, p % R], 1).astype(f)
    freq = np.power(np.float32(10000.0), np.arange(0, HD, 2, dtype=f) / f(HD))
    o["c_freq"] = np.broadcast_to((f(1.0) / freq).astype(f), (P, HD // 2)).copy()
    o["c_hmask"] = ((np.arange(U * R) // R)[:, None] == (p // S)[None, :]).astype(f) / f(WS)
    seq = BT * np.arange(NT)[None, :] + (p // S)[:, None]
    o["cond_rep"] = A["itok_B_0_15"][seq]
    o["adapter_rep"] = A["itok_B_6_15"][BT * np.arange(NT)[None, :] + (np.arange(U * R) // R)[:, None]]
    o["adapter_ids"] = A["itok_B_6_15"].reshape(1, NB)
    o["perm_cols"] = np.ascontiguousarray(A["L1_ffn_perm"].reshape(KC, P).T)
    bt = A["itok_Bx16_0_63"]
    o["page_rep"] = np.ascontiguousarray(bt.reshape(NB, CC, NPP // CC)[:, :, p // PS].transpose(2, 0, 1)).reshape(P, NB * CC)
    o["len_rep"] = np.broadcast_to(A["itok_B_207_1644"], (P, NB)).copy()
    o["pos_rep"] = A["itok_B_207_1644"][seq]
    o["cond0"] = A["L0_cond_weights"].reshape(NC * S, S)
    o["cond2"] = A["L2_cond_weights"].reshape(NC * S, S)
    o["A0"] = chunks_t(np.concatenate([A["L0_ffn_A"].reshape(E * R, D), A["L0_ffn_Wr"]], 0))
    o["B0"] = np.ascontiguousarray(A["L0_ffn_B"].transpose(0, 2, 1)).reshape(E * R, D)
    o["br_rep"] = np.broadcast_to(A["L0_ffn_br"], (P, E)).copy()
    o["ATA"] = chunks_t(A["L1_cond_lora_A_w"].reshape(NA * R, D))
    o["w1_rows"] = np.concatenate([A["L1_cond_base_weight"],
                                   A["L1_cond_lora_B_w"].transpose(1, 0, 2).reshape(D, NA * R),
                                   A["L1_cond_base_bias"].reshape(D, 1)], 1)
    up = np.zeros((P, FH, FM), f)
    dn = np.zeros((P, FH, P), f)
    for h in range(FH):
        q = slice(32 * (h % BT), 32 * (h % BT) + 32)
        up[q, h, :] = A["L1_ffn_up"][h]
        dn[:, h, q] = A["L1_ffn_down"][h]
    o["UP"], o["DN"] = up.reshape(P, -1), dn.reshape(P, -1)
    o["QK2"] = chunks_t(np.concatenate([A["L2_ffn_Wq"], A["L2_ffn_Wk"]], 0))
    o["W2"] = chunks_t(A["L2_ffn_W"])
    o["A2"] = chunks_t(A["L2_ffn_A"].reshape(E * R, D))
    o["B2"] = np.ascontiguousarray(A["L2_ffn_Bm"].transpose(0, 2, 1)).reshape(E * R, D)
    o["b2_rep"] = np.broadcast_to(A["L2_ffn_b"], (P, D)).copy()
    o["Af"] = A["L3_ffn_lora_A"].reshape(E * R, D)
    o["Bf"] = np.ascontiguousarray(A["L3_ffn_lora_B"].transpose(0, 2, 1)).reshape(E * R, D)
    o["Wf"] = chunks_t(A["L3_ffn_W"])
    o["lw_rep"] = np.repeat(A["L3_ffn_lora_weights"], R).reshape(P, 1)
    o["bf_rep"] = np.broadcast_to(A["L3_ffn_bias"], (P, D)).copy()
    w3 = []
    for hp in range(HP):
        q = A["L3_cond_Wq"][hp * QH * HD:(hp + 1) * QH * HD]
        kv = np.concatenate([A[n][hp * 2 * HD:(hp + 1) * 2 * HD] for n in ("L3_cond_Wk", "L3_cond_Wv")], 0)
        wo = A["L3_cond_Wo"][:, hp * QH * HD:(hp + 1) * QH * HD].reshape(D, QH, HD).transpose(2, 1, 0).reshape(HD, QH * D)
        w3.append(np.concatenate([chunks_t(q), chunks_t(kv), wo], 1))
    kv = np.stack([A["L3_cond_k_cache"], A["L3_cond_v_cache"]], 3)
    kv = kv.reshape(NT, P, HP * 512 // CH, CH).transpose(0, 2, 1, 3).reshape(KV_PIECES, P, CH)
    w3 = np.stack(w3).reshape(HP, P, W3_COLS // CH, CH).transpose(0, 2, 1, 3).reshape(W_PIECES, P, CH)
    wq, wk = A["L3_cond_q_norm_w"], A["L3_cond_k_norm_w"]
    h = HD // 2
    o["norm_w"] = np.broadcast_to(np.stack([wq, np.concatenate([wq[h:], wq[:h]]), wk, np.concatenate([wk[h:], wk[:h]])]), (P, 4, HD)).copy()
    wg, kg = W_PIECES // NG, KV_PIECES // NG
    parts = [x for g in range(NG) for x in (kv[g * kg:(g + 1) * kg], w3[g * wg:(g + 1) * wg])]
    o["bulk"] = np.concatenate(parts + [np.zeros((2, P, CH), f)])
    return {n: np.ascontiguousarray(x) for n, x in o.items()}


def kernel(**inputs):
    import concourse.bacc as bacc
    from concourse.bass_utils import run_bass_kernel_spmd

    nc = bacc.Bacc("TRN2", target_bir_lowering=False, num_devices=1)
    arrays = layout(inputs)
    a = {n: nc.dram_tensor(f"in_{n}", x.shape, mybir.dt.from_np(x.dtype), kind="ExternalInput").ap() for n, x in arrays.items()}
    out = nc.dram_tensor("out", [NB * S, D], F32, kind="ExternalOutput").ap()
    build(nc, a, out)
    r = run_bass_kernel_spmd(nc, [{f"in_{n}": x for n, x in arrays.items()}], core_ids=[0])
    return r.results[0]["out"].reshape(NB, S, D)
```
